# Optimizing a Trainium2 kernel written in Bass

```python
import numpy as np
import jax
import jax.numpy as jnp

def _softmax(x, axis=-1):
    return jax.nn.softmax(x, axis=axis)

def _gelu(x):
    return jax.nn.gelu(x, approximate=True)

def _silu(x):
    return jax.nn.silu(x)

def _sigmoid(x):
    return jax.nn.sigmoid(x)

def _layernorm(x, axis=-1, eps=1e-05):
    m = jnp.mean(x, axis=axis, keepdims=True)
    v = jnp.var(x, axis=axis, keepdims=True)
    return (x - m) / jnp.sqrt(v + eps)

def _scatter_add(tgt, idx, src, axis=0):
    return tgt.at[idx].add(src)

def _segment_sum(src, seg, n):
    return jax.ops.segment_sum(src, seg, n)
kernel_name = 'mk_decoder_preln_d2_seqx_r4_e046d4'

def setup_inputs(seed: int=0):
    np.random.seed(seed)
    _w = jnp.asarray

    def _rec_inputs():
        import jax
        import jax.numpy as jnp
        _rk = jax.random.key(seed)
        x = 7.22e-05 + 1 * jax.random.normal(jax.random.fold_in(_rk, 1), (4, 512, 512), jnp.float32)
        _lenS = 512 - jax.random.randint(jax.random.fold_in(_rk, 7), (4,), 0, max(1, 512 // 4) + 1, jnp.int32)
        _lenS2 = 512 - jax.random.randint(jax.random.fold_in(_rk, 8), (4,), 0, max(1, 512 // 4) + 1, jnp.int32)
        _ctx_1024P = jax.random.normal(jax.random.fold_in(_rk, 11), (4, 16, 256), jnp.float32)
        _ctx_1024c = jax.random.dirichlet(jax.random.fold_in(_rk, 511), 0.3 * jnp.ones((16,), jnp.float32), (4, 512))
        _ctx_1024t = jnp.einsum('bsk,bkd->bsd', _ctx_1024c, _ctx_1024P)
        _ctx_1024t = _ctx_1024t * jax.lax.rsqrt(jnp.mean(jnp.square(_ctx_1024t)) + 1e-12) * 0.953939
        ctx_1024 = 2.81802e-05 + 1.00001 * (_ctx_1024t + 0.3 * jax.random.normal(jax.random.fold_in(_rk, 611), (4, 512, 256), jnp.float32))
        return (x, ctx_1024)
    x, ctx_1024 = _rec_inputs()

    def _L0_attn_setup():
        import jax, jax.numpy as jnp
        import numpy as np
        Q_HEADS, KV_HEADS, HEAD_DIM, WINDOW = (16, 4, 128, 128)
        HIDDEN = 512
        ROPE_BASE = 10000.0

        def _rope_tables(T, head_dim, dtype):
            half = head_dim // 2
            inv_freq = 1.0 / ROPE_BASE ** (jnp.arange(half, dtype=jnp.float32) / half)
            t = jnp.arange(T, dtype=jnp.float32)
            freqs = jnp.outer(t, inv_freq)
            return (jnp.cos(freqs).astype(dtype), jnp.sin(freqs).astype(dtype))

        def _apply_rope(x, cos, sin):
            c = cos[None, :, None, :]
            s = sin[None, :, None, :]
            x1, x2 = jnp.split(x, 2, axis=-1)
            return jnp.concatenate([x1 * c - x2 * s, x1 * s + x2 * c], axis=-1)
        key = jax.random.key(seed)
        ks = jax.random.split(key, 5)
        B, T = (1, 1024)
        x = jax.random.normal(ks[0], (B, T, HIDDEN), dtype=jnp.float32)
        sc = 0.02
        wq = jax.random.normal(ks[1], (Q_HEADS * HEAD_DIM, HIDDEN), dtype=jnp.float32) * sc
        wk = jax.random.normal(ks[2], (KV_HEADS * HEAD_DIM, HIDDEN), dtype=jnp.float32) * sc
        wv = jax.random.normal(ks[3], (KV_HEADS * HEAD_DIM, HIDDEN), dtype=jnp.float32) * sc
        wo = jax.random.normal(ks[4], (HIDDEN, Q_HEADS * HEAD_DIM), dtype=jnp.float32) * sc
        return {'x': x, 'wq': wq, 'wk': wk, 'wv': wv, 'wo': wo}
    _L0_attn_all = _L0_attn_setup()
    _L0_attn_in = {k: v for k, v in _L0_attn_all.items() if k in ('wq', 'wk', 'wv', 'wo')}
    del _L0_attn_all

    def _L0_xattn_setup():
        import jax, jax.numpy as jnp
        import numpy as np
        key = jax.random.key(seed)
        ks = jax.random.split(key, 6)
        B, L, N, C, D = (8, 128, 512, 256, 128)
        return {'teacher_logits': jax.random.normal(ks[0], (B, L, N), dtype=jnp.float32), 'teacher_features': jax.random.normal(ks[1], (B, N, C), dtype=jnp.float32), 'Wq': jax.random.normal(ks[2], (D, C), dtype=jnp.float32) * (1.0 / np.sqrt(C)), 'bq': jnp.zeros((D,), dtype=jnp.float32), 'Wk': jax.random.normal(ks[3], (D, C), dtype=jnp.float32) * (1.0 / np.sqrt(C)), 'bk': jnp.zeros((D,), dtype=jnp.float32)}
    _L0_xattn_all = _L0_xattn_setup()
    _L0_xattn_in = {k: v for k, v in _L0_xattn_all.items() if k in ('Wq', 'bq', 'Wk', 'bk')}
    del _L0_xattn_all

    def _L0_ffn_setup():
        import jax, jax.numpy as jnp
        import numpy as np
        HIDDEN = 512
        INTER = 1376
        LUT_SIZE = 16

        def _ghost_linear(x, idx, lut):
            w = lut[idx]
            return jnp.einsum('bsh,oh->bso', x, w)
        key = jax.random.key(seed)
        k_x, k_lut, k_g, k_u, k_d = jax.random.split(key, 5)
        x = jax.random.normal(k_x, (2, 1024, HIDDEN), dtype=jnp.float32)
        lut = jax.random.normal(k_lut, (LUT_SIZE,), dtype=jnp.float32) * 0.02
        gate_idx = jax.random.randint(k_g, (INTER, HIDDEN), 0, LUT_SIZE, dtype=jnp.int32)
        up_idx = jax.random.randint(k_u, (INTER, HIDDEN), 0, LUT_SIZE, dtype=jnp.int32)
        down_idx = jax.random.randint(k_d, (HIDDEN, INTER), 0, LUT_SIZE, dtype=jnp.int32)
        return {'x': x, 'lut': lut, 'gate_idx': gate_idx, 'up_idx': up_idx, 'down_idx': down_idx}
    _L0_ffn_all = _L0_ffn_setup()
    _L0_ffn_in = {k: v for k, v in _L0_ffn_all.items() if k in ('lut', 'gate_idx', 'up_idx', 'down_idx')}
    del _L0_ffn_all

    def _L1_attn_setup():
        import jax, jax.numpy as jnp
        import numpy as np
        import math
        N_HEAD = 16
        LAYER = 1
        LAMBDA_INIT = 0.8 - 0.6 * math.exp(-0.3 * (LAYER - 1))
        key = jax.random.key(seed)
        ks = jax.random.split(key, 7)
        B, T, E = (2, 512, 512)
        s = 0.02
        return {'x': jax.random.normal(ks[0], (B, T, E), dtype=jnp.float32), 'W_attn': jax.random.normal(ks[1], (E, 3 * E), dtype=jnp.float32) * s, 'W_proj': jax.random.normal(ks[2], (E, E), dtype=jnp.float32) * s, 'lambda_q1': jax.random.normal(ks[3], (E,), dtype=jnp.float32) * 0.1, 'lambda_k1': jax.random.normal(ks[4], (E,), dtype=jnp.float32) * 0.1, 'lambda_q2': jax.random.normal(ks[5], (E,), dtype=jnp.float32) * 0.1, 'lambda_k2': jax.random.normal(ks[6], (E,), dtype=jnp.float32) * 0.1}
    _L1_attn_all = _L1_attn_setup()
    _L1_attn_in = {k: v for k, v in _L1_attn_all.items() if k in ('W_attn', 'W_proj', 'lambda_q1', 'lambda_k1', 'lambda_q2', 'lambda_k2')}
    del _L1_attn_all

    def _L1_xattn_setup():
        import jax, jax.numpy as jnp
        import numpy as np
        import math
        B, L, DM = (2, 512, 256)
        DS, DC, EXP = (16, 4, 2)
        DI = EXP * DM
        DR = math.ceil(DM / 16)
        DT_MIN, DT_MAX, DT_FLOOR = (0.001, 0.1, 0.0001)

        def _ssm_forward(hidden_states, z, in_proj_w, conv_w, conv_b, x_proj_w, dt_proj_w, dt_proj_b, A_log, D):
            b = hidden_states.shape[0]
            x = jnp.einsum('ed,bld->bel', in_proj_w, hidden_states)
            xp = jnp.pad(x, ((0, 0), (0, 0), (DC - 1, 0)))
            xc = jax.lax.conv_general_dilated(xp, conv_w[:, None, :], window_strides=(1,), padding='VALID', dimension_numbers=('NCH', 'OIH', 'NCH'), feature_group_count=DI)
            u = jax.nn.silu(xc + conv_b[None, :, None])
            x_dbl = jnp.einsum('ke,bel->bkl', x_proj_w, u)
            dt_lo = x_dbl[:, :DR]
            Bm = x_dbl[:, DR:DR + DS]
            Cm = x_dbl[:, DR + DS:]
            delta = jax.nn.softplus(jnp.einsum('er,brl->bel', dt_proj_w, dt_lo) + dt_proj_b[None, :, None])
            A = -jnp.exp(A_log)

            def step(state, xs):
                d_t, B_t, C_t, u_t = xs
                dA = jnp.exp(d_t[..., None] * A)
                state = state * dA + (d_t * u_t)[..., None] * B_t[:, None, :]
                y_t = jnp.einsum('ben,bn->be', state, C_t)
                return (state, y_t)
            xs = (jnp.moveaxis(delta, -1, 0), jnp.moveaxis(Bm, -1, 0), jnp.moveaxis(Cm, -1, 0), jnp.moveaxis(u, -1, 0))
            state0 = jnp.zeros((b, DI, DS), delta.dtype)
            _, ys = jax.lax.scan(step, state0, xs)
            y = jnp.moveaxis(ys, 0, -1)
            y = y + D[None, :, None] * u
            y = y * jax.nn.silu(z)
            return jnp.swapaxes(y, 1, 2)
        key = jax.random.key(seed)
        ks = jax.random.split(key, 8)
        hidden_states = jax.random.normal(ks[0], (B, L, DM), jnp.float32)
        z = jax.random.normal(ks[1], (B, DI, L), jnp.float32)
        in_proj_w = jax.random.normal(ks[2], (DI, DM), jnp.float32) * DM ** (-0.5)
        conv_w = jax.random.normal(ks[3], (DI, DC), jnp.float32) * DC ** (-0.5)
        conv_b = jnp.zeros((DI,), jnp.float32)
        x_proj_w = jax.random.normal(ks[4], (DR + 2 * DS, DI), jnp.float32) * DI ** (-0.5)
        dt_std = DR ** (-0.5)
        dt_proj_w = jax.random.uniform(ks[5], (DI, DR), jnp.float32, -dt_std, dt_std)
        dt = jnp.exp(jax.random.uniform(ks[6], (DI,), jnp.float32) * (math.log(DT_MAX) - math.log(DT_MIN)) + math.log(DT_MIN))
        dt = jnp.clip(dt, DT_FLOOR)
        dt_proj_b = dt + jnp.log(-jnp.expm1(-dt))
        A_log = jnp.log(jnp.broadcast_to(jnp.arange(1, DS + 1, dtype=jnp.float32), (DI, DS)))
        D = jnp.ones((DI,), jnp.float32)
        return dict(hidden_states=hidden_states, z=z, in_proj_w=in_proj_w, conv_w=conv_w, conv_b=conv_b, x_proj_w=x_proj_w, dt_proj_w=dt_proj_w, dt_proj_b=dt_proj_b, A_log=A_log, D=D)
    _L1_xattn_all = _L1_xattn_setup()
    _L1_xattn_in = {k: v for k, v in _L1_xattn_all.items() if k in ('in_proj_w', 'conv_w', 'conv_b', 'x_proj_w', 'dt_proj_w', 'dt_proj_b', 'A_log', 'D')}
    del _L1_xattn_all

    def _L1_ffn_setup():
        import math
        import jax, jax.numpy as jnp
        import numpy as np
        DIM = 512
        RANK = 8
        B, T = (4, 1024)

        def _orthogonal(key, n):
            a = jax.random.normal(key, (n, n), dtype=jnp.float32)
            q, r = jnp.linalg.qr(a)
            q = q * jnp.sign(jnp.diagonal(r))[None, :]
            return q
        key = jax.random.key(seed)
        kx, kf = jax.random.split(key)
        x = jax.random.normal(kx, (B, T, DIM), dtype=jnp.float32)
        fkeys = jax.random.split(kf, RANK)
        factors = jnp.stack([_orthogonal(fkeys[r], DIM) * (r + 1) ** (-0.5) for r in range(RANK)])
        bias = jnp.zeros((DIM,), dtype=jnp.float32)
        return {'x': x, 'factors': factors, 'bias': bias}
    _L1_ffn_all = _L1_ffn_setup()
    _L1_ffn_in = {k: v for k, v in _L1_ffn_all.items() if k in ('factors', 'bias')}
    del _L1_ffn_all
    return {'x': x, 'ctx_1024': ctx_1024, 'L0_attn_wq': _L0_attn_in['wq'], 'L0_attn_wk': _L0_attn_in['wk'], 'L0_attn_wv': _L0_attn_in['wv'], 'L0_attn_wo': _L0_attn_in['wo'], 'L0_xattn_Wq': _L0_xattn_in['Wq'], 'L0_xattn_bq': _L0_xattn_in['bq'], 'L0_xattn_Wk': _L0_xattn_in['Wk'], 'L0_xattn_bk': _L0_xattn_in['bk'], 'L0_ffn_lut': _L0_ffn_in['lut'], 'L0_ffn_gate_idx': _L0_ffn_in['gate_idx'], 'L0_ffn_up_idx': _L0_ffn_in['up_idx'], 'L0_ffn_down_idx': _L0_ffn_in['down_idx'], 'L1_attn_W_attn': _L1_attn_in['W_attn'], 'L1_attn_W_proj': _L1_attn_in['W_proj'], 'L1_attn_lambda_q1': _L1_attn_in['lambda_q1'], 'L1_attn_lambda_k1': _L1_attn_in['lambda_k1'], 'L1_attn_lambda_q2': _L1_attn_in['lambda_q2'], 'L1_attn_lambda_k2': _L1_attn_in['lambda_k2'], 'L1_xattn_in_proj_w': _L1_xattn_in['in_proj_w'], 'L1_xattn_conv_w': _L1_xattn_in['conv_w'], 'L1_xattn_conv_b': _L1_xattn_in['conv_b'], 'L1_xattn_x_proj_w': _L1_xattn_in['x_proj_w'], 'L1_xattn_dt_proj_w': _L1_xattn_in['dt_proj_w'], 'L1_xattn_dt_proj_b': _L1_xattn_in['dt_proj_b'], 'L1_xattn_A_log': _L1_xattn_in['A_log'], 'L1_xattn_D': _L1_xattn_in['D'], 'L1_ffn_factors': _L1_ffn_in['factors'], 'L1_ffn_bias': _L1_ffn_in['bias']}

def reference(x, ctx_1024, L0_attn_wq, L0_attn_wk, L0_attn_wv, L0_attn_wo, L0_xattn_Wq, L0_xattn_bq, L0_xattn_Wk, L0_xattn_bk, L0_ffn_lut, L0_ffn_gate_idx, L0_ffn_up_idx, L0_ffn_down_idx, L1_attn_W_attn, L1_attn_W_proj, L1_attn_lambda_q1, L1_attn_lambda_k1, L1_attn_lambda_q2, L1_attn_lambda_k2, L1_xattn_in_proj_w, L1_xattn_conv_w, L1_xattn_conv_b, L1_xattn_x_proj_w, L1_xattn_dt_proj_w, L1_xattn_dt_proj_b, L1_xattn_A_log, L1_xattn_D, L1_ffn_factors, L1_ffn_bias):
    import jax
    import jax.numpy as jnp

    def _L0_attn_ref(x, wq, wk, wv, wo):
        import jax, jax.numpy as jnp
        import numpy as np
        Q_HEADS, KV_HEADS, HEAD_DIM, WINDOW = (16, 4, 128, 128)
        HIDDEN = 512
        ROPE_BASE = 10000.0

        def _rope_tables(T, head_dim, dtype):
            half = head_dim // 2
            inv_freq = 1.0 / ROPE_BASE ** (jnp.arange(half, dtype=jnp.float32) / half)
            t = jnp.arange(T, dtype=jnp.float32)
            freqs = jnp.outer(t, inv_freq)
            return (jnp.cos(freqs).astype(dtype), jnp.sin(freqs).astype(dtype))

        def _apply_rope(x, cos, sin):
            c = cos[None, :, None, :]
            s = sin[None, :, None, :]
            x1, x2 = jnp.split(x, 2, axis=-1)
            return jnp.concatenate([x1 * c - x2 * s, x1 * s + x2 * c], axis=-1)
        B, T, _ = x.shape
        reps = Q_HEADS // KV_HEADS
        scale = 1.0 / np.sqrt(HEAD_DIM)
        q = jnp.einsum('bth,oh->bto', x, wq).reshape(B, T, Q_HEADS, HEAD_DIM)
        k = jnp.einsum('bth,oh->bto', x, wk).reshape(B, T, KV_HEADS, HEAD_DIM)
        v = jnp.einsum('bth,oh->bto', x, wv).reshape(B, T, KV_HEADS, HEAD_DIM)
        cos, sin = _rope_tables(T, HEAD_DIM, x.dtype)
        q = _apply_rope(q, cos, sin)
        k = _apply_rope(k, cos, sin)
        qg = q.reshape(B, T, KV_HEADS, reps, HEAD_DIM)
        scores = jnp.einsum('btgrd,bsgd->bgrts', qg, k) * scale
        idx = jnp.arange(T)
        allowed = (idx[None, :] <= idx[:, None]) & (idx[:, None] - idx[None, :] <= WINDOW)
        scores = jnp.where(allowed[None, None, None], scores, jnp.finfo(scores.dtype).min)
        probs = jax.nn.softmax(scores, axis=-1)
        out = jnp.einsum('bgrts,bsgd->btgrd', probs, v)
        out = out.reshape(B, T, Q_HEADS * HEAD_DIM)
        return jnp.einsum('bto,ho->bth', out, wo)

    def _L0_xattn_ref(teacher_logits, teacher_features, Wq, bq, Wk, bk):
        import jax, jax.numpy as jnp
        import numpy as np
        query = jnp.einsum('bnc,dc->bnd', teacher_features, Wq) + bq
        key = jnp.einsum('bnc,dc->bnd', teacher_features, Wk) + bk
        energy = jnp.einsum('bnd,bmd->bnm', query, key)
        attention = jax.nn.softmax(energy, axis=-1)
        x_m = jnp.einsum('bln,bmn->blm', teacher_logits, attention)
        return x_m

    def _L0_ffn_ref(x, lut, gate_idx, up_idx, down_idx):
        import jax, jax.numpy as jnp
        import numpy as np
        HIDDEN = 512
        INTER = 1376
        LUT_SIZE = 16

        def _ghost_linear(x, idx, lut):
            w = lut[idx]
            return jnp.einsum('bsh,oh->bso', x, w)
        gate = _ghost_linear(x, gate_idx, lut)
        up = _ghost_linear(x, up_idx, lut)
        h = jax.nn.silu(gate) * up
        return _ghost_linear(h, down_idx, lut)

    def _L1_attn_ref(x, W_attn, W_proj, lambda_q1, lambda_k1, lambda_q2, lambda_k2):
        import jax, jax.numpy as jnp
        import numpy as np
        import math
        N_HEAD = 16
        LAYER = 1
        LAMBDA_INIT = 0.8 - 0.6 * math.exp(-0.3 * (LAYER - 1))
        B, T, E = x.shape
        C = E // 2
        H = N_HEAD
        hd = E // H // 2
        scale = hd ** (-0.5)
        qkv = x @ W_attn
        q1 = qkv[..., 0 * C:1 * C].reshape(B, T, H, hd)
        k1 = qkv[..., 1 * C:2 * C].reshape(B, T, H, hd)
        q2 = qkv[..., 2 * C:3 * C].reshape(B, T, H, hd)
        k2 = qkv[..., 3 * C:4 * C].reshape(B, T, H, hd)
        v = qkv[..., 4 * C:6 * C].reshape(B, T, H, 2 * hd)
        lam = jnp.exp(jnp.dot(lambda_q1, lambda_k1)) - jnp.exp(jnp.dot(lambda_q2, lambda_k2)) + LAMBDA_INIT
        attn1 = jnp.einsum('bthd,bshd->bhts', q1, k1) * scale
        attn2 = jnp.einsum('bthd,bshd->bhts', q2, k2) * scale
        score = jax.nn.softmax(attn1 - lam * attn2, axis=-1)
        out = jnp.einsum('bhts,bshd->bthd', score, v)
        out = (1.0 - LAMBDA_INIT) * out.reshape(B, T, E)
        return out @ W_proj

    def _L1_xattn_ref(hidden_states, z, in_proj_w, conv_w, conv_b, x_proj_w, dt_proj_w, dt_proj_b, A_log, D):
        import jax, jax.numpy as jnp
        import numpy as np
        import math
        B, L, DM = (2, 512, 256)
        DS, DC, EXP = (16, 4, 2)
        DI = EXP * DM
        DR = math.ceil(DM / 16)
        DT_MIN, DT_MAX, DT_FLOOR = (0.001, 0.1, 0.0001)

        def _ssm_forward(hidden_states, z, in_proj_w, conv_w, conv_b, x_proj_w, dt_proj_w, dt_proj_b, A_log, D):
            b = hidden_states.shape[0]
            x = jnp.einsum('ed,bld->bel', in_proj_w, hidden_states)
            xp = jnp.pad(x, ((0, 0), (0, 0), (DC - 1, 0)))
            xc = jax.lax.conv_general_dilated(xp, conv_w[:, None, :], window_strides=(1,), padding='VALID', dimension_numbers=('NCH', 'OIH', 'NCH'), feature_group_count=DI)
            u = jax.nn.silu(xc + conv_b[None, :, None])
            x_dbl = jnp.einsum('ke,bel->bkl', x_proj_w, u)
            dt_lo = x_dbl[:, :DR]
            Bm = x_dbl[:, DR:DR + DS]
            Cm = x_dbl[:, DR + DS:]
            delta = jax.nn.softplus(jnp.einsum('er,brl->bel', dt_proj_w, dt_lo) + dt_proj_b[None, :, None])
            A = -jnp.exp(A_log)

            def step(state, xs):
                d_t, B_t, C_t, u_t = xs
                dA = jnp.exp(d_t[..., None] * A)
                state = state * dA + (d_t * u_t)[..., None] * B_t[:, None, :]
                y_t = jnp.einsum('ben,bn->be', state, C_t)
                return (state, y_t)
            xs = (jnp.moveaxis(delta, -1, 0), jnp.moveaxis(Bm, -1, 0), jnp.moveaxis(Cm, -1, 0), jnp.moveaxis(u, -1, 0))
            state0 = jnp.zeros((b, DI, DS), delta.dtype)
            _, ys = jax.lax.scan(step, state0, xs)
            y = jnp.moveaxis(ys, 0, -1)
            y = y + D[None, :, None] * u
            y = y * jax.nn.silu(z)
            return jnp.swapaxes(y, 1, 2)
        return _ssm_forward(hidden_states, z, in_proj_w, conv_w, conv_b, x_proj_w, dt_proj_w, dt_proj_b, A_log, D)

    def _L1_ffn_ref(x, factors, bias):
        import math
        import jax, jax.numpy as jnp
        import numpy as np
        DIM = 512
        RANK = 8
        B, T = (4, 1024)

        def _orthogonal(key, n):
            a = jax.random.normal(key, (n, n), dtype=jnp.float32)
            q, r = jnp.linalg.qr(a)
            q = q * jnp.sign(jnp.diagonal(r))[None, :]
            return q
        rank = factors.shape[0]
        mixed = jnp.einsum('btd,rde->bte', x, factors)
        mixed = mixed / math.sqrt(rank) + bias
        return mixed
    x = x + _L0_attn_ref(_layernorm(x, axis=-1), L0_attn_wq, L0_attn_wk, L0_attn_wv, L0_attn_wo)
    x = x + _L0_xattn_ref(_layernorm(x, axis=-1), ctx_1024, L0_xattn_Wq, L0_xattn_bq, L0_xattn_Wk, L0_xattn_bk)
    x = x + _L0_ffn_ref(_layernorm(x, axis=-1), L0_ffn_lut, L0_ffn_gate_idx, L0_ffn_up_idx, L0_ffn_down_idx)
    x = x + _L1_attn_ref(_layernorm(x, axis=-1), L1_attn_W_attn, L1_attn_W_proj, L1_attn_lambda_q1, L1_attn_lambda_k1, L1_attn_lambda_q2, L1_attn_lambda_k2)
    x = x + _L1_xattn_ref(ctx_1024, _layernorm(x, axis=-1), L1_xattn_in_proj_w, L1_xattn_conv_w, L1_xattn_conv_b, L1_xattn_x_proj_w, L1_xattn_dt_proj_w, L1_xattn_dt_proj_b, L1_xattn_A_log, L1_xattn_D)
    x = x + _L1_ffn_ref(_layernorm(x, axis=-1), L1_ffn_factors, L1_ffn_bias)
    return x

_drawn_inputs = setup_inputs


def setup_inputs(seed=0):
    import zlib

    import numpy as np

    out = dict(_drawn_inputs(seed))
    spreads = {'L0_xattn_bq': (0.0, 0.1),
     'L0_xattn_bk': (0.0, 0.8),
     'L1_xattn_conv_b': (0.0, 0.289),
     'L1_xattn_D': (1.0, 0.2),
     'L1_ffn_bias': (0.0, 0.1)}
    factors = {'L0_attn_wq': 5.256,
     'L0_attn_wk': 4.96,
     'L1_attn_W_attn': 8.0,
     'L1_attn_W_proj': 7.88,
     'L1_attn_lambda_q1': 8.0,
     'L1_attn_lambda_k1': 8.0,
     'L1_attn_lambda_q2': 8.0,
     'L1_attn_lambda_k2': 8.0,
     'L1_xattn_dt_proj_w': 6.298,
     'L1_xattn_dt_proj_b': 2.759}
    for name, (base, spread) in spreads.items():
        noise = np.random.default_rng([zlib.crc32(name.encode()), seed]).standard_normal(out[name].shape)
        drawn = base * np.exp(spread * noise) if base else spread * noise
        out[name] = jnp.asarray(drawn.astype(out[name].dtype))
    for name, factor in factors.items():
        out[name] = (out[name] * factor).astype(out[name].dtype)
    return out
```

```python
import math
from contextlib import ExitStack

import numpy as np

import concourse.bass as bass
from concourse import mybir

ALU = mybir.AluOpType
ACT = mybir.ActivationFunctionType
AX_X = mybir.AxisListType.X
F32 = mybir.dt.float32
F32R = mybir.dt.float32r
BF16 = mybir.dt.bfloat16
I32 = mybir.dt.int32

P = 128
B, T, D = 4, 512, 512
TT = T // P
KD = D // P
C = 256
KC = C // P
EPS = 1e-5
HEADS, KV, HD = 16, 4, 128
REPS = HEADS // KV
WINDOW = 128
MASKED = -1e30
QK = 128
INTER = 1376
OT = -(-INTER // P)
LUT = 16
DH, DHD = 16, 16
LAMBDA_INIT = 0.8 - 0.6 * math.exp(-0.3 * 0)
DI, DS, DC, DR = 512, 16, 4, 16
ET = DI // P
NQ = 4
RANK = 8
W_UP, W_DOWN = KD * INTER, 2 * KD * INTER
W_ALL = W_DOWN + OT * D
CHUNKS = 32
CH = W_ALL // CHUNKS


class Ring:

    def __init__(self, full, free, steps):
        self.full, self.free = full, free
        self.per = [0] * len(full)
        self.place = {}
        for n, step in enumerate(steps):
            b = n % len(full)
            assert step not in self.place, step
            self.place[step] = (b, self.per[b])
            self.per[b] += 1

    def at(self, step, i):
        b, nth = self.place[step]
        return b, i * self.per[b] + nth + 1

    def wait_free(self, eng, i, out=None, consumed=()):
        need = {}
        if out is not None:
            b, nth = self.place[out]
            need[b] = nth
        for step in consumed:
            b, nth = self.place[step]
            need[b] = max(need.get(b, 0), nth + 1)
        for b, count in need.items():
            eng.wait_ge(self.free[b], i * self.per[b] + count + 1)


class Core:

    def __init__(self, nc):
        self.nc, self.taken = nc, []

    def sem(self, name):
        self.taken.append(self.nc.alloc_semaphore(name=name))
        return self.taken[-1]

    def sems(self, name, n):
        return [self.sem(f"{name}{k}") for k in range(n)]

    def clear(self):
        self.nc.clear_and_free_semaphores(self.taken)
        self.taken = []
        self.nc.all_engine_barrier()


class Consts:
    def __init__(self, sb):
        self.ident = sb("ident", [P, P], F32)
        self.ident_bf = sb("ident_bf", [P, P], BF16)
        self.mask_bf = sb("mask_bf", [P, 2, 2 * P], BF16)
        self.minus_half = sb("minus_half", [P, TT], F32)
        self.ones = sb("ones", [P, P], F32)


class Norm:

    def __init__(self, core, sb, tag):
        self.stats_done = core.sem(f"{tag}_ln_stats")
        self.waited = core.sem(f"{tag}_ln_waited")
        self.var_ready = core.sem(f"{tag}_ln_var")
        self.rstd_ready = core.sem(f"{tag}_ln_rstd")
        self.xn_ready = core.sem(f"{tag}_ln_xn")
        self.stats = sb(f"{tag}_stats", [P, TT, 6], F32)
        self.mean_var = sb(f"{tag}_mean_var", [P, TT, 2], F32)
        self.var_eps = sb(f"{tag}_var_eps", [P, TT], F32)
        self.rstd = sb(f"{tag}_rstd", [P, TT], F32)
        self.xn = sb(f"{tag}_xn", [P, TT, D], F32)


def start_at_one(eng, *sems):
    for sem in sems:
        eng.sem_inc(sem, 1)


def wait_apart(eng, sem, value, waited):
    eng.wait_ge(sem, value)
    eng.sem_inc(waited, 1)


def norm_vector(nc, dve, norm, x, i):
    for tt in range(TT):
        last = nc.vector.bn_stats(norm.stats[:, tt, :], x[:, i, tt, :])
    last.then_inc(norm.stats_done, 1)
    wait_apart(dve, norm.stats_done, i * 2 + 1, norm.waited)
    for tt in range(TT):
        last = nc.vector.bn_aggr(norm.mean_var[:, tt, :], norm.stats[:, tt, :])
    last.then_inc(norm.stats_done, 1)
    dve.wait_ge(norm.stats_done, i * 2 + 2)
    nc.vector.tensor_scalar(norm.var_eps[:], norm.mean_var[:, :, 1], EPS, None, ALU.add) \
        .then_inc(norm.var_ready, 1)
    dve.wait_ge(norm.rstd_ready, i + 1)
    for tt in range(TT):
        nc.vector.tensor_scalar(norm.xn[:, tt, :], x[:, i, tt, :], norm.mean_var[:, tt, 0:1],
                                norm.rstd[:, tt:tt + 1], ALU.subtract, ALU.mult) \
            .then_inc(norm.xn_ready, 1)


def norm_gpsimd(nc, pool, norm, minus_half, i):
    pool.wait_ge(norm.var_ready, i + 1)
    nc.gpsimd.tensor_tensor(norm.rstd[:], norm.var_eps[:], minus_half[:], ALU.pow) \
        .then_inc(norm.rstd_ready, 1)


def norm_tensor(nc, pe, norm, ident, ring, banks, i):
    pe.wait_ge(norm.xn_ready, (i + 1) * TT)
    for k in range(KD):
        b, turn = ring.at(("xn", k), i)
        pe.wait_ge(ring.free[b], turn)
        for tt in range(TT):
            mm = nc.tensor.transpose(banks[b][:, tt * P:(tt + 1) * P],
                                     norm.xn[:, tt, k * P:(k + 1) * P], ident[:])
        mm.then_inc(ring.full[b], 1)


def stage_setup(core, sb, dram, x, consts):
    nc = core.nc
    loaded = core.sem("setup_loaded")
    mask_f = sb("mask_f", [P, 2, 2 * P], F32)
    with nc.Block() as block:
        @block.sync
        def _(sp):
            sp.dma_start(consts.ident[:], dram["identity"]).then_inc(loaded, 16)
            sp.dma_start(mask_f[:], dram["masks"]).then_inc(loaded, 16)
            for b in range(B):
                sp.dma_start(x[:, b], dram["x"][b].rearrange("(t p) d -> p t d", p=P)) \
                    .then_inc(loaded, 16)
            sp.wait_ge(loaded, 16 * (2 + B))

        @block.vector
        def _(dve):
            nc.vector.memset(consts.minus_half[:], -0.5)
            nc.vector.memset(consts.ones[:], 1.0)
            dve.wait_ge(loaded, 16 * (2 + B))
            nc.vector.tensor_copy(consts.ident_bf[:], consts.ident[:])
            nc.vector.tensor_copy(consts.mask_bf[:], mask_f[:])


def stage_window_attention(core, sb, psum, dram, x, consts):
    nc = core.nc
    scale = 1.0 / math.sqrt(HD)
    wq = sb("a_wq", [P, KD, HEADS * HD], F32)
    wk = sb("a_wk", [P, KD, KV * HD], F32)
    wv = sb("a_wv", [P, KD, KV * HD], F32)
    wo = sb("a_wo", [P, HEADS, D], F32)
    cos2 = sb("a_cos2", [P, T], F32)
    sin2 = sb("a_sin2", [P, T], F32)
    norm = Norm(core, sb, "a")
    xn_t = sb("a_xn_t", [P, KD, T], F32)
    q_t = sb("a_q_t", [P, REPS, T], F32)
    k_t = sb("a_k_t", [P, T], F32)
    v = sb("a_v", [P, TT, KV * HD], F32)
    rope_a = sb("a_rope_a", [P, 2, T], F32)
    rope_b = sb("a_rope_b", [P, 2, T], F32)
    prob = sb("a_prob", [P, REPS, TT, 2 * P], F32)
    prob_t = sb("a_prob_t", [P, 2, 2, REPS * P], F32)
    out_t = sb("a_out_t", [P, TT, REPS * P], F32)
    mx = sb("a_mx", [P, HEADS, TT], F32)
    neg_m = sb("a_neg_m", [P, HEADS, TT], F32)
    sums = sb("a_sums", [P, HEADS, TT], F32)
    rsum = sb("a_rsum", [P, HEADS, TT], F32)

    banks = [psum(f"a_bank{b}", [P, 512], F32) for b in range(4)]
    score = [psum(f"a_score{s}", [P, TT, 2 * P], F32) for s in range(2)]

    proj = lambda g: [("k", g)] + [("q", g, r) for r in range(REPS)]
    order = [("xn", k) for k in range(KD)] + [("v", tt) for tt in range(TT)] + proj(0)
    for g in range(KV):
        if g + 1 < KV:
            order += proj(g + 1)
        order += [("turn", g, 0, 0), ("turn", g, 1, 0), ("turn", g, 1, 1), ("pv", g, 0),
                  ("turn", g, 2, 0), ("turn", g, 2, 1), ("pv", g, 1),
                  ("turn", g, 3, 0), ("turn", g, 3, 1), ("pv", g, 2), ("pv", g, 3)]
        order += [("wo", g, tt) for tt in range(TT)]
    ring = Ring(core.sems("a_full", 4), core.sems("a_free", 4), order)

    w_in = {n: core.sem(f"a_in_{n}") for n in ("wk", "wv", "wq", "wo", "rope")}
    rope_done = core.sems("a_rope_done", 2)
    score_full = core.sems("a_score_full", 2)
    max_done = core.sem("a_max_done")
    neg_ready = core.sem("a_neg_ready")
    exp_done = core.sems("a_exp_done", 2)
    waited = core.sem("a_waited")
    rsum_ready = core.sem("a_rsum_ready")
    prob_ready = core.sem("a_prob_ready")
    PER_ROPE = KV * (1 + REPS) // 2
    PER_SLOT = HEADS // 2

    with nc.Block() as block:
        @block.sync
        def _(sp):
            sp.dma_start(wv[:], dram["wv_t"].rearrange("(k p) o -> p k o", p=P)).then_inc(w_in["wv"], 16)
            sp.dma_start(wk[:], dram["wk_t"].rearrange("(k p) o -> p k o", p=P)).then_inc(w_in["wk"], 16)
            sp.dma_start(cos2[:], dram["cos2"]).then_inc(w_in["rope"], 16)
            sp.dma_start(sin2[:], dram["sin2"]).then_inc(w_in["rope"], 16)
            sp.dma_start(wq[:], dram["wq_t"].rearrange("(k p) o -> p k o", p=P)).then_inc(w_in["wq"], 16)
            sp.dma_start(wo[:], dram["wo_t"].rearrange("(h p) o -> p h o", p=P)).then_inc(w_in["wo"], 16)

        @block.tensor
        def _(pe):
            start_at_one(pe, *rope_done, *exp_done, *ring.free)
            def project(i, g):
                for step in proj(g):
                    w = wk[:, :, g * HD:(g + 1) * HD] if step[0] == "k" else \
                        wq[:, :, (g * REPS + step[2]) * HD:(g * REPS + step[2] + 1) * HD]
                    b, turn = ring.at(step, i)
                    pe.wait_ge(ring.free[b], turn)
                    for k in range(KD):
                        mm = nc.tensor.matmul(banks[b][:], w[:, k, :], xn_t[:, k, :],
                                              start=(k == 0), stop=(k == KD - 1))
                    mm.then_inc(ring.full[b], 1)

            def scores(i, g):
                for r in range(REPS):
                    h = g * REPS + r
                    s = h % 2
                    n = g * (1 + REPS) + 1 + r
                    pe.wait_ge(rope_done[n % 2], i * PER_ROPE + n // 2 + 1 + 1)
                    if r % 2 == 0:
                        pe.wait_ge(rope_done[1 - n % 2], i * PER_ROPE + (n - 1) // 2 + 1 + 1)
                    pe.wait_ge(exp_done[s], i * PER_SLOT + h // 2 + 1)
                    for tt in range(TT):
                        out = score[s][:, tt, :]
                        nc.tensor.matmul(out, consts.ident_bf[:], consts.mask_bf[:, min(tt, 1), :],
                                         start=True, stop=False)
                        lo = P if tt == 0 else 0
                        mm = nc.tensor.matmul(out[:, lo:], q_t[:, r, tt * P:(tt + 1) * P],
                                              k_t[:, tt * P - P + lo:(tt + 1) * P],
                                              start=False, stop=True)
                    mm.then_inc(score_full[s], 1)

            def turn_probs(i, g, tt, prev):
                b, turn = ring.at(("turn", g, tt, prev), i)
                pe.wait_ge(ring.free[b], turn)
                lo = 0 if prev else P
                for r in range(REPS):
                    mm = nc.tensor.transpose(banks[b][:, r * P:(r + 1) * P],
                                             prob[:, r, tt, lo:lo + P], consts.ident[:])
                mm.then_inc(ring.full[b], 1)

            def weigh(i, g, tt):
                ring.wait_free(pe, i, ("pv", g, tt),
                               consumed=[("turn", g, tt, prev) for prev in range(min(tt, 1) + 1)])
                b, _ = ring.at(("pv", g, tt), i)
                for prev in range(min(tt, 1) + 1):
                    mm = nc.tensor.matmul(banks[b][:], v[:, tt - prev, g * HD:(g + 1) * HD],
                                          prob_t[:, tt % 2, prev, :],
                                          start=(prev == 0), stop=(prev == min(tt, 1)))
                mm.then_inc(ring.full[b], 1)

            pe.wait_ge(w_in["wv"], 16)
            with pe.Fori(0, B) as i:
                norm_tensor(nc, pe, norm, consts.ident, ring, banks, i)
                ring.wait_free(pe, i, consumed=[("xn", k) for k in range(KD)])
                for tt in range(TT):
                    b, turn = ring.at(("v", tt), i)
                    pe.wait_ge(ring.free[b], turn)
                    for k in range(KD):
                        mm = nc.tensor.matmul(banks[b][:], xn_t[:, k, tt * P:(tt + 1) * P], wv[:, k, :],
                                              start=(k == 0), stop=(k == KD - 1))
                    mm.then_inc(ring.full[b], 1)
                pe.wait_ge(w_in["wk"], 16)
                pe.wait_ge(w_in["wq"], 16)
                project(i, 0)
                for g in range(KV):
                    scores(i, g)
                    if g + 1 < KV:
                        project(i, g + 1)
                    pe.wait_ge(prob_ready, i * HEADS + (g + 1) * REPS)
                    turn_probs(i, g, 0, 0)
                    turn_probs(i, g, 1, 0)
                    turn_probs(i, g, 1, 1)
                    for tt in range(TT):
                        weigh(i, g, tt)
                        if tt + 2 < TT:
                            turn_probs(i, g, tt + 2, 0)
                            turn_probs(i, g, tt + 2, 1)
                    pe.wait_ge(w_in["wo"], 16)
                    for tt in range(TT):
                        ring.wait_free(pe, i, ("wo", g, tt), consumed=[("pv", g, tt)])
                        b, _ = ring.at(("wo", g, tt), i)
                        for r in range(REPS):
                            mm = nc.tensor.matmul(banks[b][:], out_t[:, tt, r * P:(r + 1) * P],
                                                  wo[:, g * REPS + r, :],
                                                  start=(r == 0), stop=(r == REPS - 1))
                        mm.then_inc(ring.full[b], 1)

        @block.scalar
        def _(act):
            def take(step, i, out):
                b, turn = ring.at(step, i)
                act.wait_ge(ring.full[b], turn)
                nc.scalar.copy(out, banks[b][:]).then_inc(ring.free[b], 1)

            def exponentials(i, g):
                for r in range(REPS):
                    h = g * REPS + r
                    act.wait_ge(neg_ready, i * HEADS + h + 1)
                    for tt in range(TT):
                        e = nc.scalar.activation(prob[:, r, tt, :], score[h % 2][:, tt, :], ACT.Exp,
                                                 bias=neg_m[:, h, tt:tt + 1], scale=scale,
                                                 accum_out=sums[:, h, tt:tt + 1])
                    e.then_inc(exp_done[h % 2], 1)

            with act.Fori(0, B) as i:
                for k in (1, 3):
                    take(("xn", k), i, xn_t[:, k, :])
                for tt in (1, 3):
                    take(("v", tt), i, v[:, tt, :])
                for g in range(KV):
                    exponentials(i, g)
                    take(("turn", g, 0, 0), i, prob_t[:, 0, 0, :])
                    take(("turn", g, 1, 0), i, prob_t[:, 1, 0, :])
                    for tt in range(TT):
                        take(("pv", g, tt), i, out_t[:, tt, :])
                        if tt + 2 < TT:
                            take(("turn", g, tt + 2, 0), i, prob_t[:, tt % 2, 0, :])

        @block.vector
        def _(dve):
            def take(step, i, out):
                b, turn = ring.at(step, i)
                dve.wait_ge(ring.full[b], turn)
                nc.vector.tensor_copy(out, banks[b][:]).then_inc(ring.free[b], 1)

            def rope(i, g):
                for j, step in enumerate(proj(g)):
                    n = g * (1 + REPS) + j
                    s = n % 2
                    b, turn = ring.at(step, i)
                    dve.wait_ge(ring.full[b], turn)
                    dve.wait_ge(rope_done[s], i * PER_ROPE + n // 2 + 1)
                    h = HD // 2
                    nc.vector.tensor_tensor(rope_a[:, s, :], banks[b][:], cos2[:], ALU.mult)
                    nc.vector.tensor_tensor(rope_b[0:h, s, :], banks[b][h:P, :], sin2[0:h, :], ALU.mult)
                    nc.vector.tensor_tensor(rope_b[h:P, s, :], banks[b][0:h, :], sin2[h:P, :], ALU.mult) \
                        .then_inc(ring.free[b], 1)

            def maxima(i, h):
                dve.wait_ge(score_full[h % 2], i * PER_SLOT + h // 2 + 1)
                nc.vector.tensor_reduce(mx[:, h, :], score[h % 2][:], AX_X, ALU.max).then_inc(max_done, 1)
                dve.wait_ge(max_done, i * HEADS + h + 1)
                nc.vector.tensor_scalar(neg_m[:, h, :], mx[:, h, :], -scale, None, ALU.mult) \
                    .then_inc(neg_ready, 1)

            def inverse(i, h):
                dve.wait_ge(exp_done[h % 2], i * PER_SLOT + h // 2 + 1 + 1)
                nc.vector.reciprocal(rsum[:, h, :], sums[:, h, :]).then_inc(rsum_ready, 1)

            dve.wait_ge(w_in["rope"], 32)
            with dve.Fori(0, B) as i:
                norm_vector(nc, dve, norm, x, i)
                for k in (0, 2):
                    take(("xn", k), i, xn_t[:, k, :])
                for tt in (0, 2):
                    take(("v", tt), i, v[:, tt, :])
                rope(i, 0)
                for g in range(KV):
                    for r in range(REPS):
                        maxima(i, g * REPS + r)
                        if r:
                            inverse(i, g * REPS + r - 1)
                    inverse(i, g * REPS + REPS - 1)
                    if g + 1 < KV:
                        rope(i, g + 1)
                    for tt in range(1, TT):
                        take(("turn", g, tt, 1), i, prob_t[:, tt % 2, 1, :])
                    for tt in range(TT):
                        b, turn = ring.at(("wo", g, tt), i)
                        dve.wait_ge(ring.full[b], turn)
                        nc.vector.tensor_tensor(x[:, i, tt, :], banks[b][:], x[:, i, tt, :], ALU.add) \
                            .then_inc(ring.free[b], 1)

        @block.gpsimd
        def _(pool):
            def rope_sums(i, g):
                for j, step in enumerate(proj(g)):
                    n = g * (1 + REPS) + j
                    s = n % 2
                    b, turn = ring.at(step, i)
                    pool.wait_ge(ring.free[b], turn + 1)
                    out = k_t[:] if j == 0 else q_t[:, j - 1, :]
                    nc.gpsimd.tensor_tensor(out, rope_a[:, s, :], rope_b[:, s, :], ALU.add) \
                        .then_inc(rope_done[s], 1)

            with pool.Fori(0, B) as i:
                norm_gpsimd(nc, pool, norm, consts.minus_half, i)
                rope_sums(i, 0)
                for g in range(KV):
                    for r in range(REPS):
                        h = g * REPS + r
                        wait_apart(pool, rsum_ready, i * HEADS + h + 1, waited)
                        for tt in range(TT):
                            p = nc.gpsimd.tensor_scalar(prob[:, r, tt, :], prob[:, r, tt, :],
                                                        rsum[:, h, tt:tt + 1], 1.0, ALU.mult, ALU.mult)
                        p.then_inc(prob_ready, 1)
                    if g + 1 < KV:
                        rope_sums(i, g + 1)


def stage_cross_attention(core, sb, psum, dram, x, consts):
    nc = core.nc
    wq = sb("b_wq", [P, KC, QK], F32)
    wk = sb("b_wk", [P, KC, QK], F32)
    bq = sb("b_bq", [P, 1], F32)
    bk = sb("b_bk", [P, 1], F32)
    ctx_t = sb("b_ctx_t", [P, B, KC, T], F32)
    norm = Norm(core, sb, "b")
    xn_t = sb("b_xn_t", [P, KD, T], F32)
    q_t = sb("b_q_t", [P, T], F32)
    k_t = sb("b_k_t", [P, T], F32)
    att = sb("b_att", [P, TT, T], F32)
    att_t = sb("b_att_t", [P, TT, T], F32)
    mx = sb("b_mx", [P, TT], F32)
    neg_m = sb("b_neg_m", [P, TT], F32)
    sums = sb("b_sums", [P, TT], F32)
    rsum = sb("b_rsum", [P, TT], F32)

    NB = 6
    banks = [psum(f"b_bank{b}", [P, 512], F32) for b in range(NB)]
    order = [("q",), ("k",)] + [("energy", m) for m in range(TT)] + [("xn", k) for k in range(KD)]
    order += [("turn", n) for n in range(TT)] + [("out", tt) for tt in range(TT)]
    ring = Ring(core.sems("b_full", NB), core.sems("b_free", NB), order)
    w_in = core.sem("b_in_w")
    max_done = core.sem("b_max_done")
    neg_ready = core.sem("b_neg_ready")
    waited = core.sem("b_waited")
    rsum_ready = core.sem("b_rsum_ready")
    att_ready = core.sem("b_att_ready")

    with nc.Block() as block:
        @block.sync
        def _(sp):
            sp.dma_start(wq[:], dram["x_wq_t"].rearrange("(k p) o -> p k o", p=P)).then_inc(w_in, 16)
            sp.dma_start(wk[:], dram["x_wk_t"].rearrange("(k p) o -> p k o", p=P)).then_inc(w_in, 16)
            sp.dma_start(bq[:], dram["x_bq"].rearrange("(p o) -> p o", o=1)).then_inc(w_in, 16)
            sp.dma_start(bk[:], dram["x_bk"].rearrange("(p o) -> p o", o=1)).then_inc(w_in, 16)
            sp.dma_start(ctx_t[:], dram["ctx_t"].rearrange("b (k p) t -> p b k t", p=P)).then_inc(w_in, 16)

        @block.tensor
        def _(pe):
            start_at_one(pe, *ring.free)
            pe.wait_ge(w_in, 16 * 5)
            with pe.Fori(0, B) as i:
                for step, w in ((("q",), wq), (("k",), wk)):
                    b, turn = ring.at(step, i)
                    pe.wait_ge(ring.free[b], turn)
                    for k in range(KC):
                        mm = nc.tensor.matmul(banks[b][:], w[:, k, :], ctx_t[:, i, k, :],
                                              start=(k == 0), stop=(k == KC - 1))
                    mm.then_inc(ring.full[b], 1)
                ring.wait_free(pe, i, consumed=[("q",), ("k",)])
                for m in range(TT):
                    b, turn = ring.at(("energy", m), i)
                    pe.wait_ge(ring.free[b], turn)
                    nc.tensor.matmul(banks[b][:], q_t[:, m * P:(m + 1) * P], k_t[:],
                                     start=True, stop=True).then_inc(ring.full[b], 1)
                norm_tensor(nc, pe, norm, consts.ident, ring, banks, i)
                pe.wait_ge(att_ready, (i + 1) * TT)
                for n in range(TT):
                    b, turn = ring.at(("turn", n), i)
                    pe.wait_ge(ring.free[b], turn)
                    for m in range(TT):
                        mm = nc.tensor.transpose(banks[b][:, m * P:(m + 1) * P],
                                                 att[:, m, n * P:(n + 1) * P], consts.ident[:])
                    mm.then_inc(ring.full[b], 1)
                for tt in range(TT):
                    ring.wait_free(pe, i, ("out", tt), consumed=[("xn", k) for k in range(KD)]
                                   + [("turn", n) for n in range(TT)] if tt == 0 else ())
                    b, _ = ring.at(("out", tt), i)
                    for n in range(TT):
                        mm = nc.tensor.matmul(banks[b][:], xn_t[:, n, tt * P:(tt + 1) * P], att_t[:, n, :],
                                              start=(n == 0), stop=(n == TT - 1))
                    mm.then_inc(ring.full[b], 1)


        @block.scalar
        def _(act):
            act.wait_ge(w_in, 16 * 5)
            with act.Fori(0, B) as i:
                for step, bias, out in ((("q",), bq, q_t), (("k",), bk, k_t)):
                    b, turn = ring.at(step, i)
                    act.wait_ge(ring.full[b], turn)
                    nc.scalar.activation(out[:], banks[b][:], ACT.Identity, bias=bias[:]) \
                        .then_inc(ring.free[b], 1)
                for m in range(TT):
                    act.wait_ge(neg_ready, i * TT + m + 1)
                    b, turn = ring.at(("energy", m), i)
                    nc.scalar.activation(att[:, m, :], banks[b][:], ACT.Exp, bias=neg_m[:, m:m + 1],
                                         accum_out=sums[:, m:m + 1]).then_inc(ring.free[b], 1)
                for step, out in [(("xn", k), xn_t[:, k, :]) for k in (1, 3)] + \
                        [(("turn", n), att_t[:, n, :]) for n in (0, 1, 2, 3)]:
                    b, turn = ring.at(step, i)
                    act.wait_ge(ring.full[b], turn)
                    nc.scalar.copy(out, banks[b][:]).then_inc(ring.free[b], 1)

        @block.vector
        def _(dve):
            with dve.Fori(0, B) as i:
                norm_vector(nc, dve, norm, x, i)
                for m in range(TT):
                    b, turn = ring.at(("energy", m), i)
                    dve.wait_ge(ring.full[b], turn)
                    nc.vector.tensor_reduce(mx[:, m:m + 1], banks[b][:], AX_X, ALU.max).then_inc(max_done, 1)
                    dve.wait_ge(max_done, i * TT + m + 1)
                    nc.vector.tensor_scalar(neg_m[:, m:m + 1], mx[:, m:m + 1], -1.0, None, ALU.mult) \
                        .then_inc(neg_ready, 1)
                for m in range(TT):
                    b, turn = ring.at(("energy", m), i)
                    dve.wait_ge(ring.free[b], turn + 1)
                    nc.vector.reciprocal(rsum[:, m:m + 1], sums[:, m:m + 1]).then_inc(rsum_ready, 1)
                for k in (0, 2):
                    b, turn = ring.at(("xn", k), i)
                    dve.wait_ge(ring.full[b], turn)
                    nc.vector.tensor_copy(xn_t[:, k, :], banks[b][:]).then_inc(ring.free[b], 1)
                for tt in range(TT):
                    b, turn = ring.at(("out", tt), i)
                    dve.wait_ge(ring.full[b], turn)
                    nc.vector.tensor_tensor(x[:, i, tt, :], banks[b][:], x[:, i, tt, :], ALU.add) \
                        .then_inc(ring.free[b], 1)

        @block.gpsimd
        def _(pool):
            with pool.Fori(0, B) as i:
                norm_gpsimd(nc, pool, norm, consts.minus_half, i)
                for m in range(TT):
                    wait_apart(pool, rsum_ready, i * TT + m + 1, waited)
                    nc.gpsimd.tensor_scalar(att[:, m, :], att[:, m, :], rsum[:, m:m + 1], 1.0,
                                            ALU.mult, ALU.mult).then_inc(att_ready, 1)


def stage_ffn_weights(core, sb, dram, weights):
    nc = core.nc
    lut = sb("f_lut", [P, LUT], I32)
    lut_xor = sb("f_lut_xor", [P, LUT // 2], I32)
    idx = sb("f_idx", [P, 2, CH], I32)
    mask = sb("f_mask", [P, 4, CH], I32)
    picks = sb("f_picks", [P, LUT // 2, CH], I32)
    lut_in = core.sem("f_lut_in")
    lut_ready = core.sem("f_lut_ready")
    waited = core.sem("f_waited")
    idx_in = core.sems("f_idx_in", 2)
    idx_used = core.sems("f_idx_used", 2)
    step_done = core.sem("f_step")

    with nc.Block() as block:
        @block.sync
        def _(sp):
            sp.dma_start(lut[:], dram["lut"].bitcast(I32).rearrange("(o l) -> o l", o=1)
                         .broadcast_to([P, LUT])).then_inc(lut_in, 16)
            with sp.Fori(0, CHUNKS // 2) as pair:
                for s in range(2):
                    sp.wait_ge(idx_used[s], pair + 1)
                    sp.dma_start(idx[:, s, :], dram["idx"][:, bass.ds(pair * (2 * CH) + s * CH, CH)]) \
                        .then_inc(idx_in[s], 16)

        @block.vector
        def _(dve):
            start_at_one(dve, *idx_used)
            dve.wait_ge(lut_in, 16)
            pairs = lut[:].rearrange("p (j two) -> p j two", two=2)
            nc.vector.tensor_tensor(lut_xor[:], pairs[:, :, 0], pairs[:, :, 1], ALU.bitwise_xor) \
                .then_inc(lut_ready, 1)
            dve.wait_ge(lut_ready, 1)
            with dve.Fori(0, CHUNKS // 2) as pair:
                for s in range(2):
                    def own_step(n):
                        wait_apart(dve, step_done, pair * 10 + s * 5 + n, waited)

                    dve.wait_ge(idx_in[s], pair * 16 + 16)
                    nc.vector.tensor_scalar(mask[:, 0, :], idx[:, s, :], 31, 31,
                                            ALU.logical_shift_left, ALU.arith_shift_right)
                    for bit in range(1, 4):
                        last = nc.vector.tensor_scalar(mask[:, bit, :], idx[:, s, :], 1 << bit, None,
                                                       ALU.bitwise_and)
                        if bit == 2:
                            last.then_inc(step_done, 1)
                    last.then_inc(idx_used[s], 1)
                    own_step(1)
                    for j in range(LUT // 2):
                        last = nc.vector.tensor_scalar(picks[:, j, :], mask[:, 0, :],
                                                       lut_xor[:, j:j + 1], lut[:, 2 * j:2 * j + 1],
                                                       ALU.bitwise_and, ALU.bitwise_xor)
                    last.then_inc(step_done, 1)
                    own_step(2)
                    for level in range(3):
                        half = 1 << level
                        for j in range(0, LUT // 2, 2 * half):
                            last = nc.vector.copy_predicated(picks[:, j, :], mask[:, level + 1, :],
                                                             picks[:, j + half, :])
                        last.then_inc(step_done, 1)
                        own_step(3 + level)
                    nc.vector.tensor_copy(weights[:, bass.ds(pair * (2 * CH) + s * CH, CH)].bitcast(I32),
                                          picks[:, 0, :])


def stage_ffn(core, sb, psum, dram, x, consts, weights):
    nc = core.nc
    norm = Norm(core, sb, "c")
    xn_t = sb("c_xn_t", [P, KD, T], F32)
    act_g = sb("c_act_g", [P, 2, T], F32)
    h_t = sb("c_h_t", [P, 2, T], F32)
    NB = 4
    banks = [psum(f"c_bank{b}", [P, 512], F32) for b in range(NB)]
    out = [psum(f"c_out{tt}", [P, 512], F32) for tt in range(TT)]
    order = [("xn", k) for k in range(KD)]
    for o in range(OT):
        order += [("gate", o), ("up", o)]
    ring = Ring(core.sems("c_full", NB), core.sems("c_free", NB), order)
    h_used = core.sem("c_h_used")
    out_full = core.sem("c_out_full")
    out_free = core.sem("c_out_free")
    width = [min(P, INTER - o * P) for o in range(OT)]

    with nc.Block() as block:
        @block.tensor
        def _(pe):
            start_at_one(pe, out_free, *ring.free)
            def down(i, o):
                b, turn = ring.at(("up", o), i)
                pe.wait_ge(ring.free[b], turn + 1)
                if o == 0:
                    pe.wait_ge(out_free, i * TT + 1)
                for tt in range(TT):
                    mm = nc.tensor.matmul(out[tt][:], h_t[0:width[o], o % 2, tt * P:(tt + 1) * P],
                                          weights[0:width[o], W_DOWN + o * D:W_DOWN + (o + 1) * D],
                                          start=(o == 0), stop=(o == OT - 1))
                mm.then_inc(h_used if o < OT - 1 else out_full, 1)

            with pe.Fori(0, B) as i:
                norm_tensor(nc, pe, norm, consts.ident, ring, banks, i)
                ring.wait_free(pe, i, consumed=[("xn", k) for k in range(KD)])
                for o in range(OT):
                    for kind, base in (("gate", 0), ("up", W_UP)):
                        b, turn = ring.at((kind, o), i)
                        pe.wait_ge(ring.free[b], turn)
                        for k in range(KD):
                            lo = base + k * INTER + o * P
                            mm = nc.tensor.matmul(banks[b][0:width[o], :], weights[:, lo:lo + width[o]],
                                                  xn_t[:, k, :], start=(k == 0), stop=(k == KD - 1))
                        mm.then_inc(ring.full[b], 1)
                    if o:
                        down(i, o - 1)
                down(i, OT - 1)

        @block.scalar
        def _(act):
            with act.Fori(0, B) as i:
                for k in (1, 3):
                    b, turn = ring.at(("xn", k), i)
                    act.wait_ge(ring.full[b], turn)
                    nc.scalar.copy(xn_t[:, k, :], banks[b][:]).then_inc(ring.free[b], 1)
                for o in range(OT):
                    if o >= 2:
                        b, turn = ring.at(("up", o - 2), i)
                        act.wait_ge(ring.free[b], turn + 1)
                    b, turn = ring.at(("gate", o), i)
                    act.wait_ge(ring.full[b], turn)
                    nc.scalar.activation(act_g[0:width[o], o % 2, :], banks[b][0:width[o], :], ACT.Silu) \
                        .then_inc(ring.free[b], 1)

        @block.vector
        def _(dve):
            with dve.Fori(0, B) as i:
                norm_vector(nc, dve, norm, x, i)
                for k in (0, 2):
                    b, turn = ring.at(("xn", k), i)
                    dve.wait_ge(ring.full[b], turn)
                    nc.vector.tensor_copy(xn_t[:, k, :], banks[b][:]).then_inc(ring.free[b], 1)
                for o in range(OT):
                    if o >= 2:
                        dve.wait_ge(h_used, i * (OT - 1) + o - 1)
                    b, turn = ring.at(("gate", o), i)
                    dve.wait_ge(ring.free[b], turn + 1)
                    b, turn = ring.at(("up", o), i)
                    dve.wait_ge(ring.full[b], turn)
                    nc.vector.tensor_tensor(h_t[0:width[o], o % 2, :], banks[b][0:width[o], :],
                                            act_g[0:width[o], o % 2, :], ALU.mult).then_inc(ring.free[b], 1)
                dve.wait_ge(out_full, i + 1)
                for tt in range(TT):
                    nc.vector.tensor_tensor(x[:, i, tt, :], out[tt][:], x[:, i, tt, :], ALU.add) \
                        .then_inc(out_free, 1)

        @block.gpsimd
        def _(pool):
            with pool.Fori(0, B) as i:
                norm_gpsimd(nc, pool, norm, consts.minus_half, i)


def stage_diff_attention(core, sb, psum, dram, x, consts):
    nc = core.nc
    E2 = 2 * DHD
    HG = P // E2
    GROUPS = DH // HG
    VD = D // DH
    w = sb("d_w", [P, KD, 3 * D], F32)
    wp = sb("d_wp", [P, KD, D], F32)
    lam_v = sb("d_lam_v", [P, 4, D], F32)
    lam_s = sb("d_lam_s", [P, 6], F32)
    rowsel = sb("d_rowsel", [P, 2], F32)
    coef = sb("d_coef", [P, 1], F32)
    norm = Norm(core, sb, "d")
    xn_t = sb("d_xn_t", [P, KD, T], F32)
    hi = sb("d_hi", [P, 2, T], F32R)
    lo = sb("d_lo", [P, 2, T], F32R)
    qs = sb("d_qs", [P, DH, T], F32R)
    ks = sb("d_ks", [P, DH, T], F32R)
    v = sb("d_v", [P, TT, D], F32)
    mx = sb("d_mx", [P, GROUPS, HG, TT], F32)
    neg_t = sb("d_neg_t", [HG * TT, P], F32R)
    prob_t = sb("d_prob_t", [P, 2, HG, T], F32)
    rsum = sb("d_rsum", [P, T], F32)
    out_t = sb("d_out_t", [P, GROUPS, T], F32)

    banks = [psum(f"d_bank{b}", [P, 512], F32) for b in range(2)]
    score = [psum(f"d_score{s}", [P, 2, T], F32) for s in range(2)]
    acc = psum("d_acc", [P, T], F32)
    acc_sum = psum("d_acc_sum", [P, T], F32)
    order = [("xn", k) for k in range(KD)]
    for g in range(GROUPS):
        order += [("q", g), ("k", g)]
    order += [("v", tt) for tt in range(TT)]
    for g in range(GROUPS):
        order += [("row", g, j, tt) for j in range(HG) for tt in range(TT)] + [("neg", g)]
    order += [("out", tt) for tt in range(TT)]
    ring = Ring(core.sems("d_full", 2), core.sems("d_free", 2), order)
    w_in = core.sem("d_in_w")
    lam_step = core.sem("d_lam_step")
    hi_done = core.sem("d_hi_done")
    stacked = core.sems("d_stacked", 2)
    max_in = core.sem("d_max_in")
    prob_used = core.sem("d_prob_used")
    score_full = core.sems("d_score_full", 2)
    exp_done = core.sems("d_exp_done", 2)
    acc_full = core.sem("d_acc_full")
    rsum_done = core.sem("d_rsum_done")
    acc_free = core.sem("d_acc_free")
    COPIES = 3 * HG * 16
    FILLS = GROUPS * TT

    with nc.Block() as block:
        @block.sync
        def _(sp):
            sp.dma_start(w[:], dram["d_w"].rearrange("(k p) o -> p k o", p=P)).then_inc(w_in, 16)
            sp.dma_start(wp[:], dram["d_wp"].rearrange("(k p) o -> p k o", p=P)).then_inc(w_in, 16)
            for n, name in enumerate(("lq1", "lk1", "lq2", "lk2")):
                sp.dma_start(lam_v[:, n, :], dram[name].rearrange("(o l) -> o l", o=1).broadcast_to([P, D])) \
                    .then_inc(w_in, 16)
            sp.dma_start(rowsel[:], dram["rowsel"]).then_inc(w_in, 16)
            with sp.Fori(0, B) as i:
                for g in range(GROUPS):
                    for n, (stack, parts) in enumerate(((qs, (hi, lo, hi)), (ks, (hi, hi, lo)))):
                        b, turn = ring.at(("qk"[n], g), i)
                        sp.wait_ge(ring.free[b], turn + 1)
                        for block_, part in enumerate(parts):
                            for j in range(HG):
                                sp.dma_start(stack[block_ * E2:(block_ + 1) * E2, g * HG + j, :].bitcast(F32),
                                             part[j * E2:(j + 1) * E2, n, :].bitcast(F32)) \
                                    .then_inc(stacked[n], 16)
                for g in range(GROUPS):
                    b, turn = ring.at(("neg", g), i)
                    sp.wait_ge(ring.free[b], turn + 1)
                    sp.dma_start(qs[3 * E2:3 * E2 + 1, g * HG:(g + 1) * HG, :]
                                 .rearrange("o j (t c) -> o (j t) c", c=P).bitcast(F32),
                                 neg_t[:].bitcast(F32)).then_inc(max_in, 16)

        @block.tensor
        def _(pe):
            start_at_one(pe, *exp_done, acc_free, *stacked, prob_used, acc_full, max_in, *ring.free)
            def rows(i, g, j):
                for tt in range(TT):
                    b, turn = ring.at(("row", g, j, tt), i)
                    pe.wait_ge(ring.free[b], turn)
                    nc.tensor.matmul(banks[b][:], qs[0:3 * E2, g * HG + j, tt * P:(tt + 1) * P],
                                     ks[0:3 * E2, g * HG + j, :], start=True, stop=True) \
                        .then_inc(ring.full[b], 1)

            def negate(i, g):
                ring.wait_free(pe, i, ("neg", g), consumed=[("row", g, HG - 1, tt) for tt in range(TT)])
                b, _ = ring.at(("neg", g), i)
                nc.tensor.transpose(banks[b][0:HG * TT, 0:P], mx[:, g, :, :].rearrange("p j t -> p (j t)"),
                                    consts.ident[:]).then_inc(ring.full[b], 1)

            def columns(i, g, st):
                for s in range(2):
                    pe.wait_ge(exp_done[s], i * FILLS + g * TT + st + 1)
                    for u in range(2):
                        h = g * HG + 2 * s + u
                        mm = nc.tensor.matmul(score[s][:, u, :], ks[0:3 * E2 + 1, h, st * P:(st + 1) * P],
                                              qs[0:3 * E2 + 1, h, :], start=True, stop=True)
                    mm.then_inc(score_full[s], 1)

            def weigh(i, g, st):
                if st == 0:
                    pe.wait_ge(acc_free, i * GROUPS + g + 1)
                for s in range(2):
                    pe.wait_ge(exp_done[s], i * FILLS + g * TT + st + 1 + 1)
                for j in range(HG):
                    h = g * HG + j
                    nc.tensor.matmul(acc[j * VD:(j + 1) * VD, :], v[:, st, h * VD:(h + 1) * VD],
                                     prob_t[:, st % 2, j, :], start=(st == 0), stop=(st == TT - 1))
                for j in range(HG):
                    mm = nc.tensor.matmul(acc_sum[j * VD:(j + 1) * VD, :], consts.ones[:, 0:VD],
                                          prob_t[:, st % 2, j, :], start=(st == 0), stop=(st == TT - 1))
                mm.then_inc(prob_used if st < TT - 1 else acc_full, 1)

            pe.wait_ge(w_in, 16 * 7)
            with pe.Fori(0, B) as i:
                norm_tensor(nc, pe, norm, consts.ident, ring, banks, i)
                ring.wait_free(pe, i, consumed=[("xn", k) for k in range(KD)])
                for g in range(GROUPS):
                    for n, kind in enumerate("qk"):
                        b, turn = ring.at((kind, g), i)
                        pe.wait_ge(ring.free[b], turn)
                        for k in range(KD):
                            mm = nc.tensor.matmul(banks[b][:], w[:, k, n * D + g * P:n * D + (g + 1) * P],
                                                  xn_t[:, k, :], start=(k == 0), stop=(k == KD - 1))
                        mm.then_inc(ring.full[b], 1)
                for tt in range(TT):
                    b, turn = ring.at(("v", tt), i)
                    pe.wait_ge(ring.free[b], turn)
                    for k in range(KD):
                        mm = nc.tensor.matmul(banks[b][:], xn_t[:, k, tt * P:(tt + 1) * P],
                                              w[:, k, 2 * D:3 * D], start=(k == 0), stop=(k == KD - 1))
                    mm.then_inc(ring.full[b], 1)
                for n in range(2):
                    pe.wait_ge(stacked[n], (i + 1) * (GROUPS * COPIES) + 1)
                for j in range(HG):
                    rows(i, 0, j)
                negate(i, 0)
                for g in range(GROUPS):
                    pe.wait_ge(max_in, (i * GROUPS + g) * 16 + 16 + 1)
                    columns(i, g, 0)
                    for st in range(TT):
                        if st + 1 < TT:
                            columns(i, g, st + 1)
                        if g + 1 < GROUPS:
                            rows(i, g + 1, st)
                            if st == HG - 1:
                                negate(i, g + 1)
                        weigh(i, g, st)
                pe.wait_ge(acc_free, (i + 1) * GROUPS + 1)
                for tt in range(TT):
                    b, turn = ring.at(("out", tt), i)
                    pe.wait_ge(ring.free[b], turn)
                    for g in range(GROUPS):
                        mm = nc.tensor.matmul(banks[b][:], out_t[:, g, tt * P:(tt + 1) * P], wp[:, g, :],
                                              start=(g == 0), stop=(g == GROUPS - 1))
                    mm.then_inc(ring.full[b], 1)

        @block.scalar
        def _(act):
            for n in range(2):
                act.wait_ge(lam_step, 1)
                nc.scalar.activation(lam_s[:, 2 + n:3 + n], lam_s[:, n:n + 1], ACT.Exp).then_inc(lam_step, 1)
            act.wait_ge(lam_step, 6)
            with act.Fori(0, B) as i:
                for k in (1, 3):
                    b, turn = ring.at(("xn", k), i)
                    act.wait_ge(ring.full[b], turn)
                    nc.scalar.copy(xn_t[:, k, :], banks[b][:]).then_inc(ring.free[b], 1)
                for g in range(GROUPS):
                    for n, kind in enumerate("qk"):
                        act.wait_ge(stacked[n], (i * GROUPS + g) * COPIES + 1)
                        b, turn = ring.at((kind, g), i)
                        act.wait_ge(ring.full[b], turn)
                        nc.scalar.activation(hi[:, n, :], banks[b][:], ACT.Copy if n else ACT.Identity,
                                             scale=1.0 if n else coef[:]).then_inc(hi_done, 1)
                for tt in (1, 3):
                    b, turn = ring.at(("v", tt), i)
                    act.wait_ge(ring.full[b], turn)
                    nc.scalar.copy(v[:, tt, :], banks[b][:]).then_inc(ring.free[b], 1)
                for g in range(GROUPS):
                    for st in range(TT):
                        if st >= 2:
                            act.wait_ge(prob_used, (i * GROUPS + g) * (TT - 1) + st - 1 + 1)
                        elif st == 0:
                            act.wait_ge(prob_used, (i * GROUPS + g) * (TT - 1) + 1)
                        else:
                            act.wait_ge(acc_full, i * GROUPS + g + 1)
                        for s in range(2):
                            act.wait_ge(score_full[s], i * FILLS + g * TT + st + 1)
                            nc.scalar.activation(prob_t[:, st % 2, 2 * s:2 * s + 2, :], score[s][:], ACT.Exp) \
                                .then_inc(exp_done[s], 1)

        @block.vector
        def _(dve):
            nc.vector.memset(ks[3 * E2:3 * E2 + 1, :, :].bitcast(F32), 1.0)
            dve.wait_ge(w_in, 16 * 7)
            for n in range(2):
                red = nc.vector.tensor_tensor_reduce(lam_v[:, 2 * n, :], lam_v[:, 2 * n, :], lam_v[:, 2 * n + 1, :],
                                                     1.0, 0.0, ALU.mult, ALU.add, lam_s[:, n:n + 1])
            red.then_inc(lam_step, 1)
            dve.wait_ge(lam_step, 3)
            nc.vector.tensor_tensor(lam_s[:, 4:5], lam_s[:, 2:3], lam_s[:, 3:4], ALU.subtract) \
                .then_inc(lam_step, 1)
            dve.wait_ge(lam_step, 4)
            nc.vector.tensor_scalar(lam_s[:, 5:6], lam_s[:, 4:5], LAMBDA_INIT, rowsel[:, 1:2], ALU.add, ALU.mult) \
                .then_inc(lam_step, 1)
            dve.wait_ge(lam_step, 5)
            nc.vector.tensor_tensor(coef[:], rowsel[:, 0:1], lam_s[:, 5:6], ALU.subtract).then_inc(lam_step, 1)
            dve.wait_ge(lam_step, 6)
            with dve.Fori(0, B) as i:
                norm_vector(nc, dve, norm, x, i)
                for k in (0, 2):
                    b, turn = ring.at(("xn", k), i)
                    dve.wait_ge(ring.full[b], turn)
                    nc.vector.tensor_copy(xn_t[:, k, :], banks[b][:]).then_inc(ring.free[b], 1)
                for g in range(GROUPS):
                    for n, kind in enumerate("qk"):
                        dve.wait_ge(hi_done, (i * GROUPS + g) * 2 + n + 1)
                        dve.wait_ge(stacked[n], (i * GROUPS + g) * COPIES + 1)
                        b, turn = ring.at((kind, g), i)
                        if n == 0:
                            ins = nc.vector.scalar_tensor_tensor(
                                out=lo[:, n, :], in0=banks[b][:], scalar=coef[:], in1=hi[:, n, :].bitcast(F32),
                                op0=ALU.mult, op1=ALU.subtract)
                        else:
                            ins = nc.vector.tensor_tensor(lo[:, n, :], banks[b][:], hi[:, n, :].bitcast(F32),
                                                          ALU.subtract)
                        ins.then_inc(ring.free[b], 1)
                for tt in (0, 2):
                    b, turn = ring.at(("v", tt), i)
                    dve.wait_ge(ring.full[b], turn)
                    nc.vector.tensor_copy(v[:, tt, :], banks[b][:]).then_inc(ring.free[b], 1)

                def maxima(g, j):
                    for tt in range(TT):
                        b, turn = ring.at(("row", g, j, tt), i)
                        dve.wait_ge(ring.full[b], turn)
                        nc.vector.tensor_reduce(mx[:, g, j, tt:tt + 1], banks[b][:], AX_X, ALU.max) \
                            .then_inc(ring.free[b], 1)

                def negated(g):
                    b, turn = ring.at(("neg", g), i)
                    dve.wait_ge(ring.full[b], turn)
                    dve.wait_ge(max_in, (i * GROUPS + g) * 16 + 1)
                    nc.vector.tensor_scalar(neg_t[:], banks[b][0:HG * TT, 0:P], -1.0, None, ALU.mult) \
                        .then_inc(ring.free[b], 1)

                for j in range(HG):
                    maxima(0, j)
                negated(0)
                for g in range(GROUPS):
                    if g + 1 < GROUPS:
                        for j in range(HG):
                            maxima(g + 1, j)
                        negated(g + 1)
                    dve.wait_ge(acc_full, i * GROUPS + g + 1 + 1)
                    nc.vector.reciprocal(rsum[:], acc_sum[:]).then_inc(rsum_done, 1)
                    dve.wait_ge(rsum_done, i * GROUPS + g + 1)
                    nc.vector.scalar_tensor_tensor(out=out_t[:, g, :], in0=acc[:], scalar=1.0 - LAMBDA_INIT,
                                                   in1=rsum[:], op0=ALU.mult, op1=ALU.mult).then_inc(acc_free, 1)
                for tt in range(TT):
                    b, turn = ring.at(("out", tt), i)
                    dve.wait_ge(ring.full[b], turn)
                    nc.vector.tensor_tensor(x[:, i, tt, :], banks[b][:], x[:, i, tt, :], ALU.add) \
                        .then_inc(ring.free[b], 1)

        @block.gpsimd
        def _(pool):
            with pool.Fori(0, B) as i:
                norm_gpsimd(nc, pool, norm, consts.minus_half, i)


def stage_scan_inputs(core, sb, psum, dram, scratch):
    nc = core.nc
    w_in_t = sb("m_w_in", [P, KC, DI], F32)
    w_x = sb("m_w_x", [P, ET, DR + 2 * DS], F32)
    w_dt = sb("m_w_dt", [DR, DI], F32)
    cols = sb("m_cols", [P, ET, DC + 3], F32)
    ctx_t = sb("m_ctx_t", [P, B, KC, T], F32)
    padded = sb("m_padded", [P, ET, DC - 1 + T], F32)
    conv = sb("m_conv", [P, ET, T], F32)
    u = sb("m_u", [P, ET, T], F32)
    dbl = sb("m_dbl", [DR + 2 * DS, T], F32)
    dt = sb("m_dt", [P, ET, T], F32)
    e = sb("m_e", [P, ET, T], F32)
    one_e = sb("m_one_e", [P, ET, T], F32)
    log1p = sb("m_log1p", [P, ET, T], F32)
    delta = sb("m_delta", [P, ET, T], F32)
    delta_u = sb("m_delta_u", [P, ET, T], F32)
    d_u = sb("m_d_u", [P, ET, T], F32)
    banks = [psum(f"m_bank{b}", [P, 512], F32) for b in range(6)]
    ring = Ring(core.sems("m_full", 6), core.sems("m_free", 6),
                [("x", et) for et in range(ET)] + [("dbl",)] + [("dt", et) for et in range(ET)])
    w_in = core.sem("m_in_w")
    zeroed = core.sem("m_zeroed")
    waited = core.sem("m_waited")
    conv_step = core.sem("m_conv_step")
    u_ready = core.sem("m_u_ready")
    neg_abs = core.sem("m_neg_abs")
    e_ready = core.sem("m_e_ready")
    one_e_ready = core.sem("m_one_e_ready")
    log_ready = core.sem("m_log_ready")
    log_step = core.sem("m_log_step")
    delta_ready = core.sem("m_delta_ready")
    products = core.sem("m_products")
    stored = core.sem("m_stored")
    STORES = 4 * 16

    with nc.Block() as block:
        @block.sync
        def _(sp):
            sp.dma_start(w_in_t[:], dram["m_in_t"].rearrange("(k p) e -> p k e", p=P)).then_inc(w_in, 16)
            sp.dma_start(ctx_t[:], dram["ctx_t"].rearrange("b (k p) t -> p b k t", p=P)).then_inc(w_in, 16)
            sp.dma_start(w_x[:], dram["m_x_t"].rearrange("(k p) o -> p k o", p=P)).then_inc(w_in, 16)
            sp.dma_start(w_dt[:], dram["m_dt_t"]).then_inc(w_in, 16)
            sp.dma_start(cols[:], dram["m_cols"].rearrange("(k p) o -> p k o", p=P)).then_inc(w_in, 16)
            with sp.Fori(0, B) as i:
                b, turn = ring.at(("dbl",), i)
                sp.wait_ge(ring.free[b], turn + 1)
                sp.dma_start(scratch["bc"][i], dbl[DR:DR + 2 * DS, :]).then_inc(stored, 16)
                sp.wait_ge(products, (i + 1) * ET + 1)
                for name, tile in (("delta", delta), ("delta_u", delta_u), ("y", d_u)):
                    sp.dma_start(scratch[name][i], tile[:]).then_inc(stored, 16)
            sp.wait_ge(stored, B * STORES + 1)

        @block.tensor
        def _(pe):
            start_at_one(pe, conv_step, products, u_ready, stored, *ring.free)
            pe.wait_ge(w_in, 16 * 5)
            with pe.Fori(0, B) as i:
                for et in range(ET):
                    b, turn = ring.at(("x", et), i)
                    pe.wait_ge(ring.free[b], turn)
                    for k in range(KC):
                        mm = nc.tensor.matmul(banks[b][:], w_in_t[:, k, et * P:(et + 1) * P], ctx_t[:, i, k, :],
                                              start=(k == 0), stop=(k == KC - 1))
                    mm.then_inc(ring.full[b], 1)
                pe.wait_ge(u_ready, (i + 1) * ET + 1)
                b, turn = ring.at(("dbl",), i)
                pe.wait_ge(ring.free[b], turn)
                for et in range(ET):
                    mm = nc.tensor.matmul(banks[b][0:DR + 2 * DS, :], w_x[:, et, :], u[:, et, :],
                                          start=(et == 0), stop=(et == ET - 1))
                mm.then_inc(ring.full[b], 1)
                pe.wait_ge(ring.free[b], turn + 1)
                for et in range(ET):
                    b, turn = ring.at(("dt", et), i)
                    pe.wait_ge(ring.free[b], turn)
                    nc.tensor.matmul(banks[b][:], w_dt[:, et * P:(et + 1) * P], dbl[0:DR, :],
                                     start=True, stop=True).then_inc(ring.full[b], 1)

        @block.scalar
        def _(act):
            act.wait_ge(w_in, 16 * 5)
            with act.Fori(0, B) as i:
                for et in range(ET):
                    b, turn = ring.at(("x", et), i)
                    act.wait_ge(ring.full[b], turn)
                    act.wait_ge(conv_step, i * (ET * DC) + 1)
                    nc.scalar.copy(padded[:, et, DC - 1:], banks[b][:]).then_inc(ring.free[b], 1)
                act.wait_ge(products, i * ET + 1)
                for et in range(ET):
                    act.wait_ge(conv_step, i * (ET * DC) + (DC - 1) * ET + et + 1 + 1)
                    nc.scalar.activation(u[:, et, :], conv[:, et, :], ACT.Silu, bias=cols[:, et, DC:DC + 1]) \
                        .then_inc(u_ready, 1)
                for et in range(ET):
                    act.wait_ge(neg_abs, i * ET + et + 1)
                    nc.scalar.activation(e[:, et, :], e[:, et, :], ACT.Exp).then_inc(e_ready, 1)
                for et in range(ET):
                    act.wait_ge(one_e_ready, i * ET + et + 1)
                    nc.scalar.activation(log1p[:, et, :], one_e[:, et, :], ACT.Ln).then_inc(log_ready, 1)

        @block.vector
        def _(dve):
            nc.vector.memset(padded[:, :, 0:DC - 1], 0.0).then_inc(zeroed, 1)
            dve.wait_ge(w_in, 16 * 5)
            dve.wait_ge(zeroed, 1)
            with dve.Fori(0, B) as i:
                dve.wait_ge(u_ready, i * ET + 1)
                for tap in range(DC):
                    for et in range(ET):
                        src = padded[:, et, tap:tap + T]
                        if tap == 0:
                            b, turn = ring.at(("x", et), i)
                            dve.wait_ge(ring.free[b], turn + 1)
                            ins = nc.vector.tensor_scalar(conv[:, et, :], src, cols[:, et, 0:1], None, ALU.mult)
                        else:
                            dve.wait_ge(conv_step, i * (ET * DC) + (tap - 1) * ET + et + 1 + 1)
                            ins = nc.vector.scalar_tensor_tensor(
                                out=conv[:, et, :], in0=src, scalar=cols[:, et, tap:tap + 1],
                                in1=conv[:, et, :], op0=ALU.mult, op1=ALU.add)
                        ins.then_inc(conv_step, 1)
                b, turn = ring.at(("dbl",), i)
                dve.wait_ge(ring.full[b], turn)
                dve.wait_ge(stored, i * STORES + 1)
                nc.vector.tensor_copy(dbl[:], banks[b][0:DR + 2 * DS, :]).then_inc(ring.free[b], 1)
                for et in range(ET):
                    b, turn = ring.at(("dt", et), i)
                    dve.wait_ge(ring.full[b], turn)
                    nc.vector.tensor_scalar(dt[:, et, :], banks[b][:], cols[:, et, DC + 1:DC + 2], None, ALU.add) \
                        .then_inc(ring.free[b], 1)
                for et in range(ET):
                    b, turn = ring.at(("dt", et), i)
                    dve.wait_ge(ring.free[b], turn + 1)
                    nc.vector.scalar_tensor_tensor(out=e[:, et, :], in0=dt[:, et, :], scalar=-1.0, in1=dt[:, et, :],
                                                   op0=ALU.mult, op1=ALU.min).then_inc(neg_abs, 1)
                for et in range(ET):
                    dve.wait_ge(log_ready, i * ET + et + 1)
                    nc.vector.scalar_tensor_tensor(out=e[:, et, :], in0=one_e[:, et, :], scalar=1.0, in1=e[:, et, :],
                                                   op0=ALU.subtract, op1=ALU.subtract).then_inc(log_step, 1)
                for et in range(ET):
                    dve.wait_ge(log_step, i * (2 * ET) + et + 1)
                    nc.vector.tensor_tensor(log1p[:, et, :], log1p[:, et, :], e[:, et, :], ALU.subtract) \
                        .then_inc(log_step, 1)
                for et in range(ET):
                    dve.wait_ge(log_step, i * (2 * ET) + ET + et + 1)
                    nc.vector.scalar_tensor_tensor(out=delta[:, et, :], in0=dt[:, et, :], scalar=0.0,
                                                   in1=log1p[:, et, :], op0=ALU.max, op1=ALU.add) \
                        .then_inc(delta_ready, 1)

        @block.gpsimd
        def _(pool):
            pool.wait_ge(w_in, 16 * 5)
            with pool.Fori(0, B) as i:
                for et in range(ET):
                    wait_apart(pool, e_ready, i * ET + et + 1, waited)
                    nc.gpsimd.tensor_scalar(one_e[:, et, :], e[:, et, :], 1.0, 1.0, ALU.mult, ALU.add) \
                        .then_inc(one_e_ready, 1)
                for et in range(ET):
                    wait_apart(pool, delta_ready, i * ET + et + 1, waited)
                    nc.gpsimd.tensor_scalar(d_u[:, et, :], u[:, et, :], cols[:, et, DC + 2:DC + 3], 1.0,
                                            ALU.mult, ALU.mult)
                    nc.gpsimd.tensor_tensor(delta_u[:, et, :], delta[:, et, :], u[:, et, :], ALU.mult) \
                        .then_inc(products, 1)


def stage_scan(core, sb, psum, dram, scratch, consts):
    nc = core.nc
    a = sb("s_a", [P, ET, DS], F32)
    delta = sb("s_delta", [P, 2, ET, T], F32)
    delta_u = sb("s_delta_u", [P, 2, ET, T], F32)
    y = sb("s_y", [P, 2, ET, T], F32)
    bc = sb("s_bc", [P, 2, 2, NQ, T], F32)
    decay = sb("s_decay", [P, 2, NQ, T], F32)
    state = sb("s_state", [P, 2, NQ, T], F32)
    banks = [psum(f"s_bank{b}", [P, 512], F32) for b in range(2)]
    a_in = core.sem("s_a_in")
    a_step = core.sem("s_a_step")
    seq_in = core.sems("s_seq_in", 2)
    bc_in = core.sems("s_bc_in", 2)
    decay_ready = core.sems("s_decay", 2)
    input_ready = core.sems("s_input", 2)
    scanned = core.sems("s_scanned", 2)
    weighed = core.sems("s_weighed", 2)
    y_full = core.sems("s_y_full", 2)
    y_free = core.sems("s_y_free", 2)
    stored = core.sem("s_stored")
    QUADS = DS // NQ
    CHUNKS_ = QUADS * ET
    HALF = CHUNKS_ // 2
    BC = 2 * 16

    with nc.Block() as block:
        @block.sync
        def _(sp):
            sp.dma_start(a[:], dram["m_a_log"].rearrange("(k p) n -> p k n", p=P)).then_inc(a_in, 16)
            with sp.Fori(0, B // 2) as pair:
                for half in range(2):
                    i = pair * 2 + half
                    sp.wait_ge(stored, i * 16 - half * 16 + 1)
                    for name, tile in (("delta", delta), ("delta_u", delta_u), ("y", y)):
                        sp.dma_start(tile[:, half], scratch[name][i]).then_inc(seq_in[half], 16)
                    for q in range(QUADS):
                        s = q % 2
                        for c in range(2):
                            if q >= 2:
                                sp.wait_ge(weighed[c], i * HALF + (q - 1) * (ET // 2) + 1)
                            else:
                                sp.wait_ge(weighed[c], i * HALF + 1)
                        for n in range(2):
                            rows = scratch["bc"][i, n * DS + q * NQ:n * DS + (q + 1) * NQ, :]
                            sp.dma_start(bc[:, s, n], rows.rearrange("(o n) t -> o n t", o=1)
                                         .broadcast_to([P, NQ, T])).then_inc(bc_in[s], 16)
                    for c in range(2):
                        sp.wait_ge(y_free[c], (i + 1) * HALF + 1)
                    sp.dma_start(scratch["y"][i], y[:, half]).then_inc(stored, 16)
            sp.wait_ge(stored, B * 16 + 1)

        @block.tensor
        def _(pe):
            start_at_one(pe, stored, *weighed, *y_free, *scanned, *y_full)
            with pe.Fori(0, B) as i:
                for c in range(CHUNKS_):
                    s, n = c % 2, i * HALF + c // 2
                    pe.wait_ge(weighed[s], n + 1 + 1)
                    pe.wait_ge(y_free[s], n + 1)
                    for q in range(NQ):
                        mm = nc.tensor.matmul(banks[s][:], consts.ident[:], state[:, s, q, :],
                                              start=(q == 0), stop=(q == NQ - 1))
                    mm.then_inc(y_full[s], 1)

        @block.scalar
        def _(act):
            act.wait_ge(a_in, 16)
            nc.scalar.activation(a[:], a[:], ACT.Exp).then_inc(a_step, 1)
            act.wait_ge(a_step, 3)
            with act.Fori(0, B // 2) as pair:
                for half in range(2):
                    i = pair * 2 + half
                    act.wait_ge(seq_in[half], pair * 48 + 48)
                    for c in range(CHUNKS_):
                        s, n = c % 2, i * HALF + c // 2
                        q, et = c // ET, c % ET
                        act.wait_ge(scanned[s], n + 1)
                        for u in range(NQ):
                            st = q * NQ + u
                            ins = nc.scalar.activation(decay[:, s, u, 1:], delta[:, half, et, 1:], ACT.Exp,
                                                       scale=a[:, et, st:st + 1])
                        ins.then_inc(decay_ready[s], 1)

        @block.gpsimd
        def _(pool):
            with pool.Fori(0, B // 2) as pair:
                for half in range(2):
                    i = pair * 2 + half
                    pool.wait_ge(seq_in[half], pair * 48 + 48)
                    for c in range(CHUNKS_):
                        s, n = c % 2, i * HALF + c // 2
                        q, et = c // ET, c % ET
                        if et == 0:
                            pool.wait_ge(bc_in[q % 2], i * (QUADS // 2 * BC) + (q // 2 + 1) * BC)
                        pool.wait_ge(y_full[s], n + 1)
                        nc.gpsimd.tensor_tensor(state[:, s], bc[:, q % 2, 0],
                                                delta_u[:, half, et, :].rearrange("p (o t) -> p o t", o=1)
                                                .broadcast_to([P, NQ, T]), ALU.mult).then_inc(input_ready[s], 1)

        @block.vector
        def _(dve):
            nc.vector.memset(decay[:, :, :, 0:1], 0.0).then_inc(a_step, 1)
            dve.wait_ge(a_step, 2)
            nc.vector.tensor_scalar(a[:], a[:], -1.0, None, ALU.mult).then_inc(a_step, 1)

            with dve.Fori(0, B // 2) as pair:
                for half in range(2):
                    i = pair * 2 + half

                    def add(c):
                        s, n = c % 2, i * HALF + c // 2
                        dve.wait_ge(y_full[s], n + 1 + 1)
                        if c >= ET:
                            dve.wait_ge(y_free[(c - ET) % 2], i * HALF + (c - ET) // 2 + 1 + 1)
                        nc.vector.tensor_tensor(y[:, half, c % ET, :], banks[s][:], y[:, half, c % ET, :], ALU.add) \
                            .then_inc(y_free[s], 1)

                    dve.wait_ge(seq_in[half], pair * 48 + 48)
                    for c in range(CHUNKS_):
                        s, n = c % 2, i * HALF + c // 2
                        q = c // ET
                        dve.wait_ge(decay_ready[s], n + 1)
                        dve.wait_ge(input_ready[s], n + 1)
                        flat = state[:, s].rearrange("p n t -> p (n t)")
                        nc.vector.tensor_tensor_scan(flat, decay[:, s].rearrange("p n t -> p (n t)"), flat,
                                                     0.0, ALU.mult, ALU.add).then_inc(scanned[s], 1)
                        if c:
                            add(c - 1)
                        dve.wait_ge(scanned[s], n + 1 + 1)
                        dve.wait_ge(bc_in[q % 2], i * (QUADS // 2 * BC) + (q // 2 + 1) * BC)
                        nc.vector.tensor_tensor(state[:, s], state[:, s], bc[:, q % 2, 1], ALU.mult) \
                            .then_inc(weighed[s], 1)
                    add(CHUNKS_ - 1)


def stage_gate(core, sb, psum, dram, x, consts, scratch):
    nc = core.nc
    norm = Norm(core, sb, "g")
    y = sb("g_y", [P, B, ET, T], F32)
    z = sb("g_z", [P, ET, T], F32)
    gy = sb("g_gy", [P, ET, T], F32)
    banks = [psum(f"g_bank{b}", [P, 512], F32) for b in range(TT)]
    y_in = core.sem("g_y_in")
    silu_done = core.sem("g_silu")
    gated = core.sem("g_gated")
    full = core.sems("g_full", TT)
    free = core.sems("g_free", TT)

    with nc.Block() as block:
        @block.sync
        def _(sp):
            for b in range(B):
                sp.dma_start(y[:, b], scratch["y"][b]).then_inc(y_in, 16)

        @block.scalar
        def _(act):
            with act.Fori(0, B) as i:
                act.wait_ge(norm.xn_ready, (i + 1) * TT)
                act.wait_ge(gated, i * ET + 1)
                for et in range(ET):
                    nc.scalar.activation(z[:, et, :], norm.xn[:, et, :], ACT.Silu).then_inc(silu_done, 1)

        @block.gpsimd
        def _(pool):
            pool.wait_ge(y_in, 16 * B)
            with pool.Fori(0, B) as i:
                norm_gpsimd(nc, pool, norm, consts.minus_half, i)
                for tt in range(TT):
                    pool.wait_ge(full[tt], i + 1)
                for et in range(ET):
                    pool.wait_ge(silu_done, i * ET + et + 1 + 1)
                    nc.gpsimd.tensor_tensor(gy[:, et, :], y[:, i, et, :], z[:, et, :], ALU.mult).then_inc(gated, 1)

        @block.tensor
        def _(pe):
            start_at_one(pe, gated, *free, silu_done, *full)
            with pe.Fori(0, B) as i:
                pe.wait_ge(gated, (i + 1) * ET + 1)
                for tt in range(TT):
                    pe.wait_ge(free[tt], i + 1)
                    for et in range(ET):
                        mm = nc.tensor.transpose(banks[tt][:, et * P:(et + 1) * P],
                                                 gy[:, et, tt * P:(tt + 1) * P], consts.ident[:])
                    mm.then_inc(full[tt], 1)

        @block.vector
        def _(dve):
            with dve.Fori(0, B) as i:
                dve.wait_ge(silu_done, i * ET + 1)
                norm_vector(nc, dve, norm, x, i)
                for tt in range(TT):
                    dve.wait_ge(full[tt], i + 1 + 1)
                    nc.vector.tensor_tensor(x[:, i, tt, :], banks[tt][:], x[:, i, tt, :], ALU.add) \
                        .then_inc(free[tt], 1)


def stage_mix(core, sb, psum, dram, x, consts):
    nc = core.nc
    norm = Norm(core, sb, "r")
    factors = sb("r_factors", [P, RANK, KD, D], F32)
    bias = sb("r_bias", [P, D], F32)
    xn_t = sb("r_xn_t", [P, KD, T], F32)
    res = sb("r_res", [P, 2, TT, D], F32)
    banks = [psum(f"r_bank{b}", [P, 512], F32) for b in range(8)]
    ring = Ring(core.sems("r_full", 8), core.sems("r_free", 8),
                [("xn", k) for k in range(KD)] + [("out", tt) for tt in range(TT)])
    w_in = core.sems("r_in", RANK)
    bias_in = core.sem("r_bias_in")
    summed = core.sem("r_summed")
    biased = core.sem("r_biased")
    stored = core.sems("r_stored", 2)

    with nc.Block() as block:
        @block.sync
        def _(sp):
            for r in range(RANK):
                sp.dma_start(factors[:, r], dram["factors"][r].rearrange("(k p) e -> p k e", p=P)) \
                    .then_inc(w_in[r], 16)
            sp.dma_start(bias[:], dram["bias"].rearrange("(o e) -> o e", o=1).broadcast_to([P, D])) \
                .then_inc(bias_in, 16)
            with sp.Fori(0, B // 2) as pair:
                for s in range(2):
                    i = pair * 2 + s
                    for tt in range(TT):
                        b, turn = ring.at(("out", tt), i)
                        sp.wait_ge(ring.free[b], turn + 1)
                        sp.dma_start(dram["out"][i, tt * P:(tt + 1) * P, :], res[:, s, tt, :]) \
                            .then_inc(stored[s], 16)
            for s in range(2):
                sp.wait_ge(stored[s], B // 2 * TT * 16 + 1)

        @block.gpsimd
        def _(pool):
            for r in range(1, RANK):
                pool.wait_ge(w_in[r], 16)
                if r == 1:
                    pool.wait_ge(w_in[0], 16)
                else:
                    pool.wait_ge(summed, r - 1)
                nc.gpsimd.tensor_tensor(factors[:, 0], factors[:, 0], factors[:, r], ALU.add).then_inc(summed, 1)
            pool.wait_ge(bias_in, 16)
            with pool.Fori(0, B) as i:
                norm_gpsimd(nc, pool, norm, consts.minus_half, i)
                pool.wait_ge(norm.xn_ready, (i + 1) * TT)
                for tt in range(TT):
                    nc.gpsimd.tensor_tensor(x[:, i, tt, :], x[:, i, tt, :], bias[:], ALU.add).then_inc(biased, 1)

        @block.tensor
        def _(pe):
            start_at_one(pe, *stored, *ring.free)
            with pe.Fori(0, B) as i:
                norm_tensor(nc, pe, norm, consts.ident, ring, banks, i)
                ring.wait_free(pe, i, consumed=[("xn", k) for k in range(KD)])
                pe.wait_ge(summed, RANK - 1)
                for tt in range(TT):
                    b, turn = ring.at(("out", tt), i)
                    pe.wait_ge(ring.free[b], turn)
                    for k in range(KD):
                        mm = nc.tensor.matmul(banks[b][:], xn_t[:, k, tt * P:(tt + 1) * P], factors[:, 0, k, :],
                                              start=(k == 0), stop=(k == KD - 1))
                    mm.then_inc(ring.full[b], 1)

        @block.scalar
        def _(act):
            with act.Fori(0, B) as i:
                for k in range(KD):
                    b, turn = ring.at(("xn", k), i)
                    act.wait_ge(ring.full[b], turn)
                    nc.scalar.copy(xn_t[:, k, :], banks[b][:]).then_inc(ring.free[b], 1)

        @block.vector
        def _(dve):
            with dve.Fori(0, B // 2) as pair:
                for s in range(2):
                    i = pair * 2 + s
                    norm_vector(nc, dve, norm, x, i)
                    dve.wait_ge(stored[s], pair * (TT * 16) + 1)
                    for tt in range(TT):
                        b, turn = ring.at(("out", tt), i)
                        dve.wait_ge(ring.full[b], turn)
                        dve.wait_ge(biased, i * TT + tt + 1)
                        nc.vector.scalar_tensor_tensor(out=res[:, s, tt, :], in0=banks[b][:],
                                                       scalar=1.0 / math.sqrt(RANK), in1=x[:, i, tt, :],
                                                       op0=ALU.mult, op1=ALU.add).then_inc(ring.free[b], 1)


_WEIGHTS = ("wq_t", "wk_t", "wv_t", "wo_t", "cos2", "sin2", "x_wq_t", "x_wk_t", "x_bq", "x_bk", "ctx_t",
            "lut", "idx", "d_w", "d_wp", "lq1", "lk1", "lq2", "lk2", "rowsel", "m_in_t", "m_x_t",
            "m_dt_t", "m_cols", "m_a_log", "factors", "bias", "identity", "masks", "x")
STAGES = ("A", "B", "W", "C", "D", "M", "S", "G", "R")


def program(nc, dram, stages=STAGES, dump=None):
    scratch = {
        "bc": nc.dram_tensor("scan_bc", [B, 2 * DS, T], F32, kind="Internal").ap(),
        "delta": nc.dram_tensor("scan_delta", [B, P, ET, T], F32, kind="Internal").ap(),
        "delta_u": nc.dram_tensor("scan_delta_u", [B, P, ET, T], F32, kind="Internal").ap(),
        "y": nc.dram_tensor("scan_y", [B, P, ET, T], F32, kind="Internal").ap(),
    }
    with ExitStack() as whole:
        core = Core(nc)

        def keeper(stack):
            return (lambda n, s, d: stack.enter_context(nc.sbuf_tensor(n, s, d)),
                    lambda n, s, d: stack.enter_context(nc.psum_tensor(n, s, d)))

        sb, _ = keeper(whole)
        x = sb("x_res", [P, B, TT, D], F32)
        consts = Consts(sb)
        with ExitStack() as stage:
            sb, psum = keeper(stage)
            stage_setup(core, sb, dram, x, consts)
        core.clear()
        if "A" in stages:
            with ExitStack() as stage:
                stage_window_attention(core, *keeper(stage), dram, x, consts)
            core.clear()
        if "B" in stages:
            with ExitStack() as stage:
                stage_cross_attention(core, *keeper(stage), dram, x, consts)
            core.clear()
        if "C" in stages:
            with ExitStack() as ffn:
                weights = keeper(ffn)[0]("ffn_w", [P, W_ALL], F32)
                with ExitStack() as stage:
                    stage_ffn_weights(core, keeper(stage)[0], dram, weights)
                core.clear()
                with ExitStack() as stage:
                    stage_ffn(core, *keeper(stage), dram, x, consts, weights)
                core.clear()
        if "D" in stages:
            with ExitStack() as stage:
                stage_diff_attention(core, *keeper(stage), dram, x, consts)
            core.clear()
        if "M" in stages:
            with ExitStack() as stage:
                stage_scan_inputs(core, *keeper(stage), dram, scratch)
            core.clear()
            with ExitStack() as stage:
                stage_scan(core, *keeper(stage), dram, scratch, consts)
            core.clear()
            with ExitStack() as stage:
                stage_gate(core, *keeper(stage), dram, x, consts, scratch)
            core.clear()
        if "R" in stages:
            with ExitStack() as stage:
                stage_mix(core, *keeper(stage), dram, x, consts)
            core.clear()
        if dump is not None:
            done = core.sem("dumped")
            with nc.Block() as block:
                @block.sync
                def _(sp):
                    for b in range(B):
                        sp.dma_start(dram["out"][b].rearrange("(t p) d -> p t d", p=P), x[:, b]).then_inc(done, 16)
                    sp.wait_ge(done, 16 * B)


def laid_out(v):
    c = np.ascontiguousarray
    out = {
        "x": v["x"], "ctx_t": c(v["ctx_1024"].transpose(0, 2, 1)),
        "wq_t": c(v["L0_attn_wq"].T), "wk_t": c(v["L0_attn_wk"].T), "wv_t": c(v["L0_attn_wv"].T),
        "wo_t": c(v["L0_attn_wo"].T),
        "x_wq_t": c(v["L0_xattn_Wq"].T), "x_wk_t": c(v["L0_xattn_Wk"].T),
        "x_bq": v["L0_xattn_bq"], "x_bk": v["L0_xattn_bk"],
        "lut": v["L0_ffn_lut"],
        "lq1": v["L1_attn_lambda_q1"], "lk1": v["L1_attn_lambda_k1"],
        "lq2": v["L1_attn_lambda_q2"], "lk2": v["L1_attn_lambda_k2"], "d_wp": v["L1_attn_W_proj"],
        "m_in_t": c(v["L1_xattn_in_proj_w"].T), "m_x_t": c(v["L1_xattn_x_proj_w"].T),
        "m_dt_t": c(v["L1_xattn_dt_proj_w"].T), "m_a_log": v["L1_xattn_A_log"],
        "m_cols": c(np.concatenate([v["L1_xattn_conv_w"], v["L1_xattn_conv_b"][:, None],
                                    v["L1_xattn_dt_proj_b"][:, None], v["L1_xattn_D"][:, None]], axis=1)),
        "factors": v["L1_ffn_factors"], "bias": v["L1_ffn_bias"],
    }
    tiles = lambda a: a.reshape(-1, P, a.shape[1]).transpose(1, 0, 2).reshape(P, -1)
    down = np.zeros((OT * P, D), v["L0_ffn_down_idx"].dtype)
    down[:INTER] = v["L0_ffn_down_idx"].T
    out["idx"] = c(np.concatenate([tiles(v["L0_ffn_gate_idx"].T), tiles(v["L0_ffn_up_idx"].T), tiles(down)],
                                  axis=1))
    w = v["L1_attn_W_attn"].reshape(D, 3 * D)
    part = lambda n: w[:, n * (D // 2):(n + 1) * (D // 2)].reshape(D, DH, DHD)
    out["d_w"] = c(np.concatenate([np.concatenate([part(0), part(2)], axis=2).reshape(D, D),
                                   np.concatenate([part(1), part(3)], axis=2).reshape(D, D),
                                   w[:, 2 * D:]], axis=1))
    half = HD // 2
    inv_freq = (1.0 / np.float32(10000.0) ** (np.arange(half, dtype=np.float32) / np.float32(half)))
    freqs = np.outer(np.arange(T, dtype=np.float32), inv_freq.astype(np.float32))
    cos, sin = np.cos(freqs).T.astype(np.float32), np.sin(freqs).T.astype(np.float32)
    out["cos2"], out["sin2"] = c(np.concatenate([cos, cos])), c(np.concatenate([-sin, sin]))
    out["identity"] = np.eye(P, dtype=np.float32)
    row, col = np.arange(P)[:, None], np.arange(2 * P)[None, :]
    own = (col - P <= row) & (col >= P)
    seen = np.stack([own, own | ((col < P) & (row + P - col <= WINDOW))])
    out["masks"] = c(np.where(seen, 0.0, MASKED).astype(np.float32).transpose(1, 0, 2))
    q2 = (np.arange(P) // DHD) % 2
    out["rowsel"] = c(np.stack([1 - q2, q2], axis=1).astype(np.float32) * np.float32(DHD ** -0.5))
    return out


def kernel(**inputs):
    import concourse.bacc as bacc
    from concourse.bass_utils import run_bass_kernel_spmd

    nc = bacc.Bacc("TRN2", target_bir_lowering=False, num_devices=1)
    arrays = {f"in_{k}": a for k, a in laid_out({k: np.asarray(a) for k, a in inputs.items()}).items()}
    dram = {n[3:]: nc.dram_tensor(n, a.shape, mybir.dt.from_np(a.dtype), kind="ExternalInput").ap()
            for n, a in arrays.items()}
    dram["out"] = nc.dram_tensor("out", [B, T, D], F32, kind="ExternalOutput").ap()
    program(nc, dram)
    return run_bass_kernel_spmd(nc, [arrays], core_ids=[0]).results[0]["out"]
```

```python
import math
from contextlib import ExitStack

import numpy as np

import concourse.bass as bass
from concourse import mybir

ALU = mybir.AluOpType
ACT = mybir.ActivationFunctionType
AX_X = mybir.AxisListType.X
F32 = mybir.dt.float32
F32R = mybir.dt.float32r
BF16 = mybir.dt.bfloat16
I32 = mybir.dt.int32

P = 128
B, T, D = 4, 512, 512
TT = T // P
KD = D // P
C = 256
KC = C // P
EPS = 1e-5
HEADS, KV, HD = 16, 4, 128
REPS = HEADS // KV
WINDOW = 128
MASKED = -1e30
QK = 128
INTER = 1376
OT = -(-INTER // P)
LUT = 16
DH, DHD = 16, 16
LAMBDA_INIT = 0.8 - 0.6 * math.exp(-0.3 * 0)
DI, DS, DC, DR = 512, 16, 4, 16
ET = DI // P
NQ = 4
NS = 2
RANK = 8
W_UP, W_DOWN = KD * INTER, 2 * KD * INTER
W_ALL = W_DOWN + OT * D
CHUNKS = 64
CH = W_ALL // CHUNKS


class Ring:

    def __init__(self, full, free, steps, last_steps=None):
        self.full, self.free = full, free
        self.place, self.per = self.deal(steps)
        self.last_place = self.place if last_steps is None else self.deal(last_steps)[0]

    def deal(self, steps):
        per, place = [0] * len(self.full), {}
        for n, step in enumerate(steps):
            b = n % len(self.full)
            assert step not in place, step
            place[step] = (b, per[b])
            per[b] += 1
        return place, per

    def placed(self, step, i):
        return (self.last_place if isinstance(i, int) and i == B - 1 else self.place)[step]

    def at(self, step, i):
        b, nth = self.placed(step, i)
        return b, i * self.per[b] + nth + 1

    def wait_free(self, eng, i, out=None, consumed=()):
        need = {}
        if out is not None:
            b, nth = self.placed(out, i)
            need[b] = nth
        for step in consumed:
            b, nth = self.placed(step, i)
            need[b] = max(need.get(b, 0), nth + 1)
        for b, count in need.items():
            eng.wait_ge(self.free[b], i * self.per[b] + count + 1)


class Core:

    def __init__(self, nc):
        self.nc, self.taken = nc, []

    def sem(self, name):
        self.taken.append(self.nc.alloc_semaphore(name=name))
        return self.taken[-1]

    def sems(self, name, n):
        return [self.sem(f"{name}{k}") for k in range(n)]

    def clear(self):
        self.nc.clear_and_free_semaphores(self.taken)
        self.taken = []
        self.nc.all_engine_barrier()


class Consts:
    def __init__(self, sb):
        self.ident = sb("ident", [P, P], F32)
        self.ident_bf = sb("ident_bf", [P, P], BF16)
        self.mask_bf = sb("mask_bf", [P, 2, 2 * P], BF16)
        self.minus_half = sb("minus_half", [P, TT], F32)
        self.ones = sb("ones", [P, P], F32)


class Norm:

    def __init__(self, core, sb, tag):
        self.stats_done = core.sem(f"{tag}_ln_stats")
        self.waited = core.sem(f"{tag}_ln_waited")
        self.var_ready = core.sem(f"{tag}_ln_var")
        self.rstd_ready = core.sem(f"{tag}_ln_rstd")
        self.xn_ready = core.sem(f"{tag}_ln_xn")
        self.stats = sb(f"{tag}_stats", [P, TT, 6], F32)
        self.mean_var = sb(f"{tag}_mean_var", [P, TT, 2], F32)
        self.var_eps = sb(f"{tag}_var_eps", [P, TT], F32)
        self.rstd = sb(f"{tag}_rstd", [P, TT], F32)
        self.xn = sb(f"{tag}_xn", [P, TT, D], F32)


def start_at_one(eng, *sems):
    for sem in sems:
        eng.sem_inc(sem, 1)


def wait_apart(eng, sem, value, waited):
    eng.wait_ge(sem, value)
    eng.sem_inc(waited, 1)


def passes(eng, one_pass):
    with eng.Fori(0, B - 1) as i:
        one_pass(i, True)
    one_pass(B - 1, False)


def norm_vector(nc, dve, norm, x, i):
    for tt in range(TT):
        last = nc.vector.bn_stats(norm.stats[:, tt, :], x[:, i, tt, :])
    last.then_inc(norm.stats_done, 1)
    wait_apart(dve, norm.stats_done, i * 2 + 1, norm.waited)
    for tt in range(TT):
        last = nc.vector.bn_aggr(norm.mean_var[:, tt, :], norm.stats[:, tt, :])
    last.then_inc(norm.stats_done, 1)
    dve.wait_ge(norm.stats_done, i * 2 + 2)
    nc.vector.tensor_scalar(norm.var_eps[:], norm.mean_var[:, :, 1], EPS, None, ALU.add) \
        .then_inc(norm.var_ready, 1)
    dve.wait_ge(norm.rstd_ready, i + 1)
    for tt in range(TT):
        nc.vector.tensor_scalar(norm.xn[:, tt, :], x[:, i, tt, :], norm.mean_var[:, tt, 0:1],
                                norm.rstd[:, tt:tt + 1], ALU.subtract, ALU.mult) \
            .then_inc(norm.xn_ready, 1)


def norm_gpsimd(nc, pool, norm, minus_half, i):
    pool.wait_ge(norm.var_ready, i + 1)
    nc.gpsimd.tensor_tensor(norm.rstd[:], norm.var_eps[:], minus_half[:], ALU.pow) \
        .then_inc(norm.rstd_ready, 1)


def norm_tensor(nc, pe, norm, ident, ring, banks, i, in_pass=None):
    pe.wait_ge(norm.xn_ready, (i + 1) * TT)
    for k in range(KD):
        b, turn = ring.at(("xn", k), i if in_pass is None else in_pass)
        pe.wait_ge(ring.free[b], turn)
        for tt in range(TT):
            mm = nc.tensor.transpose(banks[b][:, tt * P:(tt + 1) * P],
                                     norm.xn[:, tt, k * P:(k + 1) * P], ident[:])
        mm.then_inc(ring.full[b], 1)


def stage_setup(core, sb, dram, x, consts):
    nc = core.nc
    loaded = core.sem("setup_loaded")
    mask_f = sb("mask_f", [P, 2, 2 * P], F32)
    with nc.Block() as block:
        @block.sync
        def _(sp):
            sp.dma_start(consts.ident[:], dram["identity"]).then_inc(loaded, 16)
            sp.dma_start(mask_f[:], dram["masks"]).then_inc(loaded, 16)
            for b in range(B):
                sp.dma_start(x[:, b], dram["x"][b].rearrange("(t p) d -> p t d", p=P)) \
                    .then_inc(loaded, 16)
            sp.wait_ge(loaded, 16 * (2 + B))

        @block.vector
        def _(dve):
            nc.vector.memset(consts.minus_half[:], -0.5)
            nc.vector.memset(consts.ones[:], 1.0)
            dve.wait_ge(loaded, 16 * (2 + B))
            nc.vector.tensor_copy(consts.ident_bf[:], consts.ident[:])
            nc.vector.tensor_copy(consts.mask_bf[:], mask_f[:])


class Lookup:
    PER_PASS = CHUNKS // B
    STEPS = 5

    def __init__(self, core, sb, dram, scratch):
        self.nc, self.dram, self.scratch = core.nc, dram, scratch
        self.lut = sb("f_lut", [P, LUT], I32)
        self.lut_xor = sb("f_lut_xor", [P, LUT // 2], I32)
        self.idx = sb("f_idx", [P, 2, CH], I32)
        self.mask = sb("f_mask", [P, 4, CH], I32)
        self.picks = sb("f_picks", [P, LUT // 2, CH], I32)
        self.lut_in = core.sem("f_lut_in")
        self.lut_ready = core.sem("f_lut_ready")
        self.waited = core.sem("f_waited")
        self.idx_in = core.sems("f_idx_in", 2)
        self.step_done = core.sem("f_step")
        self.stored = core.sem("f_stored")

    def load_table(self, sp):
        sp.dma_start(self.lut[:], self.dram["lut"].bitcast(I32).rearrange("(o l) -> o l", o=1)
                     .broadcast_to([P, LUT])).then_inc(self.lut_in, 16)

    def step_value(self, i, n, steps):
        return (i * self.PER_PASS + n) * self.STEPS + steps + 1

    def sync(self, sp, i):
        def store(n):
            sp.wait_ge(self.step_done, self.step_value(i, n, self.STEPS))
            sp.dma_start(self.scratch["weights"][:, bass.ds(i * (self.PER_PASS * CH) + n * CH, CH)],
                         self.picks[:, 0, :]).then_inc(self.stored, 16)

        for n in range(self.PER_PASS):
            if n == 1:
                sp.wait_ge(self.step_done, self.step_value(i, 0, 0))
            elif n > 1:
                sp.wait_ge(self.step_done, self.step_value(i, n - 2, 1))
            sp.dma_start(self.idx[:, n % 2, :],
                         self.dram["idx"][:, bass.ds(i * (self.PER_PASS * CH) + n * CH, CH)]) \
                .then_inc(self.idx_in[n % 2], 16)
            if n:
                store(n - 1)
        store(self.PER_PASS - 1)

    def sync_end(self, sp):
        sp.wait_ge(self.stored, 16 * CHUNKS + 1)

    def vector_setup(self, dve):
        start_at_one(dve, self.step_done, self.stored)
        dve.wait_ge(self.lut_in, 16)
        pairs = self.lut[:].rearrange("p (j two) -> p j two", two=2)
        self.nc.vector.tensor_tensor(self.lut_xor[:], pairs[:, :, 0], pairs[:, :, 1], ALU.bitwise_xor) \
            .then_inc(self.lut_ready, 1)
        dve.wait_ge(self.lut_ready, 1)

    def vector(self, i, n):
        dve, mask, picks, s = self.nc.vector, self.mask, self.picks, n % 2

        def own_step(steps):
            wait_apart(dve, self.step_done, self.step_value(i, n, steps), self.waited)

        dve.wait_ge(self.idx_in[s], (i * (self.PER_PASS // 2) + n // 2 + 1) * 16)
        own_step(0)
        dve.tensor_scalar(mask[:, 0, :], self.idx[:, s, :], 31, 31,
                          ALU.logical_shift_left, ALU.arith_shift_right)
        for bit in range(1, 4):
            last = dve.tensor_scalar(mask[:, bit, :], self.idx[:, s, :], 1 << bit, None, ALU.bitwise_and)
        last.then_inc(self.step_done, 1)
        own_step(1)
        for j in reversed(range(LUT // 2)):
            if j == 0:
                dve.wait_ge(self.stored, (i * self.PER_PASS + n) * 16 + 1)
            last = dve.tensor_scalar(picks[:, j, :], mask[:, 0, :], self.lut_xor[:, j:j + 1],
                                     self.lut[:, 2 * j:2 * j + 1], ALU.bitwise_and, ALU.bitwise_xor)
        last.then_inc(self.step_done, 1)
        own_step(2)
        for level in range(3):
            half = 1 << level
            for j in range(0, LUT // 2, 2 * half):
                last = dve.copy_predicated(picks[:, j, :], mask[:, level + 1, :], picks[:, j + half, :])
            last.then_inc(self.step_done, 1)
            if level < 2:
                own_step(3 + level)


def stage_window_attention(core, sb, psum, dram, x, consts, scratch):
    nc = core.nc
    scale = 1.0 / math.sqrt(HD)
    wq = sb("a_wq", [P, KD, HEADS * HD], F32)
    wk = sb("a_wk", [P, KD, KV * HD], F32)
    wv = sb("a_wv", [P, KD, KV * HD], F32)
    wo = sb("a_wo", [P, HEADS, D], F32)
    cos2 = sb("a_cos2", [P, T], F32)
    sin2 = sb("a_sin2", [P, T], F32)
    norm = Norm(core, sb, "a")
    xn_t = sb("a_xn_t", [P, KD, T], F32)
    q_t = sb("a_q_t", [P, REPS, T], F32)
    k_t = sb("a_k_t", [P, T], F32)
    v = sb("a_v", [P, TT, KV * HD], F32)
    rope_a = sb("a_rope_a", [P, 2, T], F32)
    rope_b = sb("a_rope_b", [P, 2, T], F32)
    prob = sb("a_prob", [P, REPS, TT, 2 * P], F32)
    prob_t = sb("a_prob_t", [P, 2, 2, REPS * P], F32)
    out_t = sb("a_out_t", [P, TT, REPS * P], F32)
    mx = sb("a_mx", [P, HEADS, TT], F32)
    neg_m = sb("a_neg_m", [P, HEADS, TT], F32)
    sums = sb("a_sums", [P, HEADS, TT], F32)
    rsum = sb("a_rsum", [P, HEADS, TT], F32)

    banks = [psum(f"a_bank{b}", [P, 512], F32) for b in range(4)]
    score = [psum(f"a_score{s}", [P, TT, 2 * P], F32) for s in range(2)]

    proj = lambda g: [("k", g)] + [("q", g, r) for r in range(REPS)]
    xn_steps = [("xn", k) for k in range(KD)]
    v_steps = [("v", tt) for tt in range(TT)]

    def steps(more):
        order = []
        for g in range(KV):
            if g + 1 < KV:
                order += proj(g + 1)
            elif more:
                order += xn_steps + proj(0)
            order += [("turn", g, 0, 0), ("turn", g, 1, 0), ("turn", g, 1, 1), ("pv", g, 0),
                      ("turn", g, 2, 0), ("turn", g, 2, 1), ("pv", g, 1),
                      ("turn", g, 3, 0), ("turn", g, 3, 1), ("pv", g, 2), ("pv", g, 3)]
            order += [("wo", g, tt) for tt in range(TT)]
        return order + (v_steps if more else [])

    ring = Ring(core.sems("a_full", 4), core.sems("a_free", 4), steps(True), steps(False))
    first = Ring(core.sems("a_first_full", 4), core.sems("a_first_free", 4), xn_steps + proj(0) + v_steps)
    lookup = Lookup(core, sb, dram, scratch)

    w_in = {n: core.sem(f"a_in_{n}") for n in ("wk", "wv", "wq", "wo", "rope")}
    rope_done = core.sems("a_rope_done", 2)
    score_full = core.sems("a_score_full", 2)
    max_done = core.sem("a_max_done")
    neg_ready = core.sem("a_neg_ready")
    exp_done = core.sems("a_exp_done", 2)
    waited = core.sem("a_waited")
    rsum_ready = core.sem("a_rsum_ready")
    prob_ready = core.sem("a_prob_ready")
    PER_ROPE = KV * (1 + REPS) // 2
    PER_SLOT = HEADS // 2

    with nc.Block() as block:
        @block.sync
        def _(sp):
            sp.dma_start(wv[:], dram["wv_t"].rearrange("(k p) o -> p k o", p=P)).then_inc(w_in["wv"], 16)
            sp.dma_start(wk[:], dram["wk_t"].rearrange("(k p) o -> p k o", p=P)).then_inc(w_in["wk"], 16)
            sp.dma_start(cos2[:], dram["cos2"]).then_inc(w_in["rope"], 16)
            sp.dma_start(sin2[:], dram["sin2"]).then_inc(w_in["rope"], 16)
            sp.dma_start(wq[:], dram["wq_t"].rearrange("(k p) o -> p k o", p=P)).then_inc(w_in["wq"], 16)
            lookup.load_table(sp)
            sp.dma_start(wo[:], dram["wo_t"].rearrange("(h p) o -> p h o", p=P)).then_inc(w_in["wo"], 16)
            with sp.Fori(0, B) as i:
                lookup.sync(sp, i)
            lookup.sync_end(sp)

        @block.tensor
        def _(pe):
            start_at_one(pe, *rope_done, *exp_done, *ring.free, *first.free)

            def project(ring, i, g):
                for step in proj(g):
                    w = wk[:, :, g * HD:(g + 1) * HD] if step[0] == "k" else \
                        wq[:, :, (g * REPS + step[2]) * HD:(g * REPS + step[2] + 1) * HD]
                    b, turn = ring.at(step, i)
                    pe.wait_ge(ring.free[b], turn)
                    for k in range(KD):
                        mm = nc.tensor.matmul(banks[b][:], w[:, k, :], xn_t[:, k, :],
                                              start=(k == 0), stop=(k == KD - 1))
                    mm.then_inc(ring.full[b], 1)

            def scores(i, g):
                for r in range(REPS):
                    h = g * REPS + r
                    s = h % 2
                    n = g * (1 + REPS) + 1 + r
                    pe.wait_ge(rope_done[n % 2], i * PER_ROPE + n // 2 + 1 + 1)
                    if r % 2 == 0:
                        pe.wait_ge(rope_done[1 - n % 2], i * PER_ROPE + (n - 1) // 2 + 1 + 1)
                    pe.wait_ge(exp_done[s], i * PER_SLOT + h // 2 + 1)
                    for tt in range(TT):
                        out = score[s][:, tt, :]
                        nc.tensor.matmul(out, consts.ident_bf[:], consts.mask_bf[:, min(tt, 1), :],
                                         start=True, stop=False)
                        lo = P if tt == 0 else 0
                        mm = nc.tensor.matmul(out[:, lo:], q_t[:, r, tt * P:(tt + 1) * P],
                                              k_t[:, tt * P - P + lo:(tt + 1) * P],
                                              start=False, stop=True)
                    mm.then_inc(score_full[s], 1)

            def turn_probs(i, g, tt, prev):
                b, turn = ring.at(("turn", g, tt, prev), i)
                pe.wait_ge(ring.free[b], turn)
                lo = 0 if prev else P
                for r in range(REPS):
                    mm = nc.tensor.transpose(banks[b][:, r * P:(r + 1) * P],
                                             prob[:, r, tt, lo:lo + P], consts.ident[:])
                mm.then_inc(ring.full[b], 1)

            def weigh(i, g, tt):
                ring.wait_free(pe, i, ("pv", g, tt),
                               consumed=[("turn", g, tt, prev) for prev in range(min(tt, 1) + 1)])
                b, _ = ring.at(("pv", g, tt), i)
                for prev in range(min(tt, 1) + 1):
                    mm = nc.tensor.matmul(banks[b][:], v[:, tt - prev, g * HD:(g + 1) * HD],
                                          prob_t[:, tt % 2, prev, :],
                                          start=(prev == 0), stop=(prev == min(tt, 1)))
                mm.then_inc(ring.full[b], 1)

            def values(ring, i):
                for tt in range(TT):
                    b, turn = ring.at(("v", tt), i)
                    pe.wait_ge(ring.free[b], turn)
                    for k in range(KD):
                        mm = nc.tensor.matmul(banks[b][:], xn_t[:, k, tt * P:(tt + 1) * P], wv[:, k, :],
                                              start=(k == 0), stop=(k == KD - 1))
                    mm.then_inc(ring.full[b], 1)

            def one_pass(i, more):
                for g in range(KV):
                    if g == KV - 1 and more:
                        norm_tensor(nc, pe, norm, consts.ident, ring, banks, i + 1, in_pass=i)
                    scores(i, g)
                    if g + 1 < KV:
                        project(ring, i, g + 1)
                    elif more:
                        ring.wait_free(pe, i, consumed=xn_steps)
                        project(ring, i, 0)
                    pe.wait_ge(prob_ready, i * HEADS + (g + 1) * REPS)
                    turn_probs(i, g, 0, 0)
                    turn_probs(i, g, 1, 0)
                    turn_probs(i, g, 1, 1)
                    for tt in range(TT):
                        weigh(i, g, tt)
                        if tt + 2 < TT:
                            turn_probs(i, g, tt + 2, 0)
                            turn_probs(i, g, tt + 2, 1)
                    pe.wait_ge(w_in["wo"], 16)
                    for tt in range(TT):
                        ring.wait_free(pe, i, ("wo", g, tt), consumed=[("pv", g, tt)])
                        b, _ = ring.at(("wo", g, tt), i)
                        for r in range(REPS):
                            mm = nc.tensor.matmul(banks[b][:], out_t[:, tt, r * P:(r + 1) * P],
                                                  wo[:, g * REPS + r, :],
                                                  start=(r == 0), stop=(r == REPS - 1))
                        mm.then_inc(ring.full[b], 1)
                if more:
                    values(ring, i)

            norm_tensor(nc, pe, norm, consts.ident, first, banks, 0)
            first.wait_free(pe, 0, consumed=xn_steps)
            pe.wait_ge(w_in["wk"], 16)
            pe.wait_ge(w_in["wq"], 16)
            project(first, 0, 0)
            pe.wait_ge(w_in["wv"], 16)
            values(first, 0)
            first.wait_free(pe, 0, consumed=proj(0) + v_steps)
            passes(pe, one_pass)

        @block.scalar
        def _(act):
            def take(step, i, out, ring=ring):
                b, turn = ring.at(step, i)
                act.wait_ge(ring.full[b], turn)
                nc.scalar.copy(out, banks[b][:]).then_inc(ring.free[b], 1)

            def exponentials(i, g):
                for r in range(REPS):
                    h = g * REPS + r
                    act.wait_ge(neg_ready, i * HEADS + h + 1)
                    for tt in range(TT):
                        e = nc.scalar.activation(prob[:, r, tt, :], score[h % 2][:, tt, :], ACT.Exp,
                                                 bias=neg_m[:, h, tt:tt + 1], scale=scale,
                                                 accum_out=sums[:, h, tt:tt + 1])
                    e.then_inc(exp_done[h % 2], 1)

            def features(ring, i):
                for k in (1, 3):
                    take(("xn", k), i, xn_t[:, k, :], ring)

            def values(ring, i):
                for tt in (1, 3):
                    take(("v", tt), i, v[:, tt, :], ring)

            def one_pass(i, more):
                for g in range(KV):
                    if g == KV - 1 and more:
                        features(ring, i)
                    exponentials(i, g)
                    take(("turn", g, 0, 0), i, prob_t[:, 0, 0, :])
                    take(("turn", g, 1, 0), i, prob_t[:, 1, 0, :])
                    for tt in range(TT):
                        take(("pv", g, tt), i, out_t[:, tt, :])
                        if tt + 2 < TT:
                            take(("turn", g, tt + 2, 0), i, prob_t[:, tt % 2, 0, :])
                if more:
                    values(ring, i)

            features(first, 0)
            values(first, 0)
            passes(act, one_pass)

        @block.vector
        def _(dve):
            def take(step, i, out, ring=ring):
                b, turn = ring.at(step, i)
                dve.wait_ge(ring.full[b], turn)
                nc.vector.tensor_copy(out, banks[b][:]).then_inc(ring.free[b], 1)

            def rope(ring, in_pass, i, g):
                for j, step in enumerate(proj(g)):
                    n = g * (1 + REPS) + j
                    s = n % 2
                    b, turn = ring.at(step, in_pass)
                    dve.wait_ge(ring.full[b], turn)
                    dve.wait_ge(rope_done[s], i * PER_ROPE + n // 2 + 1)
                    h = HD // 2
                    nc.vector.tensor_tensor(rope_a[:, s, :], banks[b][:], cos2[:], ALU.mult)
                    nc.vector.tensor_tensor(rope_b[0:h, s, :], banks[b][h:P, :], sin2[0:h, :], ALU.mult)
                    nc.vector.tensor_tensor(rope_b[h:P, s, :], banks[b][0:h, :], sin2[h:P, :], ALU.mult) \
                        .then_inc(ring.free[b], 1)

            def maxima(i, h):
                dve.wait_ge(score_full[h % 2], i * PER_SLOT + h // 2 + 1)
                nc.vector.tensor_reduce(mx[:, h, :], score[h % 2][:], AX_X, ALU.max).then_inc(max_done, 1)
                dve.wait_ge(max_done, i * HEADS + h + 1)
                nc.vector.tensor_scalar(neg_m[:, h, :], mx[:, h, :], -scale, None, ALU.mult) \
                    .then_inc(neg_ready, 1)

            def inverse(i, h):
                dve.wait_ge(exp_done[h % 2], i * PER_SLOT + h // 2 + 1 + 1)
                nc.vector.reciprocal(rsum[:, h, :], sums[:, h, :]).then_inc(rsum_ready, 1)

            def features(ring, i):
                for k in (0, 2):
                    take(("xn", k), i, xn_t[:, k, :], ring)

            def values(ring, i):
                for tt in (0, 2):
                    take(("v", tt), i, v[:, tt, :], ring)

            def one_pass(i, more):
                for g in range(KV):
                    if g == KV - 1 and more:
                        features(ring, i)
                    for r in range(REPS):
                        maxima(i, g * REPS + r)
                        if r:
                            inverse(i, g * REPS + r - 1)
                    inverse(i, g * REPS + REPS - 1)
                    if g == KV - 2 and more:
                        norm_vector(nc, dve, norm, x, i + 1)
                    lookup.vector(i, g * TT)
                    if g + 1 < KV:
                        rope(ring, i, i, g + 1)
                    elif more:
                        rope(ring, i, i + 1, 0)
                    for tt in range(1, TT):
                        take(("turn", g, tt, 1), i, prob_t[:, tt % 2, 1, :])
                    for tt in range(TT):
                        if tt < TT - 1:
                            lookup.vector(i, g * TT + tt + 1)
                        b, turn = ring.at(("wo", g, tt), i)
                        dve.wait_ge(ring.full[b], turn)
                        nc.vector.tensor_tensor(x[:, i, tt, :], banks[b][:], x[:, i, tt, :], ALU.add) \
                            .then_inc(ring.free[b], 1)
                if more:
                    values(ring, i)

            norm_vector(nc, dve, norm, x, 0)
            features(first, 0)
            dve.wait_ge(w_in["rope"], 32)
            rope(first, 0, 0, 0)
            values(first, 0)
            lookup.vector_setup(dve)
            passes(dve, one_pass)

        @block.gpsimd
        def _(pool):
            def rope_sums(ring, in_pass, i, g):
                for j, step in enumerate(proj(g)):
                    n = g * (1 + REPS) + j
                    s = n % 2
                    b, turn = ring.at(step, in_pass)
                    pool.wait_ge(ring.free[b], turn + 1)
                    out = k_t[:] if j == 0 else q_t[:, j - 1, :]
                    nc.gpsimd.tensor_tensor(out, rope_a[:, s, :], rope_b[:, s, :], ALU.add) \
                        .then_inc(rope_done[s], 1)

            def one_pass(i, more):
                for g in range(KV):
                    for r in range(REPS):
                        h = g * REPS + r
                        wait_apart(pool, rsum_ready, i * HEADS + h + 1, waited)
                        for tt in range(TT):
                            p = nc.gpsimd.tensor_scalar(prob[:, r, tt, :], prob[:, r, tt, :],
                                                        rsum[:, h, tt:tt + 1], 1.0, ALU.mult, ALU.mult)
                        p.then_inc(prob_ready, 1)
                    if g == KV - 2 and more:
                        norm_gpsimd(nc, pool, norm, consts.minus_half, i + 1)
                    if g + 1 < KV:
                        rope_sums(ring, i, i, g + 1)
                    elif more:
                        rope_sums(ring, i, i + 1, 0)

            norm_gpsimd(nc, pool, norm, consts.minus_half, 0)
            rope_sums(first, 0, 0, 0)
            passes(pool, one_pass)


def stage_cross_attention(core, sb, psum, dram, x, consts, fetch):
    nc = core.nc
    wq = sb("b_wq", [P, KC, QK], F32)
    wk = sb("b_wk", [P, KC, QK], F32)
    bq = sb("b_bq", [P, 1], F32)
    bk = sb("b_bk", [P, 1], F32)
    ctx_t = sb("b_ctx_t", [P, B, KC, T], F32)
    norm = Norm(core, sb, "b")
    xn_t = sb("b_xn_t", [P, KD, T], F32)
    q_t = sb("b_q_t", [P, T], F32)
    k_t = sb("b_k_t", [P, T], F32)
    att = sb("b_att", [P, TT, T], F32)
    att_t = sb("b_att_t", [P, TT, T], F32)
    mx = sb("b_mx", [P, TT], F32)
    neg_m = sb("b_neg_m", [P, TT], F32)
    sums = sb("b_sums", [P, TT], F32)
    rsum = sb("b_rsum", [P, TT], F32)

    NB = 6
    banks = [psum(f"b_bank{b}", [P, 512], F32) for b in range(NB)]
    order = [("q",), ("k",)] + [("energy", m) for m in range(TT)] + [("xn", k) for k in range(KD)]
    order += [("turn", n) for n in range(TT)] + [("out", tt) for tt in range(TT)]
    ring = Ring(core.sems("b_full", NB), core.sems("b_free", NB), order)
    w_in = core.sem("b_in_w")
    max_done = core.sem("b_max_done")
    neg_ready = core.sem("b_neg_ready")
    waited = core.sem("b_waited")
    rsum_ready = core.sem("b_rsum_ready")
    att_ready = core.sem("b_att_ready")

    with nc.Block() as block:
        @block.sync
        def _(sp):
            sp.dma_start(wq[:], dram["x_wq_t"].rearrange("(k p) o -> p k o", p=P)).then_inc(w_in, 16)
            sp.dma_start(wk[:], dram["x_wk_t"].rearrange("(k p) o -> p k o", p=P)).then_inc(w_in, 16)
            sp.dma_start(bq[:], dram["x_bq"].rearrange("(p o) -> p o", o=1)).then_inc(w_in, 16)
            sp.dma_start(bk[:], dram["x_bk"].rearrange("(p o) -> p o", o=1)).then_inc(w_in, 16)
            sp.dma_start(ctx_t[:], dram["ctx_t"].rearrange("b (k p) t -> p b k t", p=P)).then_inc(w_in, 16)
            weights, from_dram, weights_in = fetch
            sp.dma_start(weights[:].bitcast(I32), from_dram).then_inc(weights_in, 16)

        @block.tensor
        def _(pe):
            start_at_one(pe, *ring.free)
            pe.wait_ge(w_in, 16 * 5)
            with pe.Fori(0, B) as i:
                for step, w in ((("q",), wq), (("k",), wk)):
                    b, turn = ring.at(step, i)
                    pe.wait_ge(ring.free[b], turn)
                    for k in range(KC):
                        mm = nc.tensor.matmul(banks[b][:], w[:, k, :], ctx_t[:, i, k, :],
                                              start=(k == 0), stop=(k == KC - 1))
                    mm.then_inc(ring.full[b], 1)
                ring.wait_free(pe, i, consumed=[("q",), ("k",)])
                for m in range(TT):
                    b, turn = ring.at(("energy", m), i)
                    pe.wait_ge(ring.free[b], turn)
                    nc.tensor.matmul(banks[b][:], q_t[:, m * P:(m + 1) * P], k_t[:],
                                     start=True, stop=True).then_inc(ring.full[b], 1)
                norm_tensor(nc, pe, norm, consts.ident, ring, banks, i)
                pe.wait_ge(att_ready, (i + 1) * TT)
                for n in range(TT):
                    b, turn = ring.at(("turn", n), i)
                    pe.wait_ge(ring.free[b], turn)
                    for m in range(TT):
                        mm = nc.tensor.transpose(banks[b][:, m * P:(m + 1) * P],
                                                 att[:, m, n * P:(n + 1) * P], consts.ident[:])
                    mm.then_inc(ring.full[b], 1)
                for tt in range(TT):
                    ring.wait_free(pe, i, ("out", tt), consumed=[("xn", k) for k in range(KD)]
                                   + [("turn", n) for n in range(TT)] if tt == 0 else ())
                    b, _ = ring.at(("out", tt), i)
                    for n in range(TT):
                        mm = nc.tensor.matmul(banks[b][:], xn_t[:, n, tt * P:(tt + 1) * P], att_t[:, n, :],
                                              start=(n == 0), stop=(n == TT - 1))
                    mm.then_inc(ring.full[b], 1)


        @block.scalar
        def _(act):
            act.wait_ge(w_in, 16 * 5)
            with act.Fori(0, B) as i:
                for step, bias, out in ((("q",), bq, q_t), (("k",), bk, k_t)):
                    b, turn = ring.at(step, i)
                    act.wait_ge(ring.full[b], turn)
                    nc.scalar.activation(out[:], banks[b][:], ACT.Identity, bias=bias[:]) \
                        .then_inc(ring.free[b], 1)
                for m in range(TT):
                    act.wait_ge(neg_ready, i * TT + m + 1)
                    b, turn = ring.at(("energy", m), i)
                    nc.scalar.activation(att[:, m, :], banks[b][:], ACT.Exp, bias=neg_m[:, m:m + 1],
                                         accum_out=sums[:, m:m + 1]).then_inc(ring.free[b], 1)
                for step, out in [(("xn", k), xn_t[:, k, :]) for k in (1, 3)] + \
                        [(("turn", n), att_t[:, n, :]) for n in (0, 1, 2, 3)]:
                    b, turn = ring.at(step, i)
                    act.wait_ge(ring.full[b], turn)
                    nc.scalar.copy(out, banks[b][:]).then_inc(ring.free[b], 1)

        @block.vector
        def _(dve):
            with dve.Fori(0, B) as i:
                norm_vector(nc, dve, norm, x, i)
                for m in range(TT):
                    b, turn = ring.at(("energy", m), i)
                    dve.wait_ge(ring.full[b], turn)
                    nc.vector.tensor_reduce(mx[:, m:m + 1], banks[b][:], AX_X, ALU.max).then_inc(max_done, 1)
                    dve.wait_ge(max_done, i * TT + m + 1)
                    nc.vector.tensor_scalar(neg_m[:, m:m + 1], mx[:, m:m + 1], -1.0, None, ALU.mult) \
                        .then_inc(neg_ready, 1)
                for m in range(TT):
                    b, turn = ring.at(("energy", m), i)
                    dve.wait_ge(ring.free[b], turn + 1)
                    nc.vector.reciprocal(rsum[:, m:m + 1], sums[:, m:m + 1]).then_inc(rsum_ready, 1)
                for k in (0, 2):
                    b, turn = ring.at(("xn", k), i)
                    dve.wait_ge(ring.full[b], turn)
                    nc.vector.tensor_copy(xn_t[:, k, :], banks[b][:]).then_inc(ring.free[b], 1)
                for tt in range(TT):
                    b, turn = ring.at(("out", tt), i)
                    dve.wait_ge(ring.full[b], turn)
                    nc.vector.tensor_tensor(x[:, i, tt, :], banks[b][:], x[:, i, tt, :], ALU.add) \
                        .then_inc(ring.free[b], 1)

        @block.gpsimd
        def _(pool):
            with pool.Fori(0, B) as i:
                norm_gpsimd(nc, pool, norm, consts.minus_half, i)
                for m in range(TT):
                    wait_apart(pool, rsum_ready, i * TT + m + 1, waited)
                    nc.gpsimd.tensor_scalar(att[:, m, :], att[:, m, :], rsum[:, m:m + 1], 1.0,
                                            ALU.mult, ALU.mult).then_inc(att_ready, 1)


class Scan:
    QUADS = DS // NQ
    PER_QUAD = ET * NQ // NS
    CHUNKS = QUADS * PER_QUAD
    POSITIONS = CHUNKS + 6
    SLOTS = 4

    def __init__(self, core, sb, psum, dram, scratch, consts):
        self.nc, self.dram, self.scratch, self.consts = core.nc, dram, scratch, consts
        self.a = sb("s_a", [P, ET, DS], F32)
        self.delta = sb("s_delta", [P, ET, T], F32)
        self.delta_u = sb("s_delta_u", [P, ET, T], F32)
        self.y = sb("s_y", [P, ET, T], F32)
        self.bc = sb("s_bc", [P, 2, 2, NQ, T], F32)
        self.decay = sb("s_decay", [P, 2, NS, T], F32)
        self.state = sb("s_state", [P, self.SLOTS, NS, T], F32)
        self.pair = sb("s_pair", [P, self.SLOTS, T], F32)
        self.banks = [psum(f"s_bank{b}", [P, 512], F32) for b in range(2)]
        self.a_in = core.sem("s_a_in")
        self.a_step = core.sem("s_a_step")
        self.seq_in = core.sem("s_seq_in")
        self.y_in = core.sem("s_y_in")
        self.bc_in = core.sems("s_bc_in", 2)
        self.decay_ready = core.sems("s_decay", self.SLOTS)
        self.input_ready = core.sems("s_input", self.SLOTS)
        self.scanned = core.sems("s_scanned", self.SLOTS)
        self.weighed = core.sems("s_weighed", self.SLOTS)
        self.paired = core.sems("s_paired", self.SLOTS)
        self.summed = core.sems("s_summed", self.SLOTS)
        self.added = core.sems("s_added", 2)
        self.stored = core.sem("s_stored")

    def wait(self, eng, sems, i, c):
        eng.wait_ge(sems[c % self.SLOTS], i * (self.CHUNKS // self.SLOTS) + c // self.SLOTS + 2)

    def wait_added(self, eng, i, c):
        n = c // 2
        eng.wait_ge(self.added[n % 2], i * (self.CHUNKS // 4) + n // 2 + 2)

    def wait_bc(self, eng, i, q):
        eng.wait_ge(self.bc_in[q % 2], i * (self.QUADS // 2 * 32) + (q // 2 + 1) * 32)

    def place(self, c):
        return c // self.PER_QUAD, c % self.PER_QUAD * NS // NQ, c * NS % NQ

    def load_a(self, sp):
        sp.dma_start(self.a[:], self.dram["m_a_log"].rearrange("(k p) n -> p k n", p=P)).then_inc(self.a_in, 16)

    def sync(self, sp, i):
        scratch = self.scratch
        for c in range(-self.SLOTS, 0):
            self.wait(sp, self.weighed, i, c)
        sp.dma_start(self.delta[:], scratch["delta"][i]).then_inc(self.seq_in, 16)
        sp.dma_start(self.delta_u[:], scratch["delta_u"][i]).then_inc(self.seq_in, 16)
        for q in range(self.QUADS):
            if q == 2:
                sp.wait_ge(self.stored, i * 16 + 1)
                sp.dma_start(self.y[:], scratch["y"][i]).then_inc(self.y_in, 16)
            for c in range(self.SLOTS if q else 0):
                self.wait(sp, self.weighed, i, (q - 1) * self.PER_QUAD - 1 - c)
            for n in range(2):
                rows = scratch["bc"][i, n * DS + q * NQ:n * DS + (q + 1) * NQ, :]
                sp.dma_start(self.bc[:, q % 2, n], rows.rearrange("(o n) t -> o n t", o=1)
                             .broadcast_to([P, NQ, T])).then_inc(self.bc_in[q % 2], 16)
        for c in (-1, -3):
            self.wait_added(sp, i + 1, c)
        sp.dma_start(scratch["y"][i], self.y[:]).then_inc(self.stored, 16)

    def sync_end(self, sp):
        sp.wait_ge(self.stored, B * 16 + 1)

    def tensor_setup(self, pe):
        start_at_one(pe, self.stored, *self.scanned, *self.weighed, *self.paired, *self.summed, *self.added)

    def tensor(self, i, p):
        pe, nc, c = self.nc.tensor, self.nc, p - 4
        if not 0 <= c < self.CHUNKS:
            return
        self.wait(pe, self.paired, i, c)
        if c % 2 == 0:
            self.wait_added(pe, i, c - 4)
        nc.tensor.matmul(self.banks[c // 2 % 2][:], self.consts.ident[:], self.pair[:, c % self.SLOTS, :],
                         start=(c % 2 == 0), stop=(c % 2 == 1)).then_inc(self.summed[c % self.SLOTS], 1)

    def scalar_setup(self, act):
        act.wait_ge(self.a_in, 16)
        self.nc.scalar.activation(self.a[:], self.a[:], ACT.Exp).then_inc(self.a_step, 1)
        act.wait_ge(self.a_step, 3)

    def scalar(self, i, p):
        act, c = self.nc.scalar, p
        if c >= self.CHUNKS:
            return
        if c == 0:
            act.wait_ge(self.seq_in, i * 32 + 32)
        self.wait(act, self.scanned, i, c - 2)
        q, et, n = self.place(c)
        for u in range(NS):
            st = q * NQ + n + u
            ins = self.nc.scalar.activation(self.decay[:, c % 2, u, 1:], self.delta[:, et, 1:], ACT.Exp,
                                            scale=self.a[:, et, st:st + 1])
        ins.then_inc(self.decay_ready[c % self.SLOTS], 1)

    def gpsimd(self, i, p):
        pool, s = self.nc.gpsimd, p % self.SLOTS
        if p < self.CHUNKS:
            q, et, n = self.place(p)
            if p == 0:
                pool.wait_ge(self.seq_in, i * 32 + 32)
            if p % self.PER_QUAD == 0:
                self.wait_bc(pool, i, q)
            self.wait(pool, self.paired, i, p - self.SLOTS)
            pool.tensor_tensor(self.state[:, s], self.bc[:, q % 2, 0, n:n + NS],
                               self.delta_u[:, et, :].rearrange("p (o t) -> p o t", o=1)
                               .broadcast_to([P, NS, T]), ALU.mult).then_inc(self.input_ready[s], 1)
        c = p - 2
        if 0 <= c < self.CHUNKS:
            s = c % self.SLOTS
            self.wait(pool, self.weighed, i, c)
            self.wait(pool, self.summed, i, c - self.SLOTS)
            pool.tensor_tensor(self.pair[:, s, :], self.state[:, s, 0, :], self.state[:, s, 1, :], ALU.add) \
                .then_inc(self.paired[s], 1)

    def vector_setup(self, dve):
        self.nc.vector.memset(self.decay[:, :, :, 0:1], 0.0).then_inc(self.a_step, 1)
        dve.wait_ge(self.a_step, 2)
        self.nc.vector.tensor_scalar(self.a[:], self.a[:], -1.0, None, ALU.mult).then_inc(self.a_step, 1)

    def vector(self, i, p):
        dve = self.nc.vector
        if p < self.CHUNKS:
            s = p % self.SLOTS
            dve.wait_ge(self.decay_ready[s], i * (self.CHUNKS // self.SLOTS) + p // self.SLOTS + 1)
            dve.wait_ge(self.input_ready[s], i * (self.CHUNKS // self.SLOTS) + p // self.SLOTS + 1)
            flat = self.state[:, s].rearrange("p n t -> p (n t)")
            dve.tensor_tensor_scan(flat, self.decay[:, p % 2].rearrange("p n t -> p (n t)"), flat,
                                   0.0, ALU.mult, ALU.add).then_inc(self.scanned[s], 1)
        c = p - 1
        if 0 <= c < self.CHUNKS:
            s = c % self.SLOTS
            q, et, n = self.place(c)
            self.wait(dve, self.scanned, i, c)
            if c % self.PER_QUAD == 0:
                self.wait_bc(dve, i, q)
            dve.tensor_tensor(self.state[:, s], self.state[:, s], self.bc[:, q % 2, 1, n:n + NS], ALU.mult) \
                .then_inc(self.weighed[s], 1)
        c = p - 6
        if c >= 0 and c % 2 == 1:
            q, et, _ = self.place(c)
            if c == 1:
                dve.wait_ge(self.y_in, i * 16 + 16)
            self.wait(dve, self.summed, i, c)
            if q > 0:
                self.wait_added(dve, i, c - self.PER_QUAD)
            dve.tensor_tensor(self.y[:, et, :], self.banks[c // 2 % 2][:], self.y[:, et, :], ALU.add) \
                .then_inc(self.added[c // 2 % 2], 1)


def stage_ffn(core, sb, psum, dram, x, consts, weights, weights_in, scratch):
    nc = core.nc
    norm = Norm(core, sb, "c")
    xn_t = sb("c_xn_t", [P, KD, T], F32)
    h_t = sb("c_h_t", [P, 2, T], F32)
    scan = Scan(core, sb, psum, dram, scratch, consts)
    NB = 2
    banks = [psum(f"c_bank{b}", [P, 512], F32) for b in range(NB)]
    out = [psum(f"c_out{tt}", [P, 512], F32) for tt in range(TT)]
    order = [("xn", k) for k in range(KD)]
    for o in range(OT):
        order += [("gate", o), ("up", o)]
    ring = Ring(core.sems("c_full", NB), core.sems("c_free", NB), order)
    h_used = core.sem("c_h_used")
    out_full = core.sem("c_out_full")
    out_free = core.sem("c_out_free")
    width = [min(P, INTER - o * P) for o in range(OT)]
    NORM_AT = 5
    share = lambda o: min(max(o - 1, 0), OT - 2) * scan.POSITIONS // (OT - 2)
    positions = [list(range(share(o), share(o + 1))) for o in range(OT)]

    with nc.Block() as block:
        @block.sync
        def _(sp):
            scan.load_a(sp)
            with sp.Fori(0, B) as i:
                scan.sync(sp, i)
            scan.sync_end(sp)

        @block.tensor
        def _(pe):
            start_at_one(pe, out_free, h_used, *ring.free)
            scan.tensor_setup(pe)

            def down(i, o):
                b, turn = ring.at(("up", o), i)
                pe.wait_ge(ring.free[b], turn + 1)
                if o == 0:
                    pe.wait_ge(out_free, i * TT + 1)
                for tt in range(TT):
                    mm = nc.tensor.matmul(out[tt][:], h_t[0:width[o], o % 2, tt * P:(tt + 1) * P],
                                          weights[0:width[o], W_DOWN + o * D:W_DOWN + (o + 1) * D],
                                          start=(o == 0), stop=(o == OT - 1))
                mm.then_inc(h_used if o < OT - 1 else out_full, 1)

            def one_pass(i, more):
                ring.wait_free(pe, i, consumed=[("xn", k) for k in range(KD)])
                for o in range(OT):
                    at = positions[o]
                    for n, (kind, base) in enumerate((("gate", 0), ("up", W_UP))):
                        b, turn = ring.at((kind, o), i)
                        pe.wait_ge(ring.free[b], turn)
                        for k in range(KD):
                            lo = base + k * INTER + o * P
                            mm = nc.tensor.matmul(banks[b][0:width[o], :], weights[:, lo:lo + width[o]],
                                                  xn_t[:, k, :], start=(k == 0), stop=(k == KD - 1))
                        mm.then_inc(ring.full[b], 1)
                        if at:
                            scan.tensor(i, at[n])
                    if o == OT - 1 and more:
                        norm_tensor(nc, pe, norm, consts.ident, ring, banks, i + 1)
                    if o:
                        down(i, o - 1)
                    for p in at[2:]:
                        scan.tensor(i, p)
                down(i, OT - 1)

            norm_tensor(nc, pe, norm, consts.ident, ring, banks, 0)
            pe.wait_ge(weights_in, 16)
            passes(pe, one_pass)

        @block.scalar
        def _(act):
            def evacuate(i):
                for k in (1, 3):
                    b, turn = ring.at(("xn", k), i)
                    act.wait_ge(ring.full[b], turn)
                    nc.scalar.copy(xn_t[:, k, :], banks[b][:]).then_inc(ring.free[b], 1)

            def one_pass(i, more):
                for o in range(OT):
                    if o == 1:
                        act.wait_ge(h_used, i * (OT - 1) + 1)
                    elif o == 0:
                        act.wait_ge(out_free, i * TT + 1)
                    else:
                        act.wait_ge(h_used, i * (OT - 1) + o)
                    for p in positions[o][:2]:
                        scan.scalar(i, p)
                    b, turn = ring.at(("gate", o), i)
                    act.wait_ge(ring.full[b], turn)
                    nc.scalar.activation(h_t[0:width[o], o % 2, :], banks[b][0:width[o], :], ACT.Silu) \
                        .then_inc(ring.free[b], 1)
                    for p in positions[o][2:]:
                        scan.scalar(i, p)
                if more:
                    evacuate(i + 1)

            scan.scalar_setup(act)
            evacuate(0)
            passes(act, one_pass)

        @block.vector
        def _(dve):
            def evacuate(i):
                for k in (0, 2):
                    b, turn = ring.at(("xn", k), i)
                    dve.wait_ge(ring.full[b], turn)
                    nc.vector.tensor_copy(xn_t[:, k, :], banks[b][:]).then_inc(ring.free[b], 1)

            def one_pass(i, more):
                for o in range(OT):
                    for p in positions[o][:2]:
                        scan.vector(i, p)
                    b, turn = ring.at(("gate", o), i)
                    dve.wait_ge(ring.free[b], turn + 1)
                    b, turn = ring.at(("up", o), i)
                    dve.wait_ge(ring.full[b], turn)
                    nc.vector.tensor_tensor(h_t[0:width[o], o % 2, :], banks[b][0:width[o], :],
                                            h_t[0:width[o], o % 2, :], ALU.mult).then_inc(ring.free[b], 1)
                    for p in positions[o][2:]:
                        scan.vector(i, p)
                    if o == NORM_AT and more:
                        norm_vector(nc, dve, norm, x, i + 1)
                if more:
                    evacuate(i + 1)
                dve.wait_ge(out_full, i + 1)
                for tt in range(TT):
                    nc.vector.tensor_tensor(x[:, i, tt, :], out[tt][:], x[:, i, tt, :], ALU.add) \
                        .then_inc(out_free, 1)

            norm_vector(nc, dve, norm, x, 0)
            scan.vector_setup(dve)
            evacuate(0)
            passes(dve, one_pass)

        @block.gpsimd
        def _(pool):
            def one_pass(i, more):
                for o in range(OT):
                    for p in positions[o]:
                        scan.gpsimd(i, p)
                    if o == NORM_AT and more:
                        norm_gpsimd(nc, pool, norm, consts.minus_half, i + 1)

            norm_gpsimd(nc, pool, norm, consts.minus_half, 0)
            passes(pool, one_pass)


def stage_diff_attention(core, sb, psum, dram, x, consts):
    nc = core.nc
    E2 = 2 * DHD
    HG = P // E2
    GROUPS = DH // HG
    VD = D // DH
    w = sb("d_w", [P, KD, 3 * D], F32)
    wp = sb("d_wp", [P, KD, D], F32)
    lam_v = sb("d_lam_v", [P, 4, D], F32)
    lam_s = sb("d_lam_s", [P, 6], F32)
    rowsel = sb("d_rowsel", [P, 2], F32)
    coef = sb("d_coef", [P, 1], F32)
    norm = Norm(core, sb, "d")
    xn_t = sb("d_xn_t", [P, KD, T], F32)
    hi = sb("d_hi", [P, 2, T], F32R)
    lo = sb("d_lo", [P, 2, T], F32R)
    qs = sb("d_qs", [P, DH, T], F32R)
    ks = sb("d_ks", [P, DH, T], F32R)
    v = sb("d_v", [P, TT, D], F32)
    mx = sb("d_mx", [P, GROUPS, HG, TT], F32)
    neg_t = sb("d_neg_t", [HG * TT, P], F32R)
    prob_t = sb("d_prob_t", [P, 2, HG, T], F32)
    rsum = sb("d_rsum", [P, T], F32)
    out_t = sb("d_out_t", [P, GROUPS, T], F32)

    banks = [psum(f"d_bank{b}", [P, 512], F32) for b in range(2)]
    score = [psum(f"d_score{s}", [P, 2, T], F32) for s in range(2)]
    acc = psum("d_acc", [P, T], F32)
    acc_sum = psum("d_acc_sum", [P, T], F32)
    order = [("xn", k) for k in range(KD)]
    for g in range(GROUPS):
        order += [("q", g), ("k", g)]
    order += [("v", tt) for tt in range(TT)]
    for g in range(GROUPS):
        order += [("row", g, j, tt) for j in range(HG) for tt in range(TT)] + [("neg", g)]
    order += [("out", tt) for tt in range(TT)]
    ring = Ring(core.sems("d_full", 2), core.sems("d_free", 2), order)
    w_in = core.sem("d_in_w")
    lam_step = core.sem("d_lam_step")
    hi_done = core.sem("d_hi_done")
    stacked = core.sems("d_stacked", 2)
    max_in = core.sem("d_max_in")
    prob_used = core.sem("d_prob_used")
    score_full = core.sems("d_score_full", 2)
    exp_done = core.sems("d_exp_done", 2)
    acc_full = core.sem("d_acc_full")
    rsum_done = core.sem("d_rsum_done")
    acc_free = core.sem("d_acc_free")
    COPIES = 3 * HG * 16
    FILLS = GROUPS * TT

    with nc.Block() as block:
        @block.sync
        def _(sp):
            sp.dma_start(w[:], dram["d_w"].rearrange("(k p) o -> p k o", p=P)).then_inc(w_in, 16)
            sp.dma_start(wp[:], dram["d_wp"].rearrange("(k p) o -> p k o", p=P)).then_inc(w_in, 16)
            for n, name in enumerate(("lq1", "lk1", "lq2", "lk2")):
                sp.dma_start(lam_v[:, n, :], dram[name].rearrange("(o l) -> o l", o=1).broadcast_to([P, D])) \
                    .then_inc(w_in, 16)
            sp.dma_start(rowsel[:], dram["rowsel"]).then_inc(w_in, 16)
            with sp.Fori(0, B) as i:
                for g in range(GROUPS):
                    for n, (stack, parts) in enumerate(((qs, (hi, lo, hi)), (ks, (hi, hi, lo)))):
                        b, turn = ring.at(("qk"[n], g), i)
                        sp.wait_ge(ring.free[b], turn + 1)
                        for block_, part in enumerate(parts):
                            for j in range(HG):
                                sp.dma_start(stack[block_ * E2:(block_ + 1) * E2, g * HG + j, :].bitcast(F32),
                                             part[j * E2:(j + 1) * E2, n, :].bitcast(F32)) \
                                    .then_inc(stacked[n], 16)
                for g in range(GROUPS):
                    b, turn = ring.at(("neg", g), i)
                    sp.wait_ge(ring.free[b], turn + 1)
                    sp.dma_start(qs[3 * E2:3 * E2 + 1, g * HG:(g + 1) * HG, :]
                                 .rearrange("o j (t c) -> o (j t) c", c=P).bitcast(F32),
                                 neg_t[:].bitcast(F32)).then_inc(max_in, 16)

        @block.tensor
        def _(pe):
            start_at_one(pe, *exp_done, acc_free, *stacked, prob_used, acc_full, max_in, *ring.free)
            def rows(i, g, j):
                for tt in range(TT):
                    b, turn = ring.at(("row", g, j, tt), i)
                    pe.wait_ge(ring.free[b], turn)
                    nc.tensor.matmul(banks[b][:], qs[0:3 * E2, g * HG + j, tt * P:(tt + 1) * P],
                                     ks[0:3 * E2, g * HG + j, :], start=True, stop=True) \
                        .then_inc(ring.full[b], 1)

            def negate(i, g):
                ring.wait_free(pe, i, ("neg", g), consumed=[("row", g, HG - 1, tt) for tt in range(TT)])
                b, _ = ring.at(("neg", g), i)
                nc.tensor.transpose(banks[b][0:HG * TT, 0:P], mx[:, g, :, :].rearrange("p j t -> p (j t)"),
                                    consts.ident[:]).then_inc(ring.full[b], 1)

            def columns(i, g, st):
                for s in range(2):
                    pe.wait_ge(exp_done[s], i * FILLS + g * TT + st + 1)
                    for u in range(2):
                        h = g * HG + 2 * s + u
                        mm = nc.tensor.matmul(score[s][:, u, :], ks[0:3 * E2 + 1, h, st * P:(st + 1) * P],
                                              qs[0:3 * E2 + 1, h, :], start=True, stop=True)
                    mm.then_inc(score_full[s], 1)

            def weigh(i, g, st):
                if st == 0:
                    pe.wait_ge(acc_free, i * GROUPS + g + 1)
                for s in range(2):
                    pe.wait_ge(exp_done[s], i * FILLS + g * TT + st + 1 + 1)
                for j in range(HG):
                    h = g * HG + j
                    nc.tensor.matmul(acc[j * VD:(j + 1) * VD, :], v[:, st, h * VD:(h + 1) * VD],
                                     prob_t[:, st % 2, j, :], start=(st == 0), stop=(st == TT - 1))
                for j in range(HG):
                    mm = nc.tensor.matmul(acc_sum[j * VD:(j + 1) * VD, :], consts.ones[:, 0:VD],
                                          prob_t[:, st % 2, j, :], start=(st == 0), stop=(st == TT - 1))
                mm.then_inc(prob_used if st < TT - 1 else acc_full, 1)

            pe.wait_ge(w_in, 16 * 7)
            with pe.Fori(0, B) as i:
                norm_tensor(nc, pe, norm, consts.ident, ring, banks, i)
                ring.wait_free(pe, i, consumed=[("xn", k) for k in range(KD)])
                for g in range(GROUPS):
                    for n, kind in enumerate("qk"):
                        b, turn = ring.at((kind, g), i)
                        pe.wait_ge(ring.free[b], turn)
                        for k in range(KD):
                            mm = nc.tensor.matmul(banks[b][:], w[:, k, n * D + g * P:n * D + (g + 1) * P],
                                                  xn_t[:, k, :], start=(k == 0), stop=(k == KD - 1))
                        mm.then_inc(ring.full[b], 1)
                for tt in range(TT):
                    b, turn = ring.at(("v", tt), i)
                    pe.wait_ge(ring.free[b], turn)
                    for k in range(KD):
                        mm = nc.tensor.matmul(banks[b][:], xn_t[:, k, tt * P:(tt + 1) * P],
                                              w[:, k, 2 * D:3 * D], start=(k == 0), stop=(k == KD - 1))
                    mm.then_inc(ring.full[b], 1)
                for n in range(2):
                    pe.wait_ge(stacked[n], (i + 1) * (GROUPS * COPIES) + 1)
                for j in range(HG):
                    rows(i, 0, j)
                negate(i, 0)
                for g in range(GROUPS):
                    pe.wait_ge(max_in, (i * GROUPS + g) * 16 + 16 + 1)
                    columns(i, g, 0)
                    for st in range(TT):
                        if st + 1 < TT:
                            columns(i, g, st + 1)
                        if g + 1 < GROUPS:
                            rows(i, g + 1, st)
                            if st == HG - 1:
                                negate(i, g + 1)
                        weigh(i, g, st)
                pe.wait_ge(acc_free, (i + 1) * GROUPS + 1)
                for tt in range(TT):
                    b, turn = ring.at(("out", tt), i)
                    pe.wait_ge(ring.free[b], turn)
                    for g in range(GROUPS):
                        mm = nc.tensor.matmul(banks[b][:], out_t[:, g, tt * P:(tt + 1) * P], wp[:, g, :],
                                              start=(g == 0), stop=(g == GROUPS - 1))
                    mm.then_inc(ring.full[b], 1)

        @block.scalar
        def _(act):
            for n in range(2):
                act.wait_ge(lam_step, 1)
                nc.scalar.activation(lam_s[:, 2 + n:3 + n], lam_s[:, n:n + 1], ACT.Exp).then_inc(lam_step, 1)
            act.wait_ge(lam_step, 6)
            with act.Fori(0, B) as i:
                for k in (1, 3):
                    b, turn = ring.at(("xn", k), i)
                    act.wait_ge(ring.full[b], turn)
                    nc.scalar.copy(xn_t[:, k, :], banks[b][:]).then_inc(ring.free[b], 1)
                for g in range(GROUPS):
                    for n, kind in enumerate("qk"):
                        act.wait_ge(stacked[n], (i * GROUPS + g) * COPIES + 1)
                        b, turn = ring.at((kind, g), i)
                        act.wait_ge(ring.full[b], turn)
                        nc.scalar.activation(hi[:, n, :], banks[b][:], ACT.Copy if n else ACT.Identity,
                                             scale=1.0 if n else coef[:]).then_inc(hi_done, 1)
                for tt in (1, 3):
                    b, turn = ring.at(("v", tt), i)
                    act.wait_ge(ring.full[b], turn)
                    nc.scalar.copy(v[:, tt, :], banks[b][:]).then_inc(ring.free[b], 1)
                for g in range(GROUPS):
                    for st in range(TT):
                        if st >= 2:
                            act.wait_ge(prob_used, (i * GROUPS + g) * (TT - 1) + st - 1 + 1)
                        elif st == 0:
                            act.wait_ge(prob_used, (i * GROUPS + g) * (TT - 1) + 1)
                        else:
                            act.wait_ge(acc_full, i * GROUPS + g + 1)
                        for s in range(2):
                            act.wait_ge(score_full[s], i * FILLS + g * TT + st + 1)
                            nc.scalar.activation(prob_t[:, st % 2, 2 * s:2 * s + 2, :], score[s][:], ACT.Exp) \
                                .then_inc(exp_done[s], 1)

        @block.vector
        def _(dve):
            nc.vector.memset(ks[3 * E2:3 * E2 + 1, :, :].bitcast(F32), 1.0)
            dve.wait_ge(w_in, 16 * 7)
            for n in range(2):
                red = nc.vector.tensor_tensor_reduce(lam_v[:, 2 * n, :], lam_v[:, 2 * n, :], lam_v[:, 2 * n + 1, :],
                                                     1.0, 0.0, ALU.mult, ALU.add, lam_s[:, n:n + 1])
            red.then_inc(lam_step, 1)
            dve.wait_ge(lam_step, 3)
            nc.vector.tensor_tensor(lam_s[:, 4:5], lam_s[:, 2:3], lam_s[:, 3:4], ALU.subtract) \
                .then_inc(lam_step, 1)
            dve.wait_ge(lam_step, 4)
            nc.vector.tensor_scalar(lam_s[:, 5:6], lam_s[:, 4:5], LAMBDA_INIT, rowsel[:, 1:2], ALU.add, ALU.mult) \
                .then_inc(lam_step, 1)
            dve.wait_ge(lam_step, 5)
            nc.vector.tensor_tensor(coef[:], rowsel[:, 0:1], lam_s[:, 5:6], ALU.subtract).then_inc(lam_step, 1)
            dve.wait_ge(lam_step, 6)
            with dve.Fori(0, B) as i:
                norm_vector(nc, dve, norm, x, i)
                for k in (0, 2):
                    b, turn = ring.at(("xn", k), i)
                    dve.wait_ge(ring.full[b], turn)
                    nc.vector.tensor_copy(xn_t[:, k, :], banks[b][:]).then_inc(ring.free[b], 1)
                for g in range(GROUPS):
                    for n, kind in enumerate("qk"):
                        dve.wait_ge(hi_done, (i * GROUPS + g) * 2 + n + 1)
                        dve.wait_ge(stacked[n], (i * GROUPS + g) * COPIES + 1)
                        b, turn = ring.at((kind, g), i)
                        if n == 0:
                            ins = nc.vector.scalar_tensor_tensor(
                                out=lo[:, n, :], in0=banks[b][:], scalar=coef[:], in1=hi[:, n, :].bitcast(F32),
                                op0=ALU.mult, op1=ALU.subtract)
                        else:
                            ins = nc.vector.tensor_tensor(lo[:, n, :], banks[b][:], hi[:, n, :].bitcast(F32),
                                                          ALU.subtract)
                        ins.then_inc(ring.free[b], 1)
                for tt in (0, 2):
                    b, turn = ring.at(("v", tt), i)
                    dve.wait_ge(ring.full[b], turn)
                    nc.vector.tensor_copy(v[:, tt, :], banks[b][:]).then_inc(ring.free[b], 1)

                def maxima(g, j):
                    for tt in range(TT):
                        b, turn = ring.at(("row", g, j, tt), i)
                        dve.wait_ge(ring.full[b], turn)
                        nc.vector.tensor_reduce(mx[:, g, j, tt:tt + 1], banks[b][:], AX_X, ALU.max) \
                            .then_inc(ring.free[b], 1)

                def negated(g):
                    b, turn = ring.at(("neg", g), i)
                    dve.wait_ge(ring.full[b], turn)
                    dve.wait_ge(max_in, (i * GROUPS + g) * 16 + 1)
                    nc.vector.tensor_scalar(neg_t[:], banks[b][0:HG * TT, 0:P], -1.0, None, ALU.mult) \
                        .then_inc(ring.free[b], 1)

                for j in range(HG):
                    maxima(0, j)
                negated(0)
                for g in range(GROUPS):
                    if g + 1 < GROUPS:
                        for j in range(HG):
                            maxima(g + 1, j)
                        negated(g + 1)
                    dve.wait_ge(acc_full, i * GROUPS + g + 1 + 1)
                    nc.vector.reciprocal(rsum[:], acc_sum[:]).then_inc(rsum_done, 1)
                    dve.wait_ge(rsum_done, i * GROUPS + g + 1)
                    nc.vector.scalar_tensor_tensor(out=out_t[:, g, :], in0=acc[:], scalar=1.0 - LAMBDA_INIT,
                                                   in1=rsum[:], op0=ALU.mult, op1=ALU.mult).then_inc(acc_free, 1)
                for tt in range(TT):
                    b, turn = ring.at(("out", tt), i)
                    dve.wait_ge(ring.full[b], turn)
                    nc.vector.tensor_tensor(x[:, i, tt, :], banks[b][:], x[:, i, tt, :], ALU.add) \
                        .then_inc(ring.free[b], 1)

        @block.gpsimd
        def _(pool):
            with pool.Fori(0, B) as i:
                norm_gpsimd(nc, pool, norm, consts.minus_half, i)


def stage_scan_inputs(core, sb, psum, dram, scratch):
    nc = core.nc
    w_in_t = sb("m_w_in", [P, KC, DI], F32)
    w_x = sb("m_w_x", [P, ET, DR + 2 * DS], F32)
    w_dt = sb("m_w_dt", [DR, DI], F32)
    cols = sb("m_cols", [P, ET, DC + 3], F32)
    ctx_t = sb("m_ctx_t", [P, B, KC, T], F32)
    padded = sb("m_padded", [P, ET, DC - 1 + T], F32)
    conv = sb("m_conv", [P, ET, T], F32)
    u = sb("m_u", [P, ET, T], F32)
    dbl = sb("m_dbl", [DR + 2 * DS, T], F32)
    dt = sb("m_dt", [P, ET, T], F32)
    e = sb("m_e", [P, ET, T], F32)
    one_e = sb("m_one_e", [P, ET, T], F32)
    log1p = sb("m_log1p", [P, ET, T], F32)
    delta = sb("m_delta", [P, ET, T], F32)
    delta_u = sb("m_delta_u", [P, ET, T], F32)
    d_u = sb("m_d_u", [P, ET, T], F32)
    banks = [psum(f"m_bank{b}", [P, 512], F32) for b in range(6)]
    ring = Ring(core.sems("m_full", 6), core.sems("m_free", 6),
                [("x", et) for et in range(ET)] + [("dbl",)] + [("dt", et) for et in range(ET)])
    w_in = core.sem("m_in_w")
    zeroed = core.sem("m_zeroed")
    waited = core.sem("m_waited")
    conv_step = core.sem("m_conv_step")
    u_ready = core.sem("m_u_ready")
    neg_abs = core.sem("m_neg_abs")
    e_ready = core.sem("m_e_ready")
    one_e_ready = core.sem("m_one_e_ready")
    log_ready = core.sem("m_log_ready")
    log_step = core.sem("m_log_step")
    delta_ready = core.sem("m_delta_ready")
    products = core.sem("m_products")
    stored = core.sem("m_stored")
    STORES = 4 * 16

    with nc.Block() as block:
        @block.sync
        def _(sp):
            sp.dma_start(w_in_t[:], dram["m_in_t"].rearrange("(k p) e -> p k e", p=P)).then_inc(w_in, 16)
            sp.dma_start(ctx_t[:], dram["ctx_t"].rearrange("b (k p) t -> p b k t", p=P)).then_inc(w_in, 16)
            sp.dma_start(w_x[:], dram["m_x_t"].rearrange("(k p) o -> p k o", p=P)).then_inc(w_in, 16)
            sp.dma_start(w_dt[:], dram["m_dt_t"]).then_inc(w_in, 16)
            sp.dma_start(cols[:], dram["m_cols"].rearrange("(k p) o -> p k o", p=P)).then_inc(w_in, 16)
            with sp.Fori(0, B) as i:
                b, turn = ring.at(("dbl",), i)
                sp.wait_ge(ring.free[b], turn + 1)
                sp.dma_start(scratch["bc"][i], dbl[DR:DR + 2 * DS, :]).then_inc(stored, 16)
                sp.wait_ge(products, (i + 1) * ET + 1)
                for name, tile in (("delta", delta), ("delta_u", delta_u), ("y", d_u)):
                    sp.dma_start(scratch[name][i], tile[:]).then_inc(stored, 16)
            sp.wait_ge(stored, B * STORES + 1)

        @block.tensor
        def _(pe):
            start_at_one(pe, conv_step, products, u_ready, stored, *ring.free)
            pe.wait_ge(w_in, 16 * 5)
            with pe.Fori(0, B) as i:
                for et in range(ET):
                    b, turn = ring.at(("x", et), i)
                    pe.wait_ge(ring.free[b], turn)
                    for k in range(KC):
                        mm = nc.tensor.matmul(banks[b][:], w_in_t[:, k, et * P:(et + 1) * P], ctx_t[:, i, k, :],
                                              start=(k == 0), stop=(k == KC - 1))
                    mm.then_inc(ring.full[b], 1)
                pe.wait_ge(u_ready, (i + 1) * ET + 1)
                b, turn = ring.at(("dbl",), i)
                pe.wait_ge(ring.free[b], turn)
                for et in range(ET):
                    mm = nc.tensor.matmul(banks[b][0:DR + 2 * DS, :], w_x[:, et, :], u[:, et, :],
                                          start=(et == 0), stop=(et == ET - 1))
                mm.then_inc(ring.full[b], 1)
                pe.wait_ge(ring.free[b], turn + 1)
                for et in range(ET):
                    b, turn = ring.at(("dt", et), i)
                    pe.wait_ge(ring.free[b], turn)
                    nc.tensor.matmul(banks[b][:], w_dt[:, et * P:(et + 1) * P], dbl[0:DR, :],
                                     start=True, stop=True).then_inc(ring.full[b], 1)

        @block.scalar
        def _(act):
            act.wait_ge(w_in, 16 * 5)
            with act.Fori(0, B) as i:
                for et in range(ET):
                    b, turn = ring.at(("x", et), i)
                    act.wait_ge(ring.full[b], turn)
                    act.wait_ge(conv_step, i * (ET * DC) + 1)
                    nc.scalar.copy(padded[:, et, DC - 1:], banks[b][:]).then_inc(ring.free[b], 1)
                act.wait_ge(products, i * ET + 1)
                for et in range(ET):
                    act.wait_ge(conv_step, i * (ET * DC) + (DC - 1) * ET + et + 1 + 1)
                    nc.scalar.activation(u[:, et, :], conv[:, et, :], ACT.Silu, bias=cols[:, et, DC:DC + 1]) \
                        .then_inc(u_ready, 1)
                for et in range(ET):
                    act.wait_ge(neg_abs, i * ET + et + 1)
                    nc.scalar.activation(e[:, et, :], e[:, et, :], ACT.Exp).then_inc(e_ready, 1)
                for et in range(ET):
                    act.wait_ge(one_e_ready, i * ET + et + 1)
                    nc.scalar.activation(log1p[:, et, :], one_e[:, et, :], ACT.Ln).then_inc(log_ready, 1)

        @block.vector
        def _(dve):
            nc.vector.memset(padded[:, :, 0:DC - 1], 0.0).then_inc(zeroed, 1)
            dve.wait_ge(w_in, 16 * 5)
            dve.wait_ge(zeroed, 1)
            with dve.Fori(0, B) as i:
                dve.wait_ge(u_ready, i * ET + 1)
                for tap in range(DC):
                    for et in range(ET):
                        src = padded[:, et, tap:tap + T]
                        if tap == 0:
                            b, turn = ring.at(("x", et), i)
                            dve.wait_ge(ring.free[b], turn + 1)
                            ins = nc.vector.tensor_scalar(conv[:, et, :], src, cols[:, et, 0:1], None, ALU.mult)
                        else:
                            dve.wait_ge(conv_step, i * (ET * DC) + (tap - 1) * ET + et + 1 + 1)
                            ins = nc.vector.scalar_tensor_tensor(
                                out=conv[:, et, :], in0=src, scalar=cols[:, et, tap:tap + 1],
                                in1=conv[:, et, :], op0=ALU.mult, op1=ALU.add)
                        ins.then_inc(conv_step, 1)
                b, turn = ring.at(("dbl",), i)
                dve.wait_ge(ring.full[b], turn)
                dve.wait_ge(stored, i * STORES + 1)
                nc.vector.tensor_copy(dbl[:], banks[b][0:DR + 2 * DS, :]).then_inc(ring.free[b], 1)
                for et in range(ET):
                    b, turn = ring.at(("dt", et), i)
                    dve.wait_ge(ring.full[b], turn)
                    nc.vector.tensor_scalar(dt[:, et, :], banks[b][:], cols[:, et, DC + 1:DC + 2], None, ALU.add) \
                        .then_inc(ring.free[b], 1)
                for et in range(ET):
                    b, turn = ring.at(("dt", et), i)
                    dve.wait_ge(ring.free[b], turn + 1)
                    nc.vector.scalar_tensor_tensor(out=e[:, et, :], in0=dt[:, et, :], scalar=-1.0, in1=dt[:, et, :],
                                                   op0=ALU.mult, op1=ALU.min).then_inc(neg_abs, 1)
                for et in range(ET):
                    dve.wait_ge(log_ready, i * ET + et + 1)
                    nc.vector.scalar_tensor_tensor(out=e[:, et, :], in0=one_e[:, et, :], scalar=1.0, in1=e[:, et, :],
                                                   op0=ALU.subtract, op1=ALU.subtract).then_inc(log_step, 1)
                for et in range(ET):
                    dve.wait_ge(log_step, i * (2 * ET) + et + 1)
                    nc.vector.tensor_tensor(log1p[:, et, :], log1p[:, et, :], e[:, et, :], ALU.subtract) \
                        .then_inc(log_step, 1)
                for et in range(ET):
                    dve.wait_ge(log_step, i * (2 * ET) + ET + et + 1)
                    nc.vector.scalar_tensor_tensor(out=delta[:, et, :], in0=dt[:, et, :], scalar=0.0,
                                                   in1=log1p[:, et, :], op0=ALU.max, op1=ALU.add) \
                        .then_inc(delta_ready, 1)

        @block.gpsimd
        def _(pool):
            pool.wait_ge(w_in, 16 * 5)
            with pool.Fori(0, B) as i:
                for et in range(ET):
                    wait_apart(pool, e_ready, i * ET + et + 1, waited)
                    nc.gpsimd.tensor_scalar(one_e[:, et, :], e[:, et, :], 1.0, 1.0, ALU.mult, ALU.add) \
                        .then_inc(one_e_ready, 1)
                for et in range(ET):
                    wait_apart(pool, delta_ready, i * ET + et + 1, waited)
                    nc.gpsimd.tensor_scalar(d_u[:, et, :], u[:, et, :], cols[:, et, DC + 2:DC + 3], 1.0,
                                            ALU.mult, ALU.mult)
                    nc.gpsimd.tensor_tensor(delta_u[:, et, :], delta[:, et, :], u[:, et, :], ALU.mult) \
                        .then_inc(products, 1)


def stage_gate(core, sb, psum, dram, x, consts, scratch):
    nc = core.nc
    norm = Norm(core, sb, "g")
    y = sb("g_y", [P, B, ET, T], F32)
    z = sb("g_z", [P, ET, T], F32)
    gy = sb("g_gy", [P, ET, T], F32)
    banks = [psum(f"g_bank{b}", [P, 512], F32) for b in range(TT)]
    y_in = core.sem("g_y_in")
    silu_done = core.sem("g_silu")
    gated = core.sem("g_gated")
    full = core.sems("g_full", TT)
    free = core.sems("g_free", TT)

    with nc.Block() as block:
        @block.sync
        def _(sp):
            for b in range(B):
                sp.dma_start(y[:, b], scratch["y"][b]).then_inc(y_in, 16)

        @block.scalar
        def _(act):
            with act.Fori(0, B) as i:
                act.wait_ge(norm.xn_ready, (i + 1) * TT)
                act.wait_ge(gated, i * ET + 1)
                for et in range(ET):
                    nc.scalar.activation(z[:, et, :], norm.xn[:, et, :], ACT.Silu).then_inc(silu_done, 1)

        @block.gpsimd
        def _(pool):
            pool.wait_ge(y_in, 16 * B)
            with pool.Fori(0, B) as i:
                norm_gpsimd(nc, pool, norm, consts.minus_half, i)
                for tt in range(TT):
                    pool.wait_ge(full[tt], i + 1)
                for et in range(ET):
                    pool.wait_ge(silu_done, i * ET + et + 1 + 1)
                    nc.gpsimd.tensor_tensor(gy[:, et, :], y[:, i, et, :], z[:, et, :], ALU.mult).then_inc(gated, 1)

        @block.tensor
        def _(pe):
            start_at_one(pe, gated, *free, silu_done, *full)
            with pe.Fori(0, B) as i:
                pe.wait_ge(gated, (i + 1) * ET + 1)
                for tt in range(TT):
                    pe.wait_ge(free[tt], i + 1)
                    for et in range(ET):
                        mm = nc.tensor.transpose(banks[tt][:, et * P:(et + 1) * P],
                                                 gy[:, et, tt * P:(tt + 1) * P], consts.ident[:])
                    mm.then_inc(full[tt], 1)

        @block.vector
        def _(dve):
            with dve.Fori(0, B) as i:
                dve.wait_ge(silu_done, i * ET + 1)
                norm_vector(nc, dve, norm, x, i)
                for tt in range(TT):
                    dve.wait_ge(full[tt], i + 1 + 1)
                    nc.vector.tensor_tensor(x[:, i, tt, :], banks[tt][:], x[:, i, tt, :], ALU.add) \
                        .then_inc(free[tt], 1)


def stage_mix(core, sb, psum, dram, x, consts):
    nc = core.nc
    norm = Norm(core, sb, "r")
    factors = sb("r_factors", [P, RANK, KD, D], F32)
    bias = sb("r_bias", [P, D], F32)
    xn_t = sb("r_xn_t", [P, KD, T], F32)
    res = sb("r_res", [P, 2, TT, D], F32)
    banks = [psum(f"r_bank{b}", [P, 512], F32) for b in range(8)]
    ring = Ring(core.sems("r_full", 8), core.sems("r_free", 8),
                [("xn", k) for k in range(KD)] + [("out", tt) for tt in range(TT)])
    w_in = core.sems("r_in", RANK)
    bias_in = core.sem("r_bias_in")
    summed = core.sem("r_summed")
    biased = core.sem("r_biased")
    stored = core.sems("r_stored", 2)

    with nc.Block() as block:
        @block.sync
        def _(sp):
            for r in range(RANK):
                sp.dma_start(factors[:, r], dram["factors"][r].rearrange("(k p) e -> p k e", p=P)) \
                    .then_inc(w_in[r], 16)
            sp.dma_start(bias[:], dram["bias"].rearrange("(o e) -> o e", o=1).broadcast_to([P, D])) \
                .then_inc(bias_in, 16)
            with sp.Fori(0, B // 2) as pair:
                for s in range(2):
                    i = pair * 2 + s
                    for tt in range(TT):
                        b, turn = ring.at(("out", tt), i)
                        sp.wait_ge(ring.free[b], turn + 1)
                        sp.dma_start(dram["out"][i, tt * P:(tt + 1) * P, :], res[:, s, tt, :]) \
                            .then_inc(stored[s], 16)
            for s in range(2):
                sp.wait_ge(stored[s], B // 2 * TT * 16 + 1)

        @block.gpsimd
        def _(pool):
            for r in range(1, RANK):
                pool.wait_ge(w_in[r], 16)
                if r == 1:
                    pool.wait_ge(w_in[0], 16)
                else:
                    pool.wait_ge(summed, r - 1)
                nc.gpsimd.tensor_tensor(factors[:, 0], factors[:, 0], factors[:, r], ALU.add).then_inc(summed, 1)
            pool.wait_ge(bias_in, 16)
            with pool.Fori(0, B) as i:
                norm_gpsimd(nc, pool, norm, consts.minus_half, i)
                pool.wait_ge(norm.xn_ready, (i + 1) * TT)
                for tt in range(TT):
                    nc.gpsimd.tensor_tensor(x[:, i, tt, :], x[:, i, tt, :], bias[:], ALU.add).then_inc(biased, 1)

        @block.tensor
        def _(pe):
            start_at_one(pe, *stored, *ring.free)
            with pe.Fori(0, B) as i:
                norm_tensor(nc, pe, norm, consts.ident, ring, banks, i)
                ring.wait_free(pe, i, consumed=[("xn", k) for k in range(KD)])
                pe.wait_ge(summed, RANK - 1)
                for tt in range(TT):
                    b, turn = ring.at(("out", tt), i)
                    pe.wait_ge(ring.free[b], turn)
                    for k in range(KD):
                        mm = nc.tensor.matmul(banks[b][:], xn_t[:, k, tt * P:(tt + 1) * P], factors[:, 0, k, :],
                                              start=(k == 0), stop=(k == KD - 1))
                    mm.then_inc(ring.full[b], 1)

        @block.scalar
        def _(act):
            with act.Fori(0, B) as i:
                for k in range(KD):
                    b, turn = ring.at(("xn", k), i)
                    act.wait_ge(ring.full[b], turn)
                    nc.scalar.copy(xn_t[:, k, :], banks[b][:]).then_inc(ring.free[b], 1)

        @block.vector
        def _(dve):
            with dve.Fori(0, B // 2) as pair:
                for s in range(2):
                    i = pair * 2 + s
                    norm_vector(nc, dve, norm, x, i)
                    dve.wait_ge(stored[s], pair * (TT * 16) + 1)
                    for tt in range(TT):
                        b, turn = ring.at(("out", tt), i)
                        dve.wait_ge(ring.full[b], turn)
                        dve.wait_ge(biased, i * TT + tt + 1)
                        nc.vector.scalar_tensor_tensor(out=res[:, s, tt, :], in0=banks[b][:],
                                                       scalar=1.0 / math.sqrt(RANK), in1=x[:, i, tt, :],
                                                       op0=ALU.mult, op1=ALU.add).then_inc(ring.free[b], 1)


_WEIGHTS = ("wq_t", "wk_t", "wv_t", "wo_t", "cos2", "sin2", "x_wq_t", "x_wk_t", "x_bq", "x_bk", "ctx_t",
            "lut", "idx", "d_w", "d_wp", "lq1", "lk1", "lq2", "lk2", "rowsel", "m_in_t", "m_x_t",
            "m_dt_t", "m_cols", "m_a_log", "factors", "bias", "identity", "masks", "x")
STAGES = ("A", "B", "W", "C", "D", "M", "S", "G", "R")


def program(nc, dram, stages=STAGES, dump=None):
    scratch = {
        "bc": nc.dram_tensor("scan_bc", [B, 2 * DS, T], F32, kind="Internal").ap(),
        "delta": nc.dram_tensor("scan_delta", [B, P, ET, T], F32, kind="Internal").ap(),
        "delta_u": nc.dram_tensor("scan_delta_u", [B, P, ET, T], F32, kind="Internal").ap(),
        "weights": nc.dram_tensor("ffn_weights", [P, W_ALL], I32, kind="Internal").ap(),
        "y": nc.dram_tensor("scan_y", [B, P, ET, T], F32, kind="Internal").ap(),
    }
    with ExitStack() as whole:
        core = Core(nc)

        def keeper(stack):
            return (lambda n, s, d: stack.enter_context(nc.sbuf_tensor(n, s, d)),
                    lambda n, s, d: stack.enter_context(nc.psum_tensor(n, s, d)))

        sb, _ = keeper(whole)
        x = sb("x_res", [P, B, TT, D], F32)
        consts = Consts(sb)
        with ExitStack() as stage:
            sb, psum = keeper(stage)
            stage_setup(core, sb, dram, x, consts)
        core.clear()
        if "A" in stages:
            with ExitStack() as stage:
                stage_window_attention(core, *keeper(stage), dram, x, consts, scratch)
            core.clear()
        if "B" in stages:
            with ExitStack() as ffn:
                weights = keeper(ffn)[0]("ffn_w", [P, W_ALL], F32)
                weights_in = nc.alloc_semaphore(name="ffn_weights_in")
                fetch = (weights, scratch["weights"], weights_in)
                with ExitStack() as stage:
                    stage_cross_attention(core, *keeper(stage), dram, x, consts, fetch)
                core.clear()
                with ExitStack() as stage:
                    stage_scan_inputs(core, *keeper(stage), dram, scratch)
                core.clear()
                with ExitStack() as stage:
                    stage_ffn(core, *keeper(stage), dram, x, consts, weights, weights_in, scratch)
                core.taken.append(weights_in)
                core.clear()
        if "D" in stages:
            with ExitStack() as stage:
                stage_diff_attention(core, *keeper(stage), dram, x, consts)
            core.clear()
        if "M" in stages:
            with ExitStack() as stage:
                stage_gate(core, *keeper(stage), dram, x, consts, scratch)
            core.clear()
        if "R" in stages:
            with ExitStack() as stage:
                stage_mix(core, *keeper(stage), dram, x, consts)
            core.clear()
        if dump is not None:
            done = core.sem("dumped")
            with nc.Block() as block:
                @block.sync
                def _(sp):
                    for b in range(B):
                        sp.dma_start(dram["out"][b].rearrange("(t p) d -> p t d", p=P), x[:, b]).then_inc(done, 16)
                    sp.wait_ge(done, 16 * B)


def laid_out(v):
    c = np.ascontiguousarray
    out = {
        "x": v["x"], "ctx_t": c(v["ctx_1024"].transpose(0, 2, 1)),
        "wq_t": c(v["L0_attn_wq"].T), "wk_t": c(v["L0_attn_wk"].T), "wv_t": c(v["L0_attn_wv"].T),
        "wo_t": c(v["L0_attn_wo"].T),
        "x_wq_t": c(v["L0_xattn_Wq"].T), "x_wk_t": c(v["L0_xattn_Wk"].T),
        "x_bq": v["L0_xattn_bq"], "x_bk": v["L0_xattn_bk"],
        "lut": v["L0_ffn_lut"],
        "lq1": v["L1_attn_lambda_q1"], "lk1": v["L1_attn_lambda_k1"],
        "lq2": v["L1_attn_lambda_q2"], "lk2": v["L1_attn_lambda_k2"], "d_wp": v["L1_attn_W_proj"],
        "m_in_t": c(v["L1_xattn_in_proj_w"].T), "m_x_t": c(v["L1_xattn_x_proj_w"].T),
        "m_dt_t": c(v["L1_xattn_dt_proj_w"].T), "m_a_log": v["L1_xattn_A_log"],
        "m_cols": c(np.concatenate([v["L1_xattn_conv_w"], v["L1_xattn_conv_b"][:, None],
                                    v["L1_xattn_dt_proj_b"][:, None], v["L1_xattn_D"][:, None]], axis=1)),
        "factors": v["L1_ffn_factors"], "bias": v["L1_ffn_bias"],
    }
    tiles = lambda a: a.reshape(-1, P, a.shape[1]).transpose(1, 0, 2).reshape(P, -1)
    down = np.zeros((OT * P, D), v["L0_ffn_down_idx"].dtype)
    down[:INTER] = v["L0_ffn_down_idx"].T
    out["idx"] = c(np.concatenate([tiles(v["L0_ffn_gate_idx"].T), tiles(v["L0_ffn_up_idx"].T), tiles(down)],
                                  axis=1))
    w = v["L1_attn_W_attn"].reshape(D, 3 * D)
    part = lambda n: w[:, n * (D // 2):(n + 1) * (D // 2)].reshape(D, DH, DHD)
    out["d_w"] = c(np.concatenate([np.concatenate([part(0), part(2)], axis=2).reshape(D, D),
                                   np.concatenate([part(1), part(3)], axis=2).reshape(D, D),
                                   w[:, 2 * D:]], axis=1))
    half = HD // 2
    inv_freq = (1.0 / np.float32(10000.0) ** (np.arange(half, dtype=np.float32) / np.float32(half)))
    freqs = np.outer(np.arange(T, dtype=np.float32), inv_freq.astype(np.float32))
    cos, sin = np.cos(freqs).T.astype(np.float32), np.sin(freqs).T.astype(np.float32)
    out["cos2"], out["sin2"] = c(np.concatenate([cos, cos])), c(np.concatenate([-sin, sin]))
    out["identity"] = np.eye(P, dtype=np.float32)
    row, col = np.arange(P)[:, None], np.arange(2 * P)[None, :]
    own = (col - P <= row) & (col >= P)
    seen = np.stack([own, own | ((col < P) & (row + P - col <= WINDOW))])
    out["masks"] = c(np.where(seen, 0.0, MASKED).astype(np.float32).transpose(1, 0, 2))
    q2 = (np.arange(P) // DHD) % 2
    out["rowsel"] = c(np.stack([1 - q2, q2], axis=1).astype(np.float32) * np.float32(DHD ** -0.5))
    return out


def kernel(**inputs):
    import concourse.bacc as bacc
    from concourse.bass_utils import run_bass_kernel_spmd

    nc = bacc.Bacc("TRN2", target_bir_lowering=False, num_devices=1)
    arrays = {f"in_{k}": a for k, a in laid_out({k: np.asarray(a) for k, a in inputs.items()}).items()}
    dram = {n[3:]: nc.dram_tensor(n, a.shape, mybir.dt.from_np(a.dtype), kind="ExternalInput").ap()
            for n, a in arrays.items()}
    dram["out"] = nc.dram_tensor("out", [B, T, D], F32, kind="ExternalOutput").ap()
    program(nc, dram)
    return run_bass_kernel_spmd(nc, [arrays], core_ids=[0]).results[0]["out"]
```

```python
import math
from contextlib import ExitStack

import numpy as np

import concourse.bass as bass
from concourse import mybir

ALU = mybir.AluOpType
ACT = mybir.ActivationFunctionType
AX_X = mybir.AxisListType.X
F32 = mybir.dt.float32
F32R = mybir.dt.float32r
BF16 = mybir.dt.bfloat16
I32 = mybir.dt.int32

P = 128
B, T, D = 4, 512, 512
TT = T // P
KD = D // P
C = 256
KC = C // P
EPS = 1e-5
HEADS, KV, HD = 16, 4, 128
REPS = HEADS // KV
WINDOW = 128
MASKED = -1e30
QK = 128
INTER = 1376
OT = -(-INTER // P)
LUT = 16
DH, DHD = 16, 16
LAMBDA_INIT = 0.8 - 0.6 * math.exp(-0.3 * 0)
DI, DS, DC, DR = 512, 16, 4, 16
ET = DI // P
NQ = 4
NS = 2
RANK = 8
W_UP, W_DOWN = KD * INTER, 2 * KD * INTER
W_ALL = W_DOWN + OT * D
CHUNKS = 64
CH = W_ALL // CHUNKS


class Ring:

    def __init__(self, full, free, steps, last_steps=None):
        self.full, self.free = full, free
        self.place, self.per = self.deal(steps)
        self.last_place = self.place if last_steps is None else self.deal(last_steps)[0]

    def deal(self, steps):
        per, place = [0] * len(self.full), {}
        for n, step in enumerate(steps):
            b = n % len(self.full)
            assert step not in place, step
            place[step] = (b, per[b])
            per[b] += 1
        return place, per

    def placed(self, step, i):
        return (self.last_place if isinstance(i, int) and i == B - 1 else self.place)[step]

    def at(self, step, i):
        b, nth = self.placed(step, i)
        return b, i * self.per[b] + nth + 1

    def wait_free(self, eng, i, out=None, consumed=()):
        need = {}
        if out is not None:
            b, nth = self.placed(out, i)
            need[b] = nth
        for step in consumed:
            b, nth = self.placed(step, i)
            need[b] = max(need.get(b, 0), nth + 1)
        for b, count in need.items():
            eng.wait_ge(self.free[b], i * self.per[b] + count + 1)


class Core:

    def __init__(self, nc):
        self.nc, self.taken = nc, []

    def sem(self, name):
        self.taken.append(self.nc.alloc_semaphore(name=name))
        return self.taken[-1]

    def sems(self, name, n):
        return [self.sem(f"{name}{k}") for k in range(n)]

    def clear(self):
        self.nc.clear_and_free_semaphores(self.taken)
        self.taken = []
        self.nc.all_engine_barrier()


class Consts:
    def __init__(self, sb):
        self.ident = sb("ident", [P, P], F32)
        self.ident_bf = sb("ident_bf", [P, P], BF16)
        self.mask_bf = sb("mask_bf", [P, 2, 2 * P], BF16)
        self.minus_half = sb("minus_half", [P, TT], F32)
        self.ones = sb("ones", [P, P], F32)


class Norm:

    def __init__(self, core, sb, tag):
        self.stats_done = core.sem(f"{tag}_ln_stats")
        self.waited = core.sem(f"{tag}_ln_waited")
        self.var_ready = core.sem(f"{tag}_ln_var")
        self.rstd_ready = core.sem(f"{tag}_ln_rstd")
        self.xn_ready = core.sem(f"{tag}_ln_xn")
        self.stats = sb(f"{tag}_stats", [P, TT, 6], F32)
        self.mean_var = sb(f"{tag}_mean_var", [P, TT, 2], F32)
        self.var_eps = sb(f"{tag}_var_eps", [P, TT], F32)
        self.rstd = sb(f"{tag}_rstd", [P, TT], F32)
        self.xn = sb(f"{tag}_xn", [P, TT, D], F32)


def start_at_one(eng, *sems):
    for sem in sems:
        eng.sem_inc(sem, 1)


def wait_apart(eng, sem, value, waited):
    eng.wait_ge(sem, value)
    eng.sem_inc(waited, 1)


def passes(eng, one_pass):
    with eng.Fori(0, B - 1) as i:
        one_pass(i, True)
    one_pass(B - 1, False)


def norm_vector(nc, dve, norm, x, i):
    for tt in range(TT):
        last = nc.vector.bn_stats(norm.stats[:, tt, :], x[:, i, tt, :])
    last.then_inc(norm.stats_done, 1)
    wait_apart(dve, norm.stats_done, i * 2 + 1, norm.waited)
    for tt in range(TT):
        last = nc.vector.bn_aggr(norm.mean_var[:, tt, :], norm.stats[:, tt, :])
    last.then_inc(norm.stats_done, 1)
    dve.wait_ge(norm.stats_done, i * 2 + 2)
    nc.vector.tensor_scalar(norm.var_eps[:], norm.mean_var[:, :, 1], EPS, None, ALU.add) \
        .then_inc(norm.var_ready, 1)
    dve.wait_ge(norm.rstd_ready, i + 1)
    for tt in range(TT):
        nc.vector.tensor_scalar(norm.xn[:, tt, :], x[:, i, tt, :], norm.mean_var[:, tt, 0:1],
                                norm.rstd[:, tt:tt + 1], ALU.subtract, ALU.mult) \
            .then_inc(norm.xn_ready, 1)


def norm_gpsimd(nc, pool, norm, minus_half, i):
    pool.wait_ge(norm.var_ready, i + 1)
    nc.gpsimd.tensor_tensor(norm.rstd[:], norm.var_eps[:], minus_half[:], ALU.pow) \
        .then_inc(norm.rstd_ready, 1)


def norm_tensor(nc, pe, norm, ident, ring, banks, i, in_pass=None, tiles=range(KD)):
    pe.wait_ge(norm.xn_ready, (i + 1) * TT)
    for k in tiles:
        b, turn = ring.at(("xn", k), i if in_pass is None else in_pass)
        pe.wait_ge(ring.free[b], turn)
        for tt in range(TT):
            mm = nc.tensor.transpose(banks[b][:, tt * P:(tt + 1) * P],
                                     norm.xn[:, tt, k * P:(k + 1) * P], ident[:])
        mm.then_inc(ring.full[b], 1)


def stage_setup(core, sb, dram, x, consts):
    nc = core.nc
    loaded = core.sem("setup_loaded")
    mask_f = sb("mask_f", [P, 2, 2 * P], F32)
    with nc.Block() as block:
        @block.sync
        def _(sp):
            sp.dma_start(consts.ident[:], dram["identity"]).then_inc(loaded, 16)
            sp.dma_start(mask_f[:], dram["masks"]).then_inc(loaded, 16)
            sp.dma_start(x[:, 0], dram["x"][0].rearrange("(t p) d -> p t d", p=P)).then_inc(loaded, 16)
            sp.wait_ge(loaded, 16 * 3)

        @block.vector
        def _(dve):
            nc.vector.memset(consts.minus_half[:], -0.5)
            nc.vector.memset(consts.ones[:], 1.0)
            dve.wait_ge(loaded, 16 * 3)
            nc.vector.tensor_copy(consts.ident_bf[:], consts.ident[:])
            nc.vector.tensor_copy(consts.mask_bf[:], mask_f[:])


class Lookup:
    PER_PASS = CHUNKS // B
    STEPS = 5

    def __init__(self, core, sb, dram, scratch):
        self.nc, self.dram, self.scratch = core.nc, dram, scratch
        self.lut = sb("f_lut", [P, LUT], I32)
        self.lut_xor = sb("f_lut_xor", [P, LUT // 2], I32)
        self.idx = sb("f_idx", [P, 2, CH], I32)
        self.mask = sb("f_mask", [P, 4, CH], I32)
        self.picks = sb("f_picks", [P, LUT // 2, CH], I32)
        self.lut_in = core.sem("f_lut_in")
        self.lut_ready = core.sem("f_lut_ready")
        self.waited = core.sem("f_waited")
        self.idx_in = core.sems("f_idx_in", 2)
        self.step_done = core.sem("f_step")
        self.stored = core.sem("f_stored")

    def load_table(self, sp):
        sp.dma_start(self.lut[:], self.dram["lut"].bitcast(I32).rearrange("(o l) -> o l", o=1)
                     .broadcast_to([P, LUT])).then_inc(self.lut_in, 16)

    def step_value(self, i, n, steps):
        return (i * self.PER_PASS + n) * self.STEPS + steps + 1

    def sync(self, sp, i):
        def store(n):
            sp.wait_ge(self.step_done, self.step_value(i, n, self.STEPS))
            sp.dma_start(self.scratch["weights"][:, bass.ds(i * (self.PER_PASS * CH) + n * CH, CH)],
                         self.picks[:, 0, :]).then_inc(self.stored, 16)

        for n in range(self.PER_PASS):
            if n == 1:
                sp.wait_ge(self.step_done, self.step_value(i, 0, 0))
            elif n > 1:
                sp.wait_ge(self.step_done, self.step_value(i, n - 2, 1))
            sp.dma_start(self.idx[:, n % 2, :],
                         self.dram["idx"][:, bass.ds(i * (self.PER_PASS * CH) + n * CH, CH)]) \
                .then_inc(self.idx_in[n % 2], 16)
            if n:
                store(n - 1)
        store(self.PER_PASS - 1)

    def sync_end(self, sp):
        sp.wait_ge(self.stored, 16 * CHUNKS + 1)

    def vector_setup(self, dve):
        start_at_one(dve, self.step_done, self.stored)
        dve.wait_ge(self.lut_in, 16)
        pairs = self.lut[:].rearrange("p (j two) -> p j two", two=2)
        self.nc.vector.tensor_tensor(self.lut_xor[:], pairs[:, :, 0], pairs[:, :, 1], ALU.bitwise_xor) \
            .then_inc(self.lut_ready, 1)
        dve.wait_ge(self.lut_ready, 1)

    def own_step(self, i, n, steps):
        wait_apart(self.nc.vector, self.step_done, self.step_value(i, n, steps), self.waited)

    def pick(self, i, n):
        dve, mask, picks, s = self.nc.vector, self.mask, self.picks, n % 2
        dve.wait_ge(self.idx_in[s], (i * (self.PER_PASS // 2) + n // 2 + 1) * 16)
        self.own_step(i, n, 0)
        dve.tensor_scalar(mask[:, 0, :], self.idx[:, s, :], 31, 31,
                          ALU.logical_shift_left, ALU.arith_shift_right)
        for bit in range(1, 4):
            last = dve.tensor_scalar(mask[:, bit, :], self.idx[:, s, :], 1 << bit, None, ALU.bitwise_and)
        last.then_inc(self.step_done, 1)
        self.own_step(i, n, 1)
        for j in reversed(range(LUT // 2)):
            if j == 0:
                dve.wait_ge(self.stored, (i * self.PER_PASS + n) * 16 + 1)
            last = dve.tensor_scalar(picks[:, j, :], mask[:, 0, :], self.lut_xor[:, j:j + 1],
                                     self.lut[:, 2 * j:2 * j + 1], ALU.bitwise_and, ALU.bitwise_xor)
        last.then_inc(self.step_done, 1)

    def choose(self, i, n):
        for level in range(3):
            self.own_step(i, n, 2 + level)
            half = 1 << level
            for j in range(0, LUT // 2, 2 * half):
                last = self.nc.vector.copy_predicated(self.picks[:, j, :], self.mask[:, level + 1, :],
                                                      self.picks[:, j + half, :])
            last.then_inc(self.step_done, 1)


def stage_window_attention(core, sb, psum, dram, x, consts, scratch):
    nc = core.nc
    scale = 1.0 / math.sqrt(HD)
    wq = sb("a_wq", [P, KD, HEADS * HD], F32)
    wk = sb("a_wk", [P, KD, KV * HD], F32)
    wv = sb("a_wv", [P, KD, KV * HD], F32)
    wo = sb("a_wo", [P, HEADS, D], F32)
    cos2 = sb("a_cos2", [P, T], F32)
    sin2 = sb("a_sin2", [P, T], F32)
    norm = Norm(core, sb, "a")
    xn_t = sb("a_xn_t", [P, KD, T], F32)
    q_t = sb("a_q_t", [P, REPS, T], F32)
    k_t = sb("a_k_t", [P, 2, T], F32)
    v = sb("a_v", [P, TT, KV * HD], F32)
    rope_b = sb("a_rope_b", [P, 2, T], F32)
    prob = sb("a_prob", [P, REPS, TT, 2 * P], F32)
    prob_t = sb("a_prob_t", [P, 2, 2, REPS * P], F32)
    out_t = sb("a_out_t", [P, TT, REPS * P], F32)
    mx = sb("a_mx", [P, HEADS, TT], F32)
    neg_m = sb("a_neg_m", [P, HEADS, TT], F32)
    sums = sb("a_sums", [P, HEADS, TT], F32)
    rsum = sb("a_rsum", [P, HEADS, TT], F32)

    banks = [psum(f"a_bank{b}", [P, 512], F32) for b in range(4)]
    score = [psum(f"a_score{s}", [P, TT, 2 * P], F32) for s in range(2)]

    proj = lambda g: [("k", g)] + [("q", g, r) for r in range(REPS)]
    xn_steps = [("xn", k) for k in range(KD)]
    v_steps = [("v", tt) for tt in range(TT)]

    def steps(more):
        order = []
        for g in range(KV):
            if g + 1 < KV:
                order += proj(g + 1)
            elif more:
                order += xn_steps + proj(0)
            order += [("turn", g, 0, 0), ("turn", g, 1, 0), ("turn", g, 1, 1), ("pv", g, 0),
                      ("turn", g, 2, 0), ("turn", g, 2, 1), ("pv", g, 1),
                      ("turn", g, 3, 0), ("turn", g, 3, 1), ("pv", g, 2), ("pv", g, 3)]
            order += [("wo", g, tt) for tt in range(TT)]
        return order + (v_steps if more else [])

    ring = Ring(core.sems("a_full", 4), core.sems("a_free", 4), steps(True), steps(False))
    first = Ring(core.sems("a_first_full", 4), core.sems("a_first_free", 4), xn_steps + proj(0) + v_steps)
    lookup = Lookup(core, sb, dram, scratch)

    w_in = {n: core.sem(f"a_in_{n}") for n in ("wk", "wv", "wo", "rope")}
    wq_in = core.sems("a_in_wq", KV)
    x_in = core.sem("a_in_x")
    swapped = core.sems("a_swapped", 2)
    by_sin = core.sem("a_by_sin")
    rope_done = core.sems("a_rope_done", 2)
    score_full = core.sems("a_score_full", 2)
    max_done = core.sem("a_max_done")
    neg_ready = core.sem("a_neg_ready")
    exp_done = core.sems("a_exp_done", 2)
    waited = core.sem("a_waited")
    rsum_ready = core.sem("a_rsum_ready")
    prob_ready = core.sem("a_prob_ready")
    PER_ROPE = KV * (1 + REPS) // 2
    PER_SLOT = HEADS // 2

    def roped(g, step):
        return k_t[:, g % 2, :] if step[0] == "k" else q_t[:, step[2], :]

    def load_queries(eng, g):
        columns = slice(g * REPS * HD, (g + 1) * REPS * HD)
        eng.dma_start(wq[:, :, columns], dram["wq_t"].rearrange("(k p) o -> p k o", p=P)[:, :, columns]) \
            .then_inc(wq_in[g], 16)

    with nc.Block() as block:
        @block.sync
        def _(sp):
            sp.dma_start(wk[:], dram["wk_t"].rearrange("(k p) o -> p k o", p=P)).then_inc(w_in["wk"], 16)
            sp.dma_start(cos2[:], dram["cos2"]).then_inc(w_in["rope"], 16)
            sp.dma_start(sin2[:], dram["sin2"]).then_inc(w_in["rope"], 16)
            load_queries(sp, 0)
            sp.dma_start(wv[:], dram["wv_t"].rearrange("(k p) o -> p k o", p=P)).then_inc(w_in["wv"], 16)
            lookup.load_table(sp)
            with sp.Fori(0, B) as i:
                lookup.sync(sp, i)
            lookup.sync_end(sp)

        @block.tensor
        def _(pe):
            start_at_one(pe, *rope_done, *exp_done, *ring.free, *first.free)

            def project(ring, i, g, steps):
                pe.wait_ge(wq_in[g], 16)
                for step in steps:
                    w = wk[:, :, g * HD:(g + 1) * HD] if step[0] == "k" else \
                        wq[:, :, (g * REPS + step[2]) * HD:(g * REPS + step[2] + 1) * HD]
                    b, turn = ring.at(step, i)
                    pe.wait_ge(ring.free[b], turn)
                    for k in range(KD):
                        mm = nc.tensor.matmul(banks[b][:], w[:, k, :], xn_t[:, k, :],
                                              start=(k == 0), stop=(k == KD - 1))
                    mm.then_inc(ring.full[b], 1)

            def scores(i, g, heads):
                for r in heads:
                    h = g * REPS + r
                    s = h % 2
                    n = g * (1 + REPS) + 1 + r
                    pe.wait_ge(rope_done[n % 2], i * PER_ROPE + n // 2 + 2)
                    if r == 0:
                        pe.wait_ge(rope_done[1 - n % 2], i * PER_ROPE + (n - 1) // 2 + 2)
                    pe.wait_ge(exp_done[s], i * PER_SLOT + h // 2 + 1)
                    for tt in range(TT):
                        out = score[s][:, tt, :]
                        nc.tensor.matmul(out, consts.ident_bf[:], consts.mask_bf[:, min(tt, 1), :],
                                         start=True, stop=False)
                        lo = P if tt == 0 else 0
                        mm = nc.tensor.matmul(out[:, lo:], q_t[:, r, tt * P:(tt + 1) * P],
                                              k_t[:, g % 2, tt * P - P + lo:(tt + 1) * P],
                                              start=False, stop=True)
                    mm.then_inc(score_full[s], 1)

            def turn_probs(i, g, tt, prev):
                b, turn = ring.at(("turn", g, tt, prev), i)
                pe.wait_ge(ring.free[b], turn)
                lo = 0 if prev else P
                for r in range(REPS):
                    mm = nc.tensor.transpose(banks[b][:, r * P:(r + 1) * P],
                                             prob[:, r, tt, lo:lo + P], consts.ident[:])
                mm.then_inc(ring.full[b], 1)

            def weigh(i, g, tt):
                ring.wait_free(pe, i, ("pv", g, tt),
                               consumed=[("turn", g, tt, prev) for prev in range(min(tt, 1) + 1)])
                b, _ = ring.at(("pv", g, tt), i)
                for prev in range(min(tt, 1) + 1):
                    mm = nc.tensor.matmul(banks[b][:], v[:, tt - prev, g * HD:(g + 1) * HD],
                                          prob_t[:, tt % 2, prev, :],
                                          start=(prev == 0), stop=(prev == min(tt, 1)))
                mm.then_inc(ring.full[b], 1)

            def values(ring, i):
                for tt in range(TT):
                    b, turn = ring.at(("v", tt), i)
                    pe.wait_ge(ring.free[b], turn)
                    for k in range(KD):
                        mm = nc.tensor.matmul(banks[b][:], xn_t[:, k, tt * P:(tt + 1) * P], wv[:, k, :],
                                              start=(k == 0), stop=(k == KD - 1))
                    mm.then_inc(ring.full[b], 1)

            def one_pass(i, more):
                for g in range(KV):
                    if g == KV - 1 and more:
                        norm_tensor(nc, pe, norm, consts.ident, ring, banks, i + 1, in_pass=i)
                    ng = (g + 1) % KV
                    nxt = proj(ng) if more or ng else []
                    scores(i, g, (0, 1))
                    if ng == 0 and more:
                        ring.wait_free(pe, i, consumed=xn_steps)
                    project(ring, i, ng, nxt[0:2])
                    scores(i, g, (2,))
                    project(ring, i, ng, nxt[2:3])
                    scores(i, g, (3,))
                    project(ring, i, ng, nxt[3:])
                    pe.wait_ge(prob_ready, i * HEADS + (g + 1) * REPS)
                    turn_probs(i, g, 0, 0)
                    turn_probs(i, g, 1, 0)
                    turn_probs(i, g, 1, 1)
                    for tt in range(TT):
                        weigh(i, g, tt)
                        if tt + 2 < TT:
                            turn_probs(i, g, tt + 2, 0)
                            turn_probs(i, g, tt + 2, 1)
                    pe.wait_ge(w_in["wo"], 16)
                    for tt in range(TT):
                        ring.wait_free(pe, i, ("wo", g, tt), consumed=[("pv", g, tt)])
                        b, _ = ring.at(("wo", g, tt), i)
                        for r in range(REPS):
                            mm = nc.tensor.matmul(banks[b][:], out_t[:, tt, r * P:(r + 1) * P],
                                                  wo[:, g * REPS + r, :],
                                                  start=(r == 0), stop=(r == REPS - 1))
                        mm.then_inc(ring.full[b], 1)
                if more:
                    values(ring, i)

            norm_tensor(nc, pe, norm, consts.ident, first, banks, 0)
            first.wait_free(pe, 0, consumed=xn_steps)
            pe.wait_ge(w_in["wk"], 16)
            project(first, 0, 0, proj(0))
            pe.wait_ge(w_in["wv"], 16)
            values(first, 0)
            first.wait_free(pe, 0, consumed=proj(0) + v_steps)
            passes(pe, one_pass)

        @block.scalar
        def _(act):
            def take(step, i, out, ring=ring):
                b, turn = ring.at(step, i)
                act.wait_ge(ring.full[b], turn)
                nc.scalar.copy(out, banks[b][:]).then_inc(ring.free[b], 1)

            def exponentials(i, g, heads):
                for r in heads:
                    h = g * REPS + r
                    act.wait_ge(neg_ready, i * HEADS + h + 1)
                    for tt in range(TT):
                        e = nc.scalar.activation(prob[:, r, tt, :], score[h % 2][:, tt, :], ACT.Exp,
                                                 bias=neg_m[:, h, tt:tt + 1], scale=scale,
                                                 accum_out=sums[:, h, tt:tt + 1])
                    e.then_inc(exp_done[h % 2], 1)

            def swap(ring, in_pass, i, g, steps):
                for step in steps:
                    n = g * (1 + REPS) + proj(g).index(step)
                    b, turn = ring.at(step, in_pass)
                    act.wait_ge(ring.full[b], turn)
                    act.wait_ge(rope_done[n % 2], i * PER_ROPE + n // 2 + 1)
                    h = HD // 2
                    nc.scalar.copy(rope_b[0:h, n % 2, :], banks[b][h:P, :])
                    nc.scalar.copy(rope_b[h:P, n % 2, :], banks[b][0:h, :]).then_inc(swapped[n % 2], 1)

            def features(ring, i):
                for k in (1, 3):
                    take(("xn", k), i, xn_t[:, k, :], ring)

            def values(ring, i):
                for tt in (1, 3):
                    take(("v", tt), i, v[:, tt, :], ring)

            def one_pass(i, more):
                for g in range(KV):
                    if g == KV - 1 and more:
                        features(ring, i)
                    ng = (g + 1) % KV
                    nxt = proj(ng) if more or ng else []
                    at = (ring, i, i + 1 if ng == 0 else i, ng)
                    exponentials(i, g, (0, 1))
                    swap(*at, nxt[0:2])
                    exponentials(i, g, (2,))
                    swap(*at, nxt[2:3])
                    exponentials(i, g, (3,))
                    swap(*at, nxt[3:])
                    take(("turn", g, 0, 0), i, prob_t[:, 0, 0, :])
                    take(("turn", g, 1, 0), i, prob_t[:, 1, 0, :])
                    take(("turn", g, 1, 1), i, prob_t[:, 1, 1, :])
                    for tt in range(TT):
                        take(("pv", g, tt), i, out_t[:, tt, :])
                        if tt + 2 < TT:
                            for prev in range(2):
                                take(("turn", g, tt + 2, prev), i, prob_t[:, tt % 2, prev, :])
                if more:
                    values(ring, i)

            features(first, 0)
            swap(first, 0, 0, 0, proj(0)[0:2])
            load_queries(act, 1)
            act.dma_start(wo[:], dram["wo_t"].rearrange("(h p) o -> p h o", p=P)).then_inc(w_in["wo"], 16)
            for g in range(2, KV):
                load_queries(act, g)
            for b in range(1, B):
                act.dma_start(x[:, b], dram["x"][b].rearrange("(t p) d -> p t d", p=P)).then_inc(x_in, 16)
            swap(first, 0, 0, 0, proj(0)[2:])
            values(first, 0)
            passes(act, one_pass)

        @block.vector
        def _(dve):
            def take(step, i, out, ring=ring):
                b, turn = ring.at(step, i)
                dve.wait_ge(ring.full[b], turn)
                nc.vector.tensor_copy(out, banks[b][:]).then_inc(ring.free[b], 1)

            def rope(ring, in_pass, i, g, steps):
                for step in steps:
                    n = g * (1 + REPS) + proj(g).index(step)
                    b, turn = ring.at(step, in_pass)
                    dve.wait_ge(swapped[n % 2], i * PER_ROPE + n // 2 + 1)
                    nc.vector.tensor_tensor(roped(g, step), banks[b][:], cos2[:], ALU.mult) \
                        .then_inc(ring.free[b], 1)

            def maxima(i, h):
                dve.wait_ge(score_full[h % 2], i * PER_SLOT + h // 2 + 1)
                nc.vector.tensor_reduce(mx[:, h, :], score[h % 2][:], AX_X, ALU.max).then_inc(max_done, 1)
                dve.wait_ge(max_done, i * HEADS + h + 1)
                nc.vector.tensor_scalar(neg_m[:, h, :], mx[:, h, :], -scale, None, ALU.mult) \
                    .then_inc(neg_ready, 1)

            def inverse(i, h):
                dve.wait_ge(exp_done[h % 2], i * PER_SLOT + h // 2 + 2)
                nc.vector.reciprocal(rsum[:, h, :], sums[:, h, :]).then_inc(rsum_ready, 1)

            def features(ring, i):
                for k in (0, 2):
                    take(("xn", k), i, xn_t[:, k, :], ring)

            def values(ring, i):
                for tt in (0, 2):
                    take(("v", tt), i, v[:, tt, :], ring)

            def one_pass(i, more):
                for g in range(KV):
                    if g == KV - 1 and more:
                        features(ring, i)
                    ng = (g + 1) % KV
                    nxt = proj(ng) if more or ng else []
                    at = (ring, i, i + 1 if ng == 0 else i, ng)
                    h = g * REPS
                    maxima(i, h)
                    maxima(i, h + 1)
                    inverse(i, h)
                    lookup.pick(i, g * TT)
                    rope(*at, nxt[0:2])
                    maxima(i, h + 2)
                    inverse(i, h + 1)
                    rope(*at, nxt[2:3])
                    maxima(i, h + 3)
                    inverse(i, h + 2)
                    lookup.choose(i, g * TT)
                    inverse(i, h + 3)
                    rope(*at, nxt[3:])
                    if g == KV - 2 and more:
                        wait_apart(dve, x_in, 16 * (B - 1), waited)
                        norm_vector(nc, dve, norm, x, i + 1)
                    lookup.pick(i, g * TT + 1)
                    lookup.choose(i, g * TT + 1)
                    for tt in range(TT):
                        if tt < 2:
                            lookup.pick(i, g * TT + 2 + tt)
                            lookup.choose(i, g * TT + 2 + tt)
                        b, turn = ring.at(("wo", g, tt), i)
                        dve.wait_ge(ring.full[b], turn)
                        nc.vector.tensor_tensor(x[:, i, tt, :], banks[b][:], x[:, i, tt, :], ALU.add) \
                            .then_inc(ring.free[b], 1)
                if more:
                    values(ring, i)

            norm_vector(nc, dve, norm, x, 0)
            features(first, 0)
            dve.wait_ge(w_in["rope"], 32)
            rope(first, 0, 0, 0, proj(0))
            values(first, 0)
            lookup.vector_setup(dve)
            passes(dve, one_pass)

        @block.gpsimd
        def _(pool):
            def rope_sums(ring, in_pass, i, g, steps):
                for step in steps:
                    n = g * (1 + REPS) + proj(g).index(step)
                    s = n % 2
                    b, turn = ring.at(step, in_pass)
                    pool.wait_ge(swapped[s], i * PER_ROPE + n // 2 + 1)
                    nc.gpsimd.tensor_tensor(rope_b[:, s, :], rope_b[:, s, :], sin2[:], ALU.mult).then_inc(by_sin, 1)
                    pool.wait_ge(by_sin, i * (KV * (1 + REPS)) + n + 1)
                    pool.wait_ge(ring.free[b], turn + 1)
                    nc.gpsimd.tensor_tensor(roped(g, step), roped(g, step), rope_b[:, s, :], ALU.add) \
                        .then_inc(rope_done[s], 1)

            def probabilities(i, h):
                wait_apart(pool, rsum_ready, i * HEADS + h + 1, waited)
                for tt in range(TT):
                    p = nc.gpsimd.tensor_scalar(prob[:, h % REPS, tt, :], prob[:, h % REPS, tt, :],
                                                rsum[:, h, tt:tt + 1], 1.0, ALU.mult, ALU.mult)
                p.then_inc(prob_ready, 1)

            def one_pass(i, more):
                for g in range(KV):
                    ng = (g + 1) % KV
                    nxt = proj(ng) if more or ng else []
                    at = (ring, i, i + 1 if ng == 0 else i, ng)
                    h = g * REPS
                    probabilities(i, h)
                    rope_sums(*at, nxt[0:2])
                    probabilities(i, h + 1)
                    rope_sums(*at, nxt[2:3])
                    probabilities(i, h + 2)
                    probabilities(i, h + 3)
                    rope_sums(*at, nxt[3:])
                    if g == KV - 2 and more:
                        norm_gpsimd(nc, pool, norm, consts.minus_half, i + 1)

            norm_gpsimd(nc, pool, norm, consts.minus_half, 0)
            pool.wait_ge(w_in["rope"], 32)
            rope_sums(first, 0, 0, 0, proj(0))
            passes(pool, one_pass)


def stage_context(core, sb, psum, dram, x, consts, scratch):
    nc = core.nc
    ctx_t = sb("b_ctx_t", [P, B, KC, T], F32)
    w_in = core.sem("b_in_w")
    w_rest_in = core.sem("b_in_w_rest")
    stored = core.sem("b_stored")
    STORES = 4 * 16
    waited = core.sem("b_waited")

    wq = sb("b_wq", [P, KC, QK], F32)
    wk = sb("b_wk", [P, KC, QK], F32)
    bq = sb("b_bq", [P, 1], F32)
    bk = sb("b_bk", [P, 1], F32)
    norm = Norm(core, sb, "b")
    xn_t = sb("b_xn_t", [P, KD, T], F32)
    q_t = sb("b_q_t", [P, T], F32)
    k_t = sb("b_k_t", [P, T], F32)
    att = sb("b_att", [P, TT, T], F32)
    att_t = sb("b_att_t", [P, TT, T], F32)
    mx = sb("b_mx", [P, TT], F32)
    neg_m = sb("b_neg_m", [P, TT], F32)
    sums = sb("b_sums", [P, TT], F32)
    rsum = sb("b_rsum", [P, TT], F32)
    NB = 4
    banks = [psum(f"b_bank{b}", [P, 512], F32) for b in range(NB)]
    xn_steps = [("xn", k) for k in range(KD)]
    turn_steps = [("turn", n) for n in range(TT)]
    ring = Ring(core.sems("b_full", NB), core.sems("b_free", NB),
                [("q",), ("k",)] + [("energy", m) for m in range(TT)] + xn_steps + turn_steps
                + [("out", tt) for tt in range(TT)])
    max_done = core.sem("b_max_done")
    neg_ready = core.sem("b_neg_ready")
    rsum_ready = core.sem("b_rsum_ready")
    att_ready = core.sem("b_att_ready")

    w_in_t = sb("m_w_in", [P, KC, DI], F32)
    w_x = sb("m_w_x", [P, ET, DR + 2 * DS], F32)
    w_dt = sb("m_w_dt", [DR, DI], F32)
    cols = sb("m_cols", [P, ET, DC + 3], F32)
    padded = sb("m_padded", [P, ET, DC - 1 + T], F32)
    conv = sb("m_conv", [P, ET, T], F32)
    u = sb("m_u", [P, ET, T], F32)
    dbl = sb("m_dbl", [DR + 2 * DS, T], F32)
    dt = sb("m_dt", [P, ET, T], F32)
    e = sb("m_e", [P, ET, T], F32)
    one_e = sb("m_one_e", [P, ET, T], F32)
    log1p = sb("m_log1p", [P, ET, T], F32)
    delta = sb("m_delta", [P, ET, T], F32)
    delta_u = sb("m_delta_u", [P, ET, T], F32)
    d_u = sb("m_d_u", [P, ET, T], F32)
    m_banks = [psum(f"m_bank{b}", [P, 512], F32) for b in range(4)]
    m_ring = Ring(core.sems("m_full", 4), core.sems("m_free", 4),
                  [("x", et) for et in range(ET)] + [("dbl",)] + [("dt", et) for et in range(ET)])
    zeroed = core.sem("m_zeroed")
    conv_step = core.sem("m_conv_step")
    u_ready = core.sem("m_u_ready")
    neg_abs = core.sem("m_neg_abs")
    e_ready = core.sem("m_e_ready")
    one_e_ready = core.sem("m_one_e_ready")
    log_ready = core.sem("m_log_ready")
    log_step = core.sem("m_log_step")
    delta_ready = core.sem("m_delta_ready")
    d_u_ready = core.sem("m_d_u")
    products = core.sem("m_products")

    factor = sb("r_factor", [P, 2, KD, D], F32)
    factor_sum = sb("r_factor_sum", [P, KD, D], F32)
    factor_in = core.sems("r_factor_in", 2)
    factor_added = core.sem("r_factor_added")
    PER_PASS = RANK // B
    assert PER_PASS == 2

    with nc.Block() as block:
        @block.sync
        def _(sp):
            ctx = dram["ctx_t"].rearrange("b (k p) t -> p b k t", p=P)
            sp.dma_start(ctx_t[:, 0], ctx[:, 0]).then_inc(w_in, 16)
            sp.dma_start(wq[:], dram["x_wq_t"].rearrange("(k p) o -> p k o", p=P)).then_inc(w_in, 16)
            sp.dma_start(wk[:], dram["x_wk_t"].rearrange("(k p) o -> p k o", p=P)).then_inc(w_in, 16)
            sp.dma_start(bq[:], dram["x_bq"].rearrange("(p o) -> p o", o=1)).then_inc(w_in, 16)
            sp.dma_start(bk[:], dram["x_bk"].rearrange("(p o) -> p o", o=1)).then_inc(w_in, 16)
            sp.dma_start(w_in_t[:], dram["m_in_t"].rearrange("(k p) e -> p k e", p=P)).then_inc(w_in, 16)
            sp.dma_start(w_x[:], dram["m_x_t"].rearrange("(k p) o -> p k o", p=P)).then_inc(w_rest_in, 16)
            sp.dma_start(w_dt[:], dram["m_dt_t"]).then_inc(w_rest_in, 16)
            sp.dma_start(cols[:], dram["m_cols"].rearrange("(k p) o -> p k o", p=P)).then_inc(w_rest_in, 16)
            sp.dma_start(ctx_t[:, 1:], ctx[:, 1:]).then_inc(w_rest_in, 16)
            with sp.Fori(0, B) as i:
                for s in range(2):
                    sp.wait_ge(factor_added, i * PER_PASS + max(s, 1))
                    sp.dma_start(factor[:, s], dram["factors"][i * PER_PASS + s]
                                 .rearrange("(k p) e -> p k e", p=P)).then_inc(factor_in[s], 16)
                b, turn = m_ring.at(("dbl",), i)
                sp.wait_ge(m_ring.free[b], turn + 1)
                sp.dma_start(scratch["bc"][i], dbl[DR:DR + 2 * DS, :]).then_inc(stored, 16)
                for ready, count, name, tile in ((d_u_ready, (i + 1) * ET, "y", d_u),
                                                 (delta_ready, (i + 1) * ET, "delta", delta),
                                                 (products, (i + 1) * ET + 1, "delta_u", delta_u)):
                    sp.wait_ge(ready, count)
                    sp.dma_start(scratch[name][i], tile[:]).then_inc(stored, 16)
            sp.wait_ge(factor_added, RANK + 1)
            sp.dma_start(scratch["factor_sum"], factor_sum[:]).then_inc(stored, 16)
            sp.wait_ge(stored, B * STORES + 16 + 1)

        @block.tensor
        def _(pe):
            start_at_one(pe, *ring.free, conv_step, products, u_ready, stored, *m_ring.free)

            def context_features(i, ets):
                for et in ets:
                    b, turn = m_ring.at(("x", et), i)
                    pe.wait_ge(m_ring.free[b], turn)
                    for k in range(KC):
                        mm = nc.tensor.matmul(m_banks[b][:], w_in_t[:, k, et * P:(et + 1) * P], ctx_t[:, i, k, :],
                                              start=(k == 0), stop=(k == KC - 1))
                    mm.then_inc(m_ring.full[b], 1)

            def weigh(i, tt):
                ring.wait_free(pe, i, ("out", tt), consumed=xn_steps + turn_steps if tt == 0 else ())
                b, _ = ring.at(("out", tt), i)
                for n in range(TT):
                    mm = nc.tensor.matmul(banks[b][:], xn_t[:, n, tt * P:(tt + 1) * P], att_t[:, n, :],
                                          start=(n == 0), stop=(n == TT - 1))
                mm.then_inc(ring.full[b], 1)

            pe.wait_ge(w_in, 16 * 6)
            with pe.Fori(0, B) as i:
                for step, w in ((("q",), wq), (("k",), wk)):
                    b, turn = ring.at(step, i)
                    pe.wait_ge(ring.free[b], turn)
                    for k in range(KC):
                        mm = nc.tensor.matmul(banks[b][:], w[:, k, :], ctx_t[:, i, k, :],
                                              start=(k == 0), stop=(k == KC - 1))
                    mm.then_inc(ring.full[b], 1)
                context_features(i, (0, 1))
                ring.wait_free(pe, i, consumed=[("q",), ("k",)])
                for m in range(TT):
                    b, turn = ring.at(("energy", m), i)
                    pe.wait_ge(ring.free[b], turn)
                    nc.tensor.matmul(banks[b][:], q_t[:, m * P:(m + 1) * P], k_t[:],
                                     start=True, stop=True).then_inc(ring.full[b], 1)
                context_features(i, (2, 3))
                norm_tensor(nc, pe, norm, consts.ident, ring, banks, i)
                pe.wait_ge(att_ready, (i + 1) * TT)
                for n in range(TT):
                    b, turn = ring.at(("turn", n), i)
                    pe.wait_ge(ring.free[b], turn)
                    for m in range(TT):
                        mm = nc.tensor.transpose(banks[b][:, m * P:(m + 1) * P],
                                                 att[:, m, n * P:(n + 1) * P], consts.ident[:])
                    mm.then_inc(ring.full[b], 1)
                weigh(i, 0)
                pe.wait_ge(w_rest_in, 16 * 4)
                pe.wait_ge(u_ready, (i + 1) * ET + 1)
                b, turn = m_ring.at(("dbl",), i)
                pe.wait_ge(m_ring.free[b], turn)
                for et in range(ET):
                    mm = nc.tensor.matmul(m_banks[b][0:DR + 2 * DS, :], w_x[:, et, :], u[:, et, :],
                                          start=(et == 0), stop=(et == ET - 1))
                mm.then_inc(m_ring.full[b], 1)
                weigh(i, 1)
                pe.wait_ge(m_ring.free[b], turn + 1)
                for et in range(ET):
                    b, turn = m_ring.at(("dt", et), i)
                    pe.wait_ge(m_ring.free[b], turn)
                    nc.tensor.matmul(m_banks[b][:], w_dt[:, et * P:(et + 1) * P], dbl[0:DR, :],
                                     start=True, stop=True).then_inc(m_ring.full[b], 1)
                weigh(i, 2)
                weigh(i, 3)

        @block.scalar
        def _(act):
            def pad(i, ets):
                for et in ets:
                    b, turn = m_ring.at(("x", et), i)
                    act.wait_ge(m_ring.full[b], turn)
                    act.wait_ge(conv_step, i * (ET * DC) + 1)
                    nc.scalar.copy(padded[:, et, DC - 1:], m_banks[b][:]).then_inc(m_ring.free[b], 1)

            act.wait_ge(w_in, 16 * 6)
            with act.Fori(0, B) as i:
                for step, bias, out in ((("q",), bq, q_t), (("k",), bk, k_t)):
                    b, turn = ring.at(step, i)
                    act.wait_ge(ring.full[b], turn)
                    nc.scalar.activation(out[:], banks[b][:], ACT.Identity, bias=bias[:]) \
                        .then_inc(ring.free[b], 1)
                pad(i, (0, 1))
                for m in range(TT):
                    act.wait_ge(neg_ready, i * TT + m + 1)
                    b, turn = ring.at(("energy", m), i)
                    nc.scalar.activation(att[:, m, :], banks[b][:], ACT.Exp, bias=neg_m[:, m:m + 1],
                                         accum_out=sums[:, m:m + 1]).then_inc(ring.free[b], 1)
                pad(i, (2, 3))
                for step, out in [(("xn", k), xn_t[:, k, :]) for k in (1, 3)] + \
                        [(("turn", n), att_t[:, n, :]) for n in range(TT)]:
                    b, turn = ring.at(step, i)
                    act.wait_ge(ring.full[b], turn)
                    nc.scalar.copy(out, banks[b][:]).then_inc(ring.free[b], 1)
                act.wait_ge(w_rest_in, 16 * 4)
                act.wait_ge(products, i * ET + 1)
                for et in range(ET):
                    act.wait_ge(conv_step, i * (ET * DC) + (DC - 1) * ET + et + 2)
                    nc.scalar.activation(u[:, et, :], conv[:, et, :], ACT.Silu, bias=cols[:, et, DC:DC + 1]) \
                        .then_inc(u_ready, 1)
                for et in range(ET):
                    act.wait_ge(neg_abs, i * ET + et + 1)
                    nc.scalar.activation(e[:, et, :], e[:, et, :], ACT.Exp).then_inc(e_ready, 1)
                for et in range(ET):
                    act.wait_ge(one_e_ready, i * ET + et + 1)
                    nc.scalar.activation(log1p[:, et, :], one_e[:, et, :], ACT.Ln).then_inc(log_ready, 1)

        @block.vector
        def _(dve):
            def add(i, tts):
                for tt in tts:
                    b, turn = ring.at(("out", tt), i)
                    dve.wait_ge(ring.full[b], turn)
                    nc.vector.tensor_tensor(x[:, i, tt, :], banks[b][:], x[:, i, tt, :], ALU.add) \
                        .then_inc(ring.free[b], 1)

            nc.vector.memset(padded[:, :, 0:DC - 1], 0.0).then_inc(zeroed, 1)
            dve.wait_ge(zeroed, 1)
            norm_vector(nc, dve, norm, x, 0)

            def one_pass(i, more):
                for m in range(TT):
                    b, turn = ring.at(("energy", m), i)
                    dve.wait_ge(ring.full[b], turn)
                    nc.vector.tensor_reduce(mx[:, m:m + 1], banks[b][:], AX_X, ALU.max).then_inc(max_done, 1)
                    dve.wait_ge(max_done, i * TT + m + 1)
                    nc.vector.tensor_scalar(neg_m[:, m:m + 1], mx[:, m:m + 1], -1.0, None, ALU.mult) \
                        .then_inc(neg_ready, 1)
                for m in range(TT):
                    b, turn = ring.at(("energy", m), i)
                    dve.wait_ge(ring.free[b], turn + 1)
                    nc.vector.reciprocal(rsum[:, m:m + 1], sums[:, m:m + 1]).then_inc(rsum_ready, 1)
                dve.wait_ge(w_rest_in, 16 * 4)
                dve.wait_ge(u_ready, i * ET + 1)
                for tap in range(DC):
                    for et in range(ET):
                        src = padded[:, et, tap:tap + T]
                        if tap == 0:
                            b, turn = m_ring.at(("x", et), i)
                            dve.wait_ge(m_ring.free[b], turn + 1)
                            ins = nc.vector.tensor_scalar(conv[:, et, :], src, cols[:, et, 0:1], None, ALU.mult)
                        else:
                            dve.wait_ge(conv_step, i * (ET * DC) + (tap - 1) * ET + et + 2)
                            ins = nc.vector.scalar_tensor_tensor(
                                out=conv[:, et, :], in0=src, scalar=cols[:, et, tap:tap + 1],
                                in1=conv[:, et, :], op0=ALU.mult, op1=ALU.add)
                        ins.then_inc(conv_step, 1)
                    if tap == 0:
                        for k in (0, 2):
                            b, turn = ring.at(("xn", k), i)
                            dve.wait_ge(ring.full[b], turn)
                            nc.vector.tensor_copy(xn_t[:, k, :], banks[b][:]).then_inc(ring.free[b], 1)
                b, turn = m_ring.at(("dbl",), i)
                dve.wait_ge(m_ring.full[b], turn)
                dve.wait_ge(stored, i * STORES + 1)
                nc.vector.tensor_copy(dbl[:], m_banks[b][0:DR + 2 * DS, :]).then_inc(m_ring.free[b], 1)
                add(i, (0,))
                for et in range(ET):
                    b, turn = m_ring.at(("dt", et), i)
                    dve.wait_ge(m_ring.full[b], turn)
                    nc.vector.tensor_scalar(dt[:, et, :], m_banks[b][:], cols[:, et, DC + 1:DC + 2], None, ALU.add) \
                        .then_inc(m_ring.free[b], 1)
                for et in range(ET):
                    b, turn = m_ring.at(("dt", et), i)
                    dve.wait_ge(m_ring.free[b], turn + 1)
                    nc.vector.scalar_tensor_tensor(out=e[:, et, :], in0=dt[:, et, :], scalar=-1.0, in1=dt[:, et, :],
                                                   op0=ALU.mult, op1=ALU.min).then_inc(neg_abs, 1)
                add(i, (1, 2, 3))
                if more:
                    norm_vector(nc, dve, norm, x, i + 1)
                for et in range(ET):
                    dve.wait_ge(log_ready, i * ET + et + 1)
                    nc.vector.scalar_tensor_tensor(out=e[:, et, :], in0=one_e[:, et, :], scalar=1.0, in1=e[:, et, :],
                                                   op0=ALU.subtract, op1=ALU.subtract).then_inc(log_step, 1)
                for et in range(ET):
                    dve.wait_ge(log_step, i * (2 * ET) + et + 1)
                    nc.vector.tensor_tensor(log1p[:, et, :], log1p[:, et, :], e[:, et, :], ALU.subtract) \
                        .then_inc(log_step, 1)
                for et in range(ET):
                    dve.wait_ge(log_step, i * (2 * ET) + ET + et + 1)
                    nc.vector.scalar_tensor_tensor(out=delta[:, et, :], in0=dt[:, et, :], scalar=0.0,
                                                   in1=log1p[:, et, :], op0=ALU.max, op1=ALU.add) \
                        .then_inc(delta_ready, 1)

            passes(dve, one_pass)

        @block.gpsimd
        def _(pool):
            def one_pass(i, more):
                for m in range(TT):
                    wait_apart(pool, rsum_ready, i * TT + m + 1, waited)
                    nc.gpsimd.tensor_scalar(att[:, m, :], att[:, m, :], rsum[:, m:m + 1], 1.0,
                                            ALU.mult, ALU.mult).then_inc(att_ready, 1)
                for s in range(2):
                    pool.wait_ge(factor_in[s], i * 16 + 16)
                    pool.wait_ge(factor_added, i * PER_PASS + s + 1)
                    nc.gpsimd.tensor_tensor(factor_sum[:], factor_sum[:], factor[:, s], ALU.add) \
                        .then_inc(factor_added, 1)
                wait_apart(pool, stored, i * STORES + 1, waited)
                for et in range(ET):
                    wait_apart(pool, u_ready, i * ET + et + 2, waited)
                    nc.gpsimd.tensor_scalar(d_u[:, et, :], u[:, et, :], cols[:, et, DC + 2:DC + 3], 1.0,
                                            ALU.mult, ALU.mult).then_inc(d_u_ready, 1)
                for et in range(ET):
                    wait_apart(pool, e_ready, i * ET + et + 1, waited)
                    nc.gpsimd.tensor_scalar(one_e[:, et, :], e[:, et, :], 1.0, 1.0, ALU.mult, ALU.add) \
                        .then_inc(one_e_ready, 1)
                if more:
                    norm_gpsimd(nc, pool, norm, consts.minus_half, i + 1)
                for et in range(ET):
                    pool.wait_ge(delta_ready, i * ET + et + 1)
                    nc.gpsimd.tensor_tensor(delta_u[:, et, :], delta[:, et, :], u[:, et, :], ALU.mult) \
                        .then_inc(products, 1)

            norm_gpsimd(nc, pool, norm, consts.minus_half, 0)
            nc.gpsimd.memset(factor_sum[:], 0.0).then_inc(factor_added, 1)
            pool.wait_ge(w_rest_in, 16 * 4)
            passes(pool, one_pass)


class Scan:
    QUADS = DS // NQ
    PER_QUAD = ET * NQ // NS
    CHUNKS = QUADS * PER_QUAD
    POSITIONS = CHUNKS + 6
    SLOTS = 4

    def __init__(self, core, sb, psum, dram, scratch, consts):
        self.nc, self.dram, self.scratch, self.consts = core.nc, dram, scratch, consts
        self.a = sb("s_a", [P, ET, DS], F32)
        self.delta = sb("s_delta", [P, ET, T], F32)
        self.delta_u = sb("s_delta_u", [P, ET, T], F32)
        self.y = sb("s_y", [P, ET, T], F32)
        self.bc = sb("s_bc", [P, 2, 2, NQ, T], F32)
        self.decay = sb("s_decay", [P, 2, NS, T], F32)
        self.state = sb("s_state", [P, self.SLOTS, NS, T], F32)
        self.pair = sb("s_pair", [P, self.SLOTS, T], F32)
        self.banks = [psum(f"s_bank{b}", [P, 512], F32) for b in range(2)]
        self.a_in = core.sem("s_a_in")
        self.a_step = core.sem("s_a_step")
        self.seq_in = core.sem("s_seq_in")
        self.y_in = core.sem("s_y_in")
        self.bc_in = core.sems("s_bc_in", 2)
        self.decay_ready = core.sems("s_decay", self.SLOTS)
        self.input_ready = core.sems("s_input", self.SLOTS)
        self.scanned = core.sems("s_scanned", self.SLOTS)
        self.weighed = core.sems("s_weighed", self.SLOTS)
        self.paired = core.sems("s_paired", self.SLOTS)
        self.summed = core.sems("s_summed", self.SLOTS)
        self.added = core.sems("s_added", 2)
        self.stored = core.sem("s_stored")

    def wait(self, eng, sems, i, c):
        eng.wait_ge(sems[c % self.SLOTS], i * (self.CHUNKS // self.SLOTS) + c // self.SLOTS + 2)

    def wait_added(self, eng, i, c):
        n = c // 2
        eng.wait_ge(self.added[n % 2], i * (self.CHUNKS // 4) + n // 2 + 2)

    def wait_bc(self, eng, i, q):
        eng.wait_ge(self.bc_in[q % 2], i * (self.QUADS // 2 * 32) + (q // 2 + 1) * 32)

    def place(self, c):
        return c // self.PER_QUAD, c % self.PER_QUAD * NS // NQ, c * NS % NQ

    def load_a(self, sp):
        sp.dma_start(self.a[:], self.dram["m_a_log"].rearrange("(k p) n -> p k n", p=P)).then_inc(self.a_in, 16)

    def sync(self, sp, i):
        scratch = self.scratch
        for c in range(-self.SLOTS, 0):
            self.wait(sp, self.weighed, i, c)
        sp.dma_start(self.delta[:], scratch["delta"][i]).then_inc(self.seq_in, 16)
        sp.dma_start(self.delta_u[:], scratch["delta_u"][i]).then_inc(self.seq_in, 16)
        for q in range(self.QUADS):
            if q == 2:
                sp.wait_ge(self.stored, i * 16 + 1)
                sp.dma_start(self.y[:], scratch["y"][i]).then_inc(self.y_in, 16)
            for c in range(self.SLOTS if q else 0):
                self.wait(sp, self.weighed, i, (q - 1) * self.PER_QUAD - 1 - c)
            for n in range(2):
                rows = scratch["bc"][i, n * DS + q * NQ:n * DS + (q + 1) * NQ, :]
                sp.dma_start(self.bc[:, q % 2, n], rows.rearrange("(o n) t -> o n t", o=1)
                             .broadcast_to([P, NQ, T])).then_inc(self.bc_in[q % 2], 16)
        for c in (-1, -3):
            self.wait_added(sp, i + 1, c)
        sp.dma_start(scratch["y"][i], self.y[:]).then_inc(self.stored, 16)

    def sync_end(self, sp):
        sp.wait_ge(self.stored, B * 16 + 1)

    def tensor_setup(self, pe):
        start_at_one(pe, self.stored, *self.scanned, *self.weighed, *self.paired, *self.summed, *self.added)

    def tensor(self, i, p):
        pe, nc, c = self.nc.tensor, self.nc, p - 4
        if not 0 <= c < self.CHUNKS:
            return
        self.wait(pe, self.paired, i, c)
        if c % 2 == 0:
            self.wait_added(pe, i, c - 4)
        nc.tensor.matmul(self.banks[c // 2 % 2][:], self.consts.ident[:], self.pair[:, c % self.SLOTS, :],
                         start=(c % 2 == 0), stop=(c % 2 == 1)).then_inc(self.summed[c % self.SLOTS], 1)

    def scalar_setup(self, act):
        act.wait_ge(self.a_in, 16)
        self.nc.scalar.activation(self.a[:], self.a[:], ACT.Exp).then_inc(self.a_step, 1)
        act.wait_ge(self.a_step, 3)

    def scalar(self, i, p):
        act, c = self.nc.scalar, p
        if c >= self.CHUNKS:
            return
        if c == 0:
            act.wait_ge(self.seq_in, i * 32 + 32)
        self.wait(act, self.scanned, i, c - 2)
        q, et, n = self.place(c)
        for u in range(NS):
            st = q * NQ + n + u
            ins = self.nc.scalar.activation(self.decay[:, c % 2, u, 1:], self.delta[:, et, 1:], ACT.Exp,
                                            scale=self.a[:, et, st:st + 1])
        ins.then_inc(self.decay_ready[c % self.SLOTS], 1)

    def gpsimd(self, i, p):
        pool, s = self.nc.gpsimd, p % self.SLOTS
        if p < self.CHUNKS:
            q, et, n = self.place(p)
            if p == 0:
                pool.wait_ge(self.seq_in, i * 32 + 32)
            if p % self.PER_QUAD == 0:
                self.wait_bc(pool, i, q)
            self.wait(pool, self.paired, i, p - self.SLOTS)
            pool.tensor_tensor(self.state[:, s], self.bc[:, q % 2, 0, n:n + NS],
                               self.delta_u[:, et, :].rearrange("p (o t) -> p o t", o=1)
                               .broadcast_to([P, NS, T]), ALU.mult).then_inc(self.input_ready[s], 1)
        c = p - 2
        if 0 <= c < self.CHUNKS:
            s = c % self.SLOTS
            self.wait(pool, self.weighed, i, c)
            self.wait(pool, self.summed, i, c - self.SLOTS)
            pool.tensor_tensor(self.pair[:, s, :], self.state[:, s, 0, :], self.state[:, s, 1, :], ALU.add) \
                .then_inc(self.paired[s], 1)

    def vector_setup(self, dve):
        self.nc.vector.memset(self.decay[:, :, :, 0:1], 0.0).then_inc(self.a_step, 1)
        dve.wait_ge(self.a_step, 2)
        self.nc.vector.tensor_scalar(self.a[:], self.a[:], -1.0, None, ALU.mult).then_inc(self.a_step, 1)

    def vector(self, i, p):
        dve = self.nc.vector
        if p < self.CHUNKS:
            s = p % self.SLOTS
            dve.wait_ge(self.decay_ready[s], i * (self.CHUNKS // self.SLOTS) + p // self.SLOTS + 1)
            dve.wait_ge(self.input_ready[s], i * (self.CHUNKS // self.SLOTS) + p // self.SLOTS + 1)
            flat = self.state[:, s].rearrange("p n t -> p (n t)")
            dve.tensor_tensor_scan(flat, self.decay[:, p % 2].rearrange("p n t -> p (n t)"), flat,
                                   0.0, ALU.mult, ALU.add).then_inc(self.scanned[s], 1)
        c = p - 1
        if 0 <= c < self.CHUNKS:
            s = c % self.SLOTS
            q, et, n = self.place(c)
            self.wait(dve, self.scanned, i, c)
            if c % self.PER_QUAD == 0:
                self.wait_bc(dve, i, q)
            dve.tensor_tensor(self.state[:, s], self.state[:, s], self.bc[:, q % 2, 1, n:n + NS], ALU.mult) \
                .then_inc(self.weighed[s], 1)
        c = p - 6
        if c >= 0 and c % 2 == 1:
            q, et, _ = self.place(c)
            if c == 1:
                dve.wait_ge(self.y_in, i * 16 + 16)
            self.wait(dve, self.summed, i, c)
            if q > 0:
                self.wait_added(dve, i, c - self.PER_QUAD)
            dve.tensor_tensor(self.y[:, et, :], self.banks[c // 2 % 2][:], self.y[:, et, :], ALU.add) \
                .then_inc(self.added[c // 2 % 2], 1)


def stage_ffn(core, sb, psum, dram, x, consts, scratch):
    nc = core.nc
    weights = sb("c_weights", [P, W_ALL], F32)
    weights_in = core.sems("c_weights_in", OT)
    norm = Norm(core, sb, "c")
    xn_t = sb("c_xn_t", [P, KD, T], F32)
    h_t = sb("c_h_t", [P, 2, T], F32)
    scan = Scan(core, sb, psum, dram, scratch, consts)
    NB = 2
    banks = [psum(f"c_bank{b}", [P, 512], F32) for b in range(NB)]
    out = [psum(f"c_out{tt}", [P, 512], F32) for tt in range(TT)]
    order = [("xn", k) for k in range(KD)]
    for o in range(OT):
        order += [("gate", o), ("up", o)]
    ring = Ring(core.sems("c_full", NB), core.sems("c_free", NB), order)
    h_used = core.sem("c_h_used")
    out_full = core.sem("c_out_full")
    out_free = core.sem("c_out_free")
    width = [min(P, INTER - o * P) for o in range(OT)]
    NORM_AT = 9
    share = lambda o: min(max(o - 1, 0), OT - 2) * scan.POSITIONS // (OT - 2)
    positions = [list(range(share(o), share(o + 1))) for o in range(OT)]

    EARLY = 2

    def load_weights(eng, o):
        def columns(a):
            return a[:, 0:W_DOWN].rearrange("p (k o) -> p k o", o=INTER)[:, :, o * P:o * P + width[o]]
        down = slice(W_DOWN + o * D, W_DOWN + (o + 1) * D)
        eng.dma_start(columns(weights).bitcast(I32), columns(scratch["weights"])).then_inc(weights_in[o], 16)
        eng.dma_start(weights[:, down].bitcast(I32), scratch["weights"][:, down]).then_inc(weights_in[o], 16)

    with nc.Block() as block:
        @block.sync
        def _(sp):
            for o in range(EARLY):
                load_weights(sp, o)
            scan.load_a(sp)
            with sp.Fori(0, B) as i:
                scan.sync(sp, i)
            scan.sync_end(sp)

        @block.tensor
        def _(pe):
            start_at_one(pe, out_free, h_used, *ring.free)
            scan.tensor_setup(pe)

            def down(i, o):
                b, turn = ring.at(("up", o), i)
                pe.wait_ge(ring.free[b], turn + 1)
                if o == 0:
                    pe.wait_ge(out_free, i * TT + 1)
                for tt in range(TT):
                    mm = nc.tensor.matmul(out[tt][:], h_t[0:width[o], o % 2, tt * P:(tt + 1) * P],
                                          weights[0:width[o], W_DOWN + o * D:W_DOWN + (o + 1) * D],
                                          start=(o == 0), stop=(o == OT - 1))
                mm.then_inc(h_used if o < OT - 1 else out_full, 1)

            def one_pass(i, more):
                ring.wait_free(pe, i, consumed=[("xn", k) for k in range(KD)])
                for o in range(OT):
                    at = positions[o]
                    pe.wait_ge(weights_in[o], 16 * 2)
                    for n, (kind, base) in enumerate((("gate", 0), ("up", W_UP))):
                        b, turn = ring.at((kind, o), i)
                        pe.wait_ge(ring.free[b], turn)
                        for k in range(KD):
                            lo = base + k * INTER + o * P
                            mm = nc.tensor.matmul(banks[b][0:width[o], :], weights[:, lo:lo + width[o]],
                                                  xn_t[:, k, :], start=(k == 0), stop=(k == KD - 1))
                        mm.then_inc(ring.full[b], 1)
                        if at:
                            scan.tensor(i, at[n])
                    if o == OT - 1 and more:
                        norm_tensor(nc, pe, norm, consts.ident, ring, banks, i + 1, tiles=(0, 1))
                    if o:
                        down(i, o - 1)
                    if o == OT - 1 and more:
                        norm_tensor(nc, pe, norm, consts.ident, ring, banks, i + 1, tiles=(2, 3))
                    for p in at[2:]:
                        scan.tensor(i, p)
                down(i, OT - 1)

            norm_tensor(nc, pe, norm, consts.ident, ring, banks, 0)
            passes(pe, one_pass)

        @block.scalar
        def _(act):
            def evacuate(i):
                for k in (1, 3):
                    b, turn = ring.at(("xn", k), i)
                    act.wait_ge(ring.full[b], turn)
                    nc.scalar.copy(xn_t[:, k, :], banks[b][:]).then_inc(ring.free[b], 1)

            def one_pass(i, more):
                for o in range(OT):
                    if o == 1:
                        act.wait_ge(h_used, i * (OT - 1) + 1)
                    elif o == 0:
                        act.wait_ge(out_free, i * TT + 1)
                    else:
                        act.wait_ge(h_used, i * (OT - 1) + o)
                    for p in positions[o][:2]:
                        scan.scalar(i, p)
                    b, turn = ring.at(("gate", o), i)
                    act.wait_ge(ring.full[b], turn)
                    nc.scalar.activation(h_t[0:width[o], o % 2, :], banks[b][0:width[o], :], ACT.Silu) \
                        .then_inc(ring.free[b], 1)
                    for p in positions[o][2:]:
                        scan.scalar(i, p)
                if more:
                    evacuate(i + 1)

            evacuate(0)
            for o in range(EARLY, OT):
                load_weights(act, o)
            scan.scalar_setup(act)
            passes(act, one_pass)

        @block.vector
        def _(dve):
            def evacuate(i):
                for k in (0, 2):
                    b, turn = ring.at(("xn", k), i)
                    dve.wait_ge(ring.full[b], turn)
                    nc.vector.tensor_copy(xn_t[:, k, :], banks[b][:]).then_inc(ring.free[b], 1)

            def one_pass(i, more):
                for o in range(OT):
                    for p in positions[o][:2]:
                        scan.vector(i, p)
                    b, turn = ring.at(("gate", o), i)
                    dve.wait_ge(ring.free[b], turn + 1)
                    b, turn = ring.at(("up", o), i)
                    dve.wait_ge(ring.full[b], turn)
                    nc.vector.tensor_tensor(h_t[0:width[o], o % 2, :], banks[b][0:width[o], :],
                                            h_t[0:width[o], o % 2, :], ALU.mult).then_inc(ring.free[b], 1)
                    for p in positions[o][2:]:
                        scan.vector(i, p)
                    if o == NORM_AT and more:
                        norm_vector(nc, dve, norm, x, i + 1)
                if more:
                    evacuate(i + 1)
                dve.wait_ge(out_full, i + 1)
                for tt in range(TT):
                    nc.vector.tensor_tensor(x[:, i, tt, :], out[tt][:], x[:, i, tt, :], ALU.add) \
                        .then_inc(out_free, 1)

            norm_vector(nc, dve, norm, x, 0)
            evacuate(0)
            scan.vector_setup(dve)
            passes(dve, one_pass)

        @block.gpsimd
        def _(pool):
            def one_pass(i, more):
                for o in range(OT):
                    for p in positions[o]:
                        scan.gpsimd(i, p)
                    if o == NORM_AT and more:
                        norm_gpsimd(nc, pool, norm, consts.minus_half, i + 1)

            norm_gpsimd(nc, pool, norm, consts.minus_half, 0)
            passes(pool, one_pass)


def stage_diff_attention(core, sb, psum, dram, x, consts, scratch):
    nc = core.nc
    E2 = 2 * DHD
    HG = P // E2
    GROUPS = DH // HG
    VD = D // DH
    w = sb("d_w", [P, KD, 3 * D], F32)
    wp = sb("d_wp", [P, KD, D], F32)
    lam_v = sb("d_lam_v", [P, 4, D], F32)
    lam_s = sb("d_lam_s", [P, 6], F32)
    rowsel = sb("d_rowsel", [P, 2], F32)
    coef = sb("d_coef", [P, 1], F32)
    norm = Norm(core, sb, "d")
    xn_t = sb("d_xn_t", [P, KD, T], F32)
    hi = sb("d_hi", [P, 2, T], F32R)
    lo = sb("d_lo", [P, 2, T], F32R)
    qs = sb("d_qs", [P, DH, T], F32R)
    ks = sb("d_ks", [P, DH, T], F32R)
    v = sb("d_v", [P, TT, D], F32)
    mx = sb("d_mx", [P, GROUPS, HG, TT], F32)
    neg_t = sb("d_neg_t", [HG * TT, P], F32R)
    prob_t = sb("d_prob_t", [P, 2, HG, T], F32)
    rsum = sb("d_rsum", [P, T], F32)
    out_t = sb("d_out_t", [P, GROUPS, T], F32)

    banks = [psum(f"d_bank{b}", [P, 512], F32) for b in range(4)]
    score = [psum(f"d_score{s}", [P, T], F32) for s in range(2)]
    acc = psum("d_acc", [P, T], F32)
    acc_sum = psum("d_acc_sum", [P, T], F32)
    ROWS = HG * TT
    ROWS_AT = ((0, 2), (2, 7), (7, 11), (11, 16))
    xn_steps = [("xn", k) for k in range(KD)]
    v_steps = [("v", tt) for tt in range(TT)]
    rows_steps = lambda g, a, z: [("row", g, m) for m in range(a, z)]

    def steps(more):
        order = []
        for g in range(GROUPS):
            rg, pg = (g + 1) % GROUPS, (g + 2) % GROUPS
            rows_on, proj_on = more or g + 1 < GROUPS, more or g + 2 < GROUPS
            for half in range(4):
                order += rows_steps(rg, *ROWS_AT[half]) if rows_on else []
                if half in (0, 2) and proj_on:
                    order += [("q" if half == 0 else "k", pg)]
            order += [("neg", rg)] if rows_on else []
            order += xn_steps if g == 1 and more else []
        return order + (v_steps if more else []) + [("out", tt) for tt in range(TT)]

    ring = Ring(core.sems("d_full", 4), core.sems("d_free", 4), steps(True), steps(False))
    first = Ring(core.sems("d_first_full", 4), core.sems("d_first_free", 4),
                 xn_steps + [("q", 0), ("k", 0), ("q", 1), ("k", 1)] + v_steps
                 + rows_steps(0, 0, ROWS) + [("neg", 0)])
    w_in = core.sems("d_in_w", 4)
    lam_in = core.sem("d_in_lam")
    lam_step = core.sem("d_lam_step")
    waited = core.sem("d_waited")
    hi_done = core.sem("d_hi_done")
    stacked = core.sems("d_stacked", 2)
    max_in = core.sem("d_max_in")
    prob_used = core.sem("d_prob_used")
    score_full = core.sems("d_score_full", 2)
    exp_done = core.sems("d_exp_done", 2)
    acc_full = core.sem("d_acc_full")
    rsum_done = core.sem("d_rsum_done")
    acc_free = core.sem("d_acc_free")
    COPIES = 3 * HG * 16
    FILLS = HG // 2 * TT

    with nc.Block() as block:
        @block.sync
        def _(sp):
            for n, name in enumerate(("lq1", "lk1", "lq2", "lk2")):
                sp.dma_start(lam_v[:, n, :], dram[name].rearrange("(o l) -> o l", o=1).broadcast_to([P, D])) \
                    .then_inc(lam_in, 16)
            sp.dma_start(rowsel[:], dram["rowsel"]).then_inc(lam_in, 16)
            for n in range(3):
                part = slice(n * D, (n + 1) * D)
                sp.dma_start(w[:, :, part], dram["d_w"].rearrange("(k p) o -> p k o", p=P)[:, :, part]) \
                    .then_inc(w_in[n], 16)
            sp.dma_start(wp[:], dram["d_wp"].rearrange("(k p) o -> p k o", p=P)).then_inc(w_in[3], 16)

            def stack(ring, in_pass, g):
                for n, (rows, parts) in enumerate(((qs, (hi, lo, hi)), (ks, (hi, hi, lo)))):
                    b, turn = ring.at(("qk"[n], g), in_pass)
                    sp.wait_ge(ring.free[b], turn + 1)
                    for block_, part in enumerate(parts):
                        for j in range(HG):
                            sp.dma_start(rows[block_ * E2:(block_ + 1) * E2, g * HG + j, :].bitcast(F32),
                                         part[j * E2:(j + 1) * E2, n, :].bitcast(F32)) \
                                .then_inc(stacked[n], 16)

            def one_pass(i, more):
                for g in range(GROUPS):
                    if more or g + 2 < GROUPS:
                        stack(ring, i, (g + 2) % GROUPS)

            for g in range(2):
                stack(first, 0, g)
            passes(sp, one_pass)

        @block.tensor
        def _(pe):
            start_at_one(pe, *exp_done, acc_free, *stacked, prob_used, acc_full, *ring.free, *first.free)

            def project(ring, in_pass, kind, g):
                b, turn = ring.at((kind, g), in_pass)
                pe.wait_ge(ring.free[b], turn)
                lo = "qk".index(kind) * D + g * P
                for k in range(KD):
                    mm = nc.tensor.matmul(banks[b][:], w[:, k, lo:lo + P], xn_t[:, k, :],
                                          start=(k == 0), stop=(k == KD - 1))
                mm.then_inc(ring.full[b], 1)

            def values(ring, in_pass, tt):
                b, turn = ring.at(("v", tt), in_pass)
                pe.wait_ge(ring.free[b], turn)
                for k in range(KD):
                    mm = nc.tensor.matmul(banks[b][:], xn_t[:, k, tt * P:(tt + 1) * P],
                                          w[:, k, 2 * D:3 * D], start=(k == 0), stop=(k == KD - 1))
                mm.then_inc(ring.full[b], 1)

            def rows(ring, in_pass, g, a, z):
                for m in range(a, z):
                    j, tt = m // TT, m % TT
                    b, turn = ring.at(("row", g, m), in_pass)
                    pe.wait_ge(ring.free[b], turn)
                    nc.tensor.matmul(banks[b][:], qs[0:3 * E2, g * HG + j, tt * P:(tt + 1) * P],
                                     ks[0:3 * E2, g * HG + j, :], start=True, stop=True) \
                        .then_inc(ring.full[b], 1)

            def negate(ring, in_pass, g):
                ring.wait_free(pe, in_pass, ("neg", g),
                               consumed=rows_steps(g, ROWS - TT, ROWS))
                b, _ = ring.at(("neg", g), in_pass)
                nc.tensor.transpose(banks[b][0:HG * TT, 0:P], mx[:, g, :, :].rearrange("p j t -> p (j t)"),
                                    consts.ident[:]).then_inc(ring.full[b], 1)

            def columns(n, g, st, half):
                if st == 0 and half == 0:
                    pe.wait_ge(max_in, n * 16 + 16)
                for s in range(2):
                    h = g * HG + 2 * half + s
                    pe.wait_ge(exp_done[s], n * FILLS + st * 2 + half + 1)
                    nc.tensor.matmul(score[s][:], ks[0:3 * E2 + 1, h, st * P:(st + 1) * P],
                                     qs[0:3 * E2 + 1, h, :], start=True, stop=True).then_inc(score_full[s], 1)

            def weigh(n, g, st, half):
                if half == 0:
                    if st == 0:
                        pe.wait_ge(acc_free, n + 1)
                    for s in range(2):
                        pe.wait_ge(exp_done[s], n * FILLS + st * 2 + 2 + 1)
                for j in range(HG):
                    h = g * HG + j
                    out = (acc_sum if half else acc)[j * VD:(j + 1) * VD, :]
                    left = consts.ones[:, 0:VD] if half else v[:, st, h * VD:(h + 1) * VD]
                    mm = nc.tensor.matmul(out, left, prob_t[:, st % 2, j, :], start=(st == 0), stop=(st == TT - 1))
                if half:
                    mm.then_inc(prob_used if st < TT - 1 else acc_full, 1)

            def one_pass(i, more):
                for g in range(GROUPS):
                    n = i * GROUPS + g
                    rg, pg = (g + 1) % GROUPS, (g + 2) % GROUPS
                    rows_on, proj_on = more or g + 1 < GROUPS, more or g + 2 < GROUPS
                    if rows_on:
                        for m in range(2):
                            pe.wait_ge(stacked[m], (n + 2) * COPIES + 1)
                    for st in range(TT):
                        if st == 0:
                            columns(n, g, 0, 1)
                        elif st < TT - 1:
                            columns(n, g, st + 1, 0)
                        if st < 2 and rows_on:
                            rows(ring, i, rg, *ROWS_AT[2 * st])
                        if st < 2 and proj_on:
                            project(ring, i, "qk"[st], pg)
                        if st == 0:
                            columns(n, g, 1, 0)
                        weigh(n, g, st, 0)
                        if st < TT - 1:
                            columns(n, g, st + 1, 1)
                        if st < 2 and rows_on:
                            rows(ring, i, rg, *ROWS_AT[2 * st + 1])
                        weigh(n, g, st, 1)
                        if st == 1 and rows_on:
                            negate(ring, i, rg)
                    if g == 1 and more:
                        norm_tensor(nc, pe, norm, consts.ident, ring, banks, i + 1, in_pass=i)
                    if g + 1 < GROUPS:
                        columns(n + 1, g + 1, 0, 0)
                    if g == 1 and more:
                        ring.wait_free(pe, i, consumed=xn_steps)
                for tt in range(TT):
                    if more:
                        values(ring, i, tt)
                        if tt == 1:
                            columns((i + 1) * GROUPS, 0, 0, 0)
                pe.wait_ge(acc_free, (i + 1) * GROUPS + 1)
                for tt in range(TT):
                    b, turn = ring.at(("out", tt), i)
                    pe.wait_ge(ring.free[b], turn)
                    for g in range(GROUPS):
                        mm = nc.tensor.matmul(banks[b][:], out_t[:, g, tt * P:(tt + 1) * P], wp[:, g, :],
                                              start=(g == 0), stop=(g == GROUPS - 1))
                    mm.then_inc(ring.full[b], 1)

            norm_tensor(nc, pe, norm, consts.ident, first, banks, 0)
            first.wait_free(pe, 0, consumed=xn_steps)
            for g in range(2):
                for n, kind in enumerate("qk"):
                    pe.wait_ge(w_in[n], 16)
                    project(first, 0, kind, g)
            for n in (2, 3):
                pe.wait_ge(w_in[n], 16)
            for tt in range(TT):
                values(first, 0, tt)
            for m in range(2):
                pe.wait_ge(stacked[m], COPIES + 1)
            rows(first, 0, 0, 0, ROWS)
            negate(first, 0, 0)
            columns(0, 0, 0, 0)
            first.wait_free(pe, 0, consumed=rows_steps(0, ROWS - TT, ROWS) + [("neg", 0)])
            passes(pe, one_pass)

        @block.scalar
        def _(act):
            def features(ring, in_pass):
                for k in (1, 3):
                    b, turn = ring.at(("xn", k), in_pass)
                    act.wait_ge(ring.full[b], turn)
                    nc.scalar.copy(xn_t[:, k, :], banks[b][:]).then_inc(ring.free[b], 1)

            def values(ring, in_pass, tt):
                b, turn = ring.at(("v", tt), in_pass)
                act.wait_ge(ring.full[b], turn)
                nc.scalar.copy(v[:, tt, :], banks[b][:]).then_inc(ring.free[b], 1)

            def high(ring, in_pass, n, kind, g):
                m = "qk".index(kind)
                act.wait_ge(stacked[m], n * COPIES + 1)
                b, turn = ring.at((kind, g), in_pass)
                act.wait_ge(ring.full[b], turn)
                nc.scalar.activation(hi[:, m, :], banks[b][:], ACT.Copy if m else ACT.Identity,
                                     scale=1.0 if m else coef[:]).then_inc(hi_done, 1)

            def exponentials(n, st, half):
                if half == 0:
                    if st >= 2:
                        act.wait_ge(prob_used, n * (TT - 1) + st - 1 + 1)
                    elif st == 0:
                        act.wait_ge(prob_used, n * (TT - 1) + 1)
                    else:
                        act.wait_ge(acc_full, n + 1)
                for s in range(2):
                    act.wait_ge(score_full[s], n * FILLS + st * 2 + half + 1)
                    nc.scalar.activation(prob_t[:, st % 2, 2 * half + s, :], score[s][:], ACT.Exp) \
                        .then_inc(exp_done[s], 1)

            def one_pass(i, more):
                for g in range(GROUPS):
                    n = i * GROUPS + g
                    proj_on = more or g + 2 < GROUPS
                    exponentials(n, 0, 1)
                    for st in range(TT - 1):
                        if st > 0:
                            exponentials(n, st + 1, 0)
                        if st < 2 and proj_on:
                            high(ring, i, n + 2, "qk"[st], (g + 2) % GROUPS)
                        if st == 0:
                            exponentials(n, 1, 0)
                        exponentials(n, st + 1, 1)
                    if g == 1 and more:
                        features(ring, i)
                    if g + 1 < GROUPS:
                        exponentials(n + 1, 0, 0)
                if more:
                    values(ring, i, 1)
                    exponentials((i + 1) * GROUPS, 0, 0)
                    values(ring, i, 3)

            for n in range(2):
                act.wait_ge(lam_step, 1)
                nc.scalar.activation(lam_s[:, 2 + n:3 + n], lam_s[:, n:n + 1], ACT.Exp).then_inc(lam_step, 1)
            features(first, 0)
            act.wait_ge(lam_step, 6)
            for g in range(2):
                for kind in "qk":
                    high(first, 0, g, kind, g)
            for tt in (1, 3):
                values(first, 0, tt)
            exponentials(0, 0, 0)
            passes(act, one_pass)

        @block.vector
        def _(dve):
            def features(ring, in_pass):
                for k in (0, 2):
                    b, turn = ring.at(("xn", k), in_pass)
                    dve.wait_ge(ring.full[b], turn)
                    nc.vector.tensor_copy(xn_t[:, k, :], banks[b][:]).then_inc(ring.free[b], 1)

            def values(ring, in_pass):
                for tt in (0, 2):
                    b, turn = ring.at(("v", tt), in_pass)
                    dve.wait_ge(ring.full[b], turn)
                    nc.vector.tensor_copy(v[:, tt, :], banks[b][:]).then_inc(ring.free[b], 1)

            def low(ring, in_pass, n, kind, g):
                m = "qk".index(kind)
                dve.wait_ge(hi_done, n * 2 + m + 1)
                dve.wait_ge(stacked[m], n * COPIES + 1)
                b, turn = ring.at((kind, g), in_pass)
                if m == 0:
                    ins = nc.vector.scalar_tensor_tensor(
                        out=lo[:, m, :], in0=banks[b][:], scalar=coef[:], in1=hi[:, m, :].bitcast(F32),
                        op0=ALU.mult, op1=ALU.subtract)
                else:
                    ins = nc.vector.tensor_tensor(lo[:, m, :], banks[b][:], hi[:, m, :].bitcast(F32),
                                                  ALU.subtract)
                ins.then_inc(ring.free[b], 1)

            def maxima(ring, in_pass, g, a, z):
                for m in range(a, z):
                    b, turn = ring.at(("row", g, m), in_pass)
                    dve.wait_ge(ring.full[b], turn)
                    nc.vector.tensor_reduce(mx[:, g, m // TT, m % TT:m % TT + 1], banks[b][:], AX_X, ALU.max) \
                        .then_inc(ring.free[b], 1)

            def negated(ring, in_pass, n, g):
                b, turn = ring.at(("neg", g), in_pass)
                dve.wait_ge(ring.full[b], turn)
                if ring is not first:
                    dve.wait_ge(max_in, n * 16)
                nc.vector.tensor_scalar(neg_t[:], banks[b][0:HG * TT, 0:P], -1.0, None, ALU.mult) \
                    .then_inc(ring.free[b], 1)

            def finish(n, g):
                dve.wait_ge(acc_full, n + 2)
                nc.vector.reciprocal(rsum[:], acc_sum[:]).then_inc(rsum_done, 1)
                dve.wait_ge(rsum_done, n + 1)
                nc.vector.scalar_tensor_tensor(out=out_t[:, g, :], in0=acc[:], scalar=1.0 - LAMBDA_INIT,
                                               in1=rsum[:], op0=ALU.mult, op1=ALU.mult).then_inc(acc_free, 1)

            def one_pass(i, more):
                for g in range(GROUPS):
                    n = i * GROUPS + g
                    rg, pg = (g + 1) % GROUPS, (g + 2) % GROUPS
                    rows_on, proj_on = more or g + 1 < GROUPS, more or g + 2 < GROUPS
                    if g:
                        finish(n - 1, g - 1)
                    for half in range(4):
                        if rows_on:
                            maxima(ring, i, rg, *ROWS_AT[half])
                        if half in (0, 2) and proj_on:
                            low(ring, i, n + 2, "q" if half == 0 else "k", pg)
                    if rows_on:
                        negated(ring, i, n + 1, rg)
                    if g == 0 and more:
                        norm_vector(nc, dve, norm, x, i + 1)
                    if g == 1 and more:
                        features(ring, i)
                finish(i * GROUPS + GROUPS - 1, GROUPS - 1)
                if more:
                    values(ring, i)
                for tt in range(TT):
                    b, turn = ring.at(("out", tt), i)
                    dve.wait_ge(ring.full[b], turn)
                    nc.vector.tensor_tensor(x[:, i, tt, :], banks[b][:], x[:, i, tt, :], ALU.add) \
                        .then_inc(ring.free[b], 1)

            nc.vector.memset(ks[3 * E2:3 * E2 + 1, :, :].bitcast(F32), 1.0)
            norm_vector(nc, dve, norm, x, 0)
            features(first, 0)
            dve.wait_ge(lam_in, 16 * 5)
            for n in range(2):
                red = nc.vector.tensor_tensor_reduce(lam_v[:, 2 * n, :], lam_v[:, 2 * n, :], lam_v[:, 2 * n + 1, :],
                                                     1.0, 0.0, ALU.mult, ALU.add, lam_s[:, n:n + 1])
            red.then_inc(lam_step, 1)
            dve.wait_ge(lam_step, 3)
            nc.vector.tensor_tensor(lam_s[:, 4:5], lam_s[:, 2:3], lam_s[:, 3:4], ALU.subtract) \
                .then_inc(lam_step, 1)
            dve.wait_ge(lam_step, 4)
            nc.vector.tensor_scalar(lam_s[:, 5:6], lam_s[:, 4:5], LAMBDA_INIT, rowsel[:, 1:2], ALU.add, ALU.mult) \
                .then_inc(lam_step, 1)
            dve.wait_ge(lam_step, 5)
            nc.vector.tensor_tensor(coef[:], rowsel[:, 0:1], lam_s[:, 5:6], ALU.subtract).then_inc(lam_step, 1)
            dve.wait_ge(lam_step, 6)
            for g in range(2):
                for kind in "qk":
                    low(first, 0, g, kind, g)
            values(first, 0)
            maxima(first, 0, 0, 0, ROWS)
            negated(first, 0, 0, 0)
            passes(dve, one_pass)

        @block.gpsimd
        def _(pool):
            def store_maxima(ring, in_pass, g):
                b, turn = ring.at(("neg", g), in_pass)
                wait_apart(pool, ring.free[b], turn + 1, waited)
                pool.dma_start(qs[3 * E2:3 * E2 + 1, g * HG:(g + 1) * HG, :]
                               .rearrange("o j (t c) -> o (j t) c", c=P).bitcast(F32),
                               neg_t[:].bitcast(F32)).then_inc(max_in, 16)

            def one_pass(i, more):
                for g in range(GROUPS):
                    if more or g + 1 < GROUPS:
                        store_maxima(ring, i, (g + 1) % GROUPS)
                    if g == 0 and more:
                        norm_gpsimd(nc, pool, norm, consts.minus_half, i + 1)

            norm_gpsimd(nc, pool, norm, consts.minus_half, 0)
            store_maxima(first, 0, 0)
            passes(pool, one_pass)


def stage_gate_and_mix(core, sb, psum, dram, x, consts, scratch):
    nc = core.nc
    gate_norm = Norm(core, sb, "g")
    y = sb("g_y", [P, B, ET, T], F32)
    z = sb("g_z", [P, ET, T], F32)
    gy = sb("g_gy", [P, ET, T], F32)
    y_in = core.sems("g_y_in", B)
    silu_done = core.sem("g_silu")
    gated = core.sem("g_gated")

    norm = Norm(core, sb, "r")
    factors = sb("r_factors", [P, KD, D], F32)
    bias = sb("r_bias", [P, D], F32)
    xn_t = sb("r_xn_t", [P, KD, T], F32)
    factors_in = core.sem("r_in")
    bias_in = core.sem("r_bias_in")
    biased = core.sem("r_biased")
    stored = core.sem("r_stored")

    banks = [psum(f"r_bank{b}", [P, 512], F32) for b in range(8)]
    gate_steps = [("gate", tt) for tt in range(TT)]
    out_steps = [("out", tt) for tt in range(TT)]
    xn_steps = [("xn", k) for k in range(KD)]
    ring = Ring(core.sems("r_full", 8), core.sems("r_free", 8), gate_steps + out_steps + xn_steps, out_steps)
    first = Ring(core.sems("r_first_full", 8), core.sems("r_first_free", 8), gate_steps + xn_steps)

    def passes(eng, one_pass):
        with eng.Fori(0, B - 2) as i:
            one_pass(i, True, True)
        one_pass(B - 2, True, False)
        one_pass(B - 1, False, False)

    with nc.Block() as block:
        @block.sync
        def _(sp):
            def one_pass(i, *_):
                for tt in range(TT):
                    b, turn = ring.at(("out", tt), i)
                    sp.wait_ge(ring.free[b], turn + 1)
                    sp.dma_start(dram["out"][i, tt * P:(tt + 1) * P, :], x[:, i, tt, :]).then_inc(stored, 16)

            sp.dma_start(y[:, 0], scratch["y"][0]).then_inc(y_in[0], 16)
            sp.dma_start(factors[:], scratch["factor_sum"]).then_inc(factors_in, 16)
            sp.dma_start(bias[:], dram["bias"].rearrange("(o e) -> o e", o=1).broadcast_to([P, D])) \
                .then_inc(bias_in, 16)
            for b in range(1, B):
                sp.dma_start(y[:, b], scratch["y"][b]).then_inc(y_in[b], 16)
            passes(sp, one_pass)
            sp.wait_ge(stored, B * TT * 16)

        @block.tensor
        def _(pe):
            start_at_one(pe, *ring.free, *first.free, gated, silu_done)

            def turn_gated(ring, in_pass, i):
                pe.wait_ge(gated, (i + 1) * ET + 1)
                for tt in range(TT):
                    b, turn = ring.at(("gate", tt), in_pass)
                    pe.wait_ge(ring.free[b], turn)
                    for et in range(ET):
                        mm = nc.tensor.transpose(banks[b][:, et * P:(et + 1) * P],
                                                 gy[:, et, tt * P:(tt + 1) * P], consts.ident[:])
                    mm.then_inc(ring.full[b], 1)

            def one_pass(i, more, _):
                if more:
                    turn_gated(ring, i, i + 1)
                for tt in range(TT):
                    b, turn = ring.at(("out", tt), i)
                    pe.wait_ge(ring.free[b], turn)
                    for k in range(KD):
                        mm = nc.tensor.matmul(banks[b][:], xn_t[:, k, tt * P:(tt + 1) * P], factors[:, k, :],
                                              start=(k == 0), stop=(k == KD - 1))
                    mm.then_inc(ring.full[b], 1)
                if more:
                    norm_tensor(nc, pe, norm, consts.ident, ring, banks, i + 1, in_pass=i)
                    ring.wait_free(pe, i, consumed=xn_steps)

            turn_gated(first, 0, 0)
            norm_tensor(nc, pe, norm, consts.ident, first, banks, 0)
            first.wait_free(pe, 0, consumed=xn_steps)
            pe.wait_ge(factors_in, 16)
            passes(pe, one_pass)

        @block.scalar
        def _(act):
            def silu(i):
                act.wait_ge(gate_norm.xn_ready, (i + 1) * TT)
                act.wait_ge(gated, i * ET + 1)
                for et in range(ET):
                    nc.scalar.activation(z[:, et, :], gate_norm.xn[:, et, :], ACT.Silu).then_inc(silu_done, 1)

            def features(ring, in_pass):
                for k in range(KD):
                    b, turn = ring.at(("xn", k), in_pass)
                    act.wait_ge(ring.full[b], turn)
                    nc.scalar.copy(xn_t[:, k, :], banks[b][:]).then_inc(ring.free[b], 1)

            def one_pass(i, more, more2):
                if more2:
                    silu(i + 2)
                if more:
                    features(ring, i)

            silu(0)
            silu(1)
            features(first, 0)
            passes(act, one_pass)

        @block.gpsimd
        def _(pool):
            def gate(ring, in_pass, i, before=True):
                if before:
                    for tt in range(TT):
                        b, turn = ring.at(("gate", tt), in_pass)
                        pool.wait_ge(ring.full[b], turn)
                for et in range(ET):
                    pool.wait_ge(silu_done, i * ET + et + 2)
                    nc.gpsimd.tensor_tensor(gy[:, et, :], y[:, i, et, :], z[:, et, :], ALU.mult).then_inc(gated, 1)

            def add_bias(i):
                pool.wait_ge(norm.xn_ready, (i + 1) * TT)
                for tt in range(TT):
                    nc.gpsimd.tensor_tensor(x[:, i, tt, :], x[:, i, tt, :], bias[:], ALU.add).then_inc(biased, 1)

            def one_pass(i, more, more2):
                if more:
                    norm_gpsimd(nc, pool, norm, consts.minus_half, i + 1)
                if more2:
                    norm_gpsimd(nc, pool, gate_norm, consts.minus_half, i + 2)
                    gate(ring, i, i + 2)
                if more:
                    add_bias(i + 1)

            norm_gpsimd(nc, pool, gate_norm, consts.minus_half, 0)
            pool.wait_ge(y_in[0], 16)
            gate(first, 0, 0, before=False)
            norm_gpsimd(nc, pool, gate_norm, consts.minus_half, 1)
            norm_gpsimd(nc, pool, norm, consts.minus_half, 0)
            for b in range(1, B):
                pool.wait_ge(y_in[b], 16)
            gate(first, 0, 1)
            pool.wait_ge(bias_in, 16)
            add_bias(0)
            passes(pool, one_pass)

        @block.vector
        def _(dve):
            def add_gated(ring, in_pass, i):
                for tt in range(TT):
                    b, turn = ring.at(("gate", tt), in_pass)
                    dve.wait_ge(ring.full[b], turn)
                    nc.vector.tensor_tensor(x[:, i, tt, :], banks[b][:], x[:, i, tt, :], ALU.add) \
                        .then_inc(ring.free[b], 1)

            def ready_for_norm(ring, in_pass):
                for tt in range(TT):
                    b, turn = ring.at(("gate", tt), in_pass)
                    wait_apart(dve, ring.free[b], turn + 1, norm.waited)

            def norm_gate(i):
                wait_apart(dve, silu_done, i * ET + 1, gate_norm.waited)
                norm_vector(nc, dve, gate_norm, x, i)

            def one_pass(i, more, more2):
                if more:
                    add_gated(ring, i, i + 1)
                    ready_for_norm(ring, i)
                    norm_vector(nc, dve, norm, x, i + 1)
                if more2:
                    norm_gate(i + 2)
                for tt in range(TT):
                    b, turn = ring.at(("out", tt), i)
                    dve.wait_ge(ring.full[b], turn)
                    dve.wait_ge(biased, i * TT + tt + 1)
                    nc.vector.scalar_tensor_tensor(out=x[:, i, tt, :], in0=banks[b][:],
                                                   scalar=1.0 / math.sqrt(RANK), in1=x[:, i, tt, :],
                                                   op0=ALU.mult, op1=ALU.add).then_inc(ring.free[b], 1)

            norm_gate(0)
            norm_gate(1)
            add_gated(first, 0, 0)
            ready_for_norm(first, 0)
            norm_vector(nc, dve, norm, x, 0)
            passes(dve, one_pass)


def program(nc, dram):
    scratch = {
        "bc": nc.dram_tensor("scan_bc", [B, 2 * DS, T], F32, kind="Internal").ap(),
        "delta": nc.dram_tensor("scan_delta", [B, P, ET, T], F32, kind="Internal").ap(),
        "delta_u": nc.dram_tensor("scan_delta_u", [B, P, ET, T], F32, kind="Internal").ap(),
        "factor_sum": nc.dram_tensor("mix_factors", [P, KD, D], F32, kind="Internal").ap(),
        "weights": nc.dram_tensor("ffn_weights", [P, W_ALL], I32, kind="Internal").ap(),
        "y": nc.dram_tensor("scan_y", [B, P, ET, T], F32, kind="Internal").ap(),
    }
    with ExitStack() as whole:
        core = Core(nc)

        def keeper(stack):
            return (lambda n, s, d: stack.enter_context(nc.sbuf_tensor(n, s, d)),
                    lambda n, s, d: stack.enter_context(nc.psum_tensor(n, s, d)))

        sb, _ = keeper(whole)
        x = sb("x_res", [P, B, TT, D], F32)
        consts = Consts(sb)
        with ExitStack() as stage:
            sb, psum = keeper(stage)
            stage_setup(core, sb, dram, x, consts)
        core.clear()
        for stage in (stage_window_attention, stage_context, stage_ffn, stage_diff_attention, stage_gate_and_mix):
            with ExitStack() as held:
                stage(core, *keeper(held), dram, x, consts, scratch)
            core.clear()


def laid_out(v):
    c = np.ascontiguousarray
    out = {
        "x": v["x"], "ctx_t": c(v["ctx_1024"].transpose(0, 2, 1)),
        "wq_t": c(v["L0_attn_wq"].T), "wk_t": c(v["L0_attn_wk"].T), "wv_t": c(v["L0_attn_wv"].T),
        "wo_t": c(v["L0_attn_wo"].T),
        "x_wq_t": c(v["L0_xattn_Wq"].T), "x_wk_t": c(v["L0_xattn_Wk"].T),
        "x_bq": v["L0_xattn_bq"], "x_bk": v["L0_xattn_bk"],
        "lut": v["L0_ffn_lut"],
        "lq1": v["L1_attn_lambda_q1"], "lk1": v["L1_attn_lambda_k1"],
        "lq2": v["L1_attn_lambda_q2"], "lk2": v["L1_attn_lambda_k2"], "d_wp": v["L1_attn_W_proj"],
        "m_in_t": c(v["L1_xattn_in_proj_w"].T), "m_x_t": c(v["L1_xattn_x_proj_w"].T),
        "m_dt_t": c(v["L1_xattn_dt_proj_w"].T), "m_a_log": v["L1_xattn_A_log"],
        "m_cols": c(np.concatenate([v["L1_xattn_conv_w"], v["L1_xattn_conv_b"][:, None],
                                    v["L1_xattn_dt_proj_b"][:, None], v["L1_xattn_D"][:, None]], axis=1)),
        "factors": v["L1_ffn_factors"], "bias": v["L1_ffn_bias"],
    }
    tiles = lambda a: a.reshape(-1, P, a.shape[1]).transpose(1, 0, 2).reshape(P, -1)
    down = np.zeros((OT * P, D), v["L0_ffn_down_idx"].dtype)
    down[:INTER] = v["L0_ffn_down_idx"].T
    out["idx"] = c(np.concatenate([tiles(v["L0_ffn_gate_idx"].T), tiles(v["L0_ffn_up_idx"].T), tiles(down)],
                                  axis=1))
    w = v["L1_attn_W_attn"].reshape(D, 3 * D)
    part = lambda n: w[:, n * (D // 2):(n + 1) * (D // 2)].reshape(D, DH, DHD)
    out["d_w"] = c(np.concatenate([np.concatenate([part(0), part(2)], axis=2).reshape(D, D),
                                   np.concatenate([part(1), part(3)], axis=2).reshape(D, D),
                                   w[:, 2 * D:]], axis=1))
    half = HD // 2
    inv_freq = (1.0 / np.float32(10000.0) ** (np.arange(half, dtype=np.float32) / np.float32(half)))
    freqs = np.outer(np.arange(T, dtype=np.float32), inv_freq.astype(np.float32))
    cos, sin = np.cos(freqs).T.astype(np.float32), np.sin(freqs).T.astype(np.float32)
    out["cos2"], out["sin2"] = c(np.concatenate([cos, cos])), c(np.concatenate([-sin, sin]))
    out["identity"] = np.eye(P, dtype=np.float32)
    row, col = np.arange(P)[:, None], np.arange(2 * P)[None, :]
    own = (col - P <= row) & (col >= P)
    seen = np.stack([own, own | ((col < P) & (row + P - col <= WINDOW))])
    out["masks"] = c(np.where(seen, 0.0, MASKED).astype(np.float32).transpose(1, 0, 2))
    q2 = (np.arange(P) // DHD) % 2
    out["rowsel"] = c(np.stack([1 - q2, q2], axis=1).astype(np.float32) * np.float32(DHD ** -0.5))
    return out


def kernel(**inputs):
    import concourse.bacc as bacc
    from concourse.bass_utils import run_bass_kernel_spmd

    nc = bacc.Bacc("TRN2", target_bir_lowering=False, num_devices=1)
    arrays = {f"in_{k}": a for k, a in laid_out({k: np.asarray(a) for k, a in inputs.items()}).items()}
    dram = {n[3:]: nc.dram_tensor(n, a.shape, mybir.dt.from_np(a.dtype), kind="ExternalInput").ap()
            for n, a in arrays.items()}
    dram["out"] = nc.dram_tensor("out", [B, T, D], F32, kind="ExternalOutput").ap()
    program(nc, dram)
    return run_bass_kernel_spmd(nc, [arrays], core_ids=[0]).results[0]["out"]
```
